# Optimizing a Trainium2 kernel written in Bass

```python
import numpy as np
import jax
import jax.numpy as jnp

def _softmax(x, axis=-1):
    return jax.nn.softmax(x, axis=axis)

def _gelu(x):
    return jax.nn.gelu(x, approximate=True)

def _silu(x):
    return jax.nn.silu(x)

def _sigmoid(x):
    return jax.nn.sigmoid(x)

def _layernorm(x, axis=-1, eps=1e-05):
    m = jnp.mean(x, axis=axis, keepdims=True)
    v = jnp.var(x, axis=axis, keepdims=True)
    return (x - m) / jnp.sqrt(v + eps)

def _scatter_add(tgt, idx, src, axis=0):
    return tgt.at[idx].add(src)

def _segment_sum(src, seg, n):
    return jax.ops.segment_sum(src, seg, n)
kernel_name = 'mk_seq_postln_d4_jaxref_r8_f38138'

def setup_inputs(seed: int=0):
    np.random.seed(seed)
    _w = jnp.asarray

    def _L0_attn_setup():
        import jax, jax.numpy as jnp
        import numpy as np
        H = 8
        G = 4
        HQ = H * G
        key = jax.random.key(seed)
        k0, k1, k2, k3 = jax.random.split(key, 4)
        B, N, D = (2, 256, 256)
        s = 1.0 / np.sqrt(D)
        x = jax.random.normal(k0, (B, N, D), jnp.float32)
        Wq = jax.random.normal(k1, (D, D), jnp.float32) * s
        Wkv = jax.random.normal(k2, (D, 2 * D // G), jnp.float32) * s
        Wp = jax.random.normal(k3, (D, D), jnp.float32) * s
        bp = jnp.zeros((D,), jnp.float32)
        return {'x': x, 'Wq': Wq, 'Wkv': Wkv, 'Wp': Wp, 'bp': bp}
    _L0_attn_in = _L0_attn_setup()

    def _L0_ffn_setup():
        import jax, jax.numpy as jnp
        import numpy as np
        D_MODEL = 256
        D_EXPERT = 1024
        EPS = 1e-08

        def ternary_quant(w):
            scale = jnp.mean(jnp.abs(w)) + EPS
            q = jnp.clip(jnp.round(w / scale), -1.0, 1.0) * scale
            return w + jax.lax.stop_gradient(q - w)
        key = jax.random.key(seed)
        k_x, k_up, k_gate, k_down = jax.random.split(key, 4)
        std_in = 1.0 / np.sqrt(D_MODEL)
        std_exp = 1.0 / np.sqrt(D_EXPERT)
        return {'x': jax.random.normal(k_x, (4, 256, D_MODEL), dtype=jnp.float32), 'W_up': jax.random.normal(k_up, (D_EXPERT, D_MODEL), dtype=jnp.float32) * std_in, 'W_gate': jax.random.normal(k_gate, (D_EXPERT, D_MODEL), dtype=jnp.float32) * std_in, 'W_down': jax.random.normal(k_down, (D_MODEL, D_EXPERT), dtype=jnp.float32) * std_exp}
    _L0_ffn_in = _L0_ffn_setup()

    def _L1_attn_setup():
        import jax, jax.numpy as jnp
        import numpy as np
        B, S, H = (4, 256, 256)
        key = jax.random.key(seed)
        k1, k2, k3 = jax.random.split(key, 3)
        xav_qkv = float(np.sqrt(6.0 / (H + 3 * H)))
        xav_out = float(np.sqrt(6.0 / (H + H)))
        return {'hidden_states': jax.random.normal(k1, (B, S, H), dtype=jnp.float32), 'w_qkv': jax.random.uniform(k2, (3 * H, H), minval=-xav_qkv, maxval=xav_qkv, dtype=jnp.float32), 'b_qkv': jnp.zeros((3 * H,), dtype=jnp.float32), 'w_out': jax.random.uniform(k3, (H, H), minval=-xav_out, maxval=xav_out, dtype=jnp.float32), 'b_out': jnp.zeros((H,), dtype=jnp.float32)}
    _L1_attn_in = _L1_attn_setup()

    def _L1_ffn_setup():
        import jax, jax.numpy as jnp
        import numpy as np
        H, I, E, K = (256, 512, 8, 2)
        B, S = (1, 256)

        def _silu_mul(gu):
            d = gu.shape[-1] // 2
            return jax.nn.silu(gu[..., :d]) * gu[..., d:]
        key = jax.random.key(seed)
        ks = jax.random.split(key, 6)
        w_scale = 0.02
        return {'x': jax.random.normal(ks[0], (B, S, H), jnp.float32), 'gate_w': jax.random.normal(ks[1], (H, E), jnp.float32) * w_scale, 'base_gate_up': jax.random.normal(ks[2], (H, 2 * I), jnp.float32) * w_scale, 'base_down': jax.random.normal(ks[3], (I, H), jnp.float32) * w_scale, 'expert_gate_up': jax.random.normal(ks[4], (E, H, 2 * I), jnp.float32) * w_scale, 'expert_down': jax.random.normal(ks[5], (E, I, H), jnp.float32) * w_scale}
    _L1_ffn_in = _L1_ffn_setup()

    def _L2_attn_setup():
        import jax, jax.numpy as jnp
        import numpy as np
        B, SQ, H = (2, 256, 256)
        NH = 16
        HN = H // NH
        key = jax.random.key(seed)
        ks = jax.random.split(key, 6)
        query = jax.random.normal(ks[0], (B, SQ, H), dtype=jnp.float32)
        k_in = jax.random.normal(ks[1], (B, SQ, H), dtype=jnp.float32)
        v_in = jax.random.normal(ks[2], (B, SQ, H), dtype=jnp.float32)
        Wqkv = jax.random.normal(ks[3], (3 * H, H), dtype=jnp.float32) * (1.0 / np.sqrt(H))
        Wproj = jax.random.normal(ks[4], (H, H), dtype=jnp.float32) * (1.0 / np.sqrt(H))
        bproj = jnp.zeros((H,), dtype=jnp.float32)
        return {'query': query, 'key': k_in, 'value': v_in, 'Wqkv': Wqkv, 'Wproj': Wproj, 'bproj': bproj}
    _L2_attn_in = _L2_attn_setup()

    def _L2_ffn_setup():
        import jax, jax.numpy as jnp
        import numpy as np
        HIDDEN = 256
        INTER = 688
        LUT_SIZE = 16

        def _ghost_linear(x, idx, lut):
            w = lut[idx]
            return jnp.einsum('bsh,oh->bso', x, w)
        key = jax.random.key(seed)
        k_x, k_lut, k_g, k_u, k_d = jax.random.split(key, 5)
        x = jax.random.normal(k_x, (2, 512, HIDDEN), dtype=jnp.float32)
        lut = jax.random.normal(k_lut, (LUT_SIZE,), dtype=jnp.float32) * 0.02
        gate_idx = jax.random.randint(k_g, (INTER, HIDDEN), 0, LUT_SIZE, dtype=jnp.int32)
        up_idx = jax.random.randint(k_u, (INTER, HIDDEN), 0, LUT_SIZE, dtype=jnp.int32)
        down_idx = jax.random.randint(k_d, (HIDDEN, INTER), 0, LUT_SIZE, dtype=jnp.int32)
        return {'x': x, 'lut': lut, 'gate_idx': gate_idx, 'up_idx': up_idx, 'down_idx': down_idx}
    _L2_ffn_in = _L2_ffn_setup()

    def _L3_attn_setup():
        import jax, jax.numpy as jnp
        import numpy as np
        N_EMBD = 256
        N_HEADS = 16
        HEAD_DIM = N_EMBD // N_HEADS
        THETA = 10000.0

        def _rope_tables(seq_len, head_dim):
            inv = 1.0 / THETA ** (jnp.arange(0, head_dim, 2, dtype=jnp.float32) / head_dim)
            pos = jnp.arange(seq_len, dtype=jnp.float32)
            freqs = jnp.outer(pos, inv)
            return (jnp.cos(freqs)[None, :, None, :], jnp.sin(freqs)[None, :, None, :])

        def _apply_rope(t, cos, sin):
            B, S, H, D = t.shape
            tr = t.reshape(B, S, H, D // 2, 2)
            x0, x1 = (tr[..., 0], tr[..., 1])
            r0 = x0 * cos - x1 * sin
            r1 = x0 * sin + x1 * cos
            return jnp.stack([r0, r1], axis=-1).reshape(B, S, H, D)
        key = jax.random.key(seed)
        ks = jax.random.split(key, 9)
        B, S, E = (4, 256, N_EMBD)
        scale = 1.0 / np.sqrt(E)
        inp = {'x': jax.random.normal(ks[0], (B, S, E), dtype=jnp.float32), 'Wq': jax.random.normal(ks[1], (E, E), dtype=jnp.float32) * scale, 'bq': jnp.zeros((E,), dtype=jnp.float32), 'Wk': jax.random.normal(ks[2], (E, E), dtype=jnp.float32) * scale, 'bk': jnp.zeros((E,), dtype=jnp.float32), 'Wv': jax.random.normal(ks[3], (E, E), dtype=jnp.float32) * scale, 'bv': jnp.zeros((E,), dtype=jnp.float32), 'Wo': jax.random.normal(ks[4], (E, E), dtype=jnp.float32) * scale, 'bo': jnp.zeros((E,), dtype=jnp.float32)}
        return inp
    _L3_attn_in = _L3_attn_setup()

    def _L3_ffn_setup():
        import jax, jax.numpy as jnp
        import numpy as np
        H = 256
        I = 128
        K = 8
        E = 128
        TOPK = 4
        EPS = 1e-08
        key = jax.random.key(seed)
        ks = jax.random.split(key, 10)
        s = 0.02
        return {'x': jax.random.normal(ks[0], (4, 256, H), jnp.float32), 'w_router': jax.random.normal(ks[1], (H, E), jnp.float32) * s, 'w_gate': jax.random.normal(ks[2], (H, K * I), jnp.float32) * s, 'w_up': jax.random.normal(ks[3], (H, K * I), jnp.float32) * s, 'w_down': jax.random.normal(ks[4], (I, H), jnp.float32) * s, 'amplitudes': jax.random.normal(ks[5], (E, K, 2), jnp.float32) * 0.1, 'expert_scale': jnp.ones((E,), jnp.float32), 'shared_w_gate': jax.random.normal(ks[6], (H, 2 * I), jnp.float32) * s, 'shared_w_up': jax.random.normal(ks[7], (H, 2 * I), jnp.float32) * s, 'shared_w_down': jax.random.normal(ks[8], (2 * I, H), jnp.float32) * s}
    _L3_ffn_in = _L3_ffn_setup()
    _d = {'L0_attn_x': _L0_attn_in['x'], 'L0_attn_Wq': _L0_attn_in['Wq'], 'L0_attn_Wkv': _L0_attn_in['Wkv'], 'L0_attn_Wp': _L0_attn_in['Wp'], 'L0_attn_bp': _L0_attn_in['bp'], 'L0_ffn_W_up': _L0_ffn_in['W_up'], 'L0_ffn_W_gate': _L0_ffn_in['W_gate'], 'L0_ffn_W_down': _L0_ffn_in['W_down'], 'L1_attn_w_qkv': _L1_attn_in['w_qkv'], 'L1_attn_b_qkv': _L1_attn_in['b_qkv'], 'L1_attn_w_out': _L1_attn_in['w_out'], 'L1_attn_b_out': _L1_attn_in['b_out'], 'L1_ffn_gate_w': _L1_ffn_in['gate_w'], 'L1_ffn_base_gate_up': _L1_ffn_in['base_gate_up'], 'L1_ffn_base_down': _L1_ffn_in['base_down'], 'L1_ffn_expert_gate_up': _L1_ffn_in['expert_gate_up'], 'L1_ffn_expert_down': _L1_ffn_in['expert_down'], 'L2_attn_key': _L2_attn_in['key'], 'L2_attn_value': _L2_attn_in['value'], 'L2_attn_Wqkv': _L2_attn_in['Wqkv'], 'L2_attn_Wproj': _L2_attn_in['Wproj'], 'L2_attn_bproj': _L2_attn_in['bproj'], 'L2_ffn_lut': _L2_ffn_in['lut'], 'L2_ffn_gate_idx': _L2_ffn_in['gate_idx'], 'L2_ffn_up_idx': _L2_ffn_in['up_idx'], 'L2_ffn_down_idx': _L2_ffn_in['down_idx'], 'L3_attn_Wq': _L3_attn_in['Wq'], 'L3_attn_bq': _L3_attn_in['bq'], 'L3_attn_Wk': _L3_attn_in['Wk'], 'L3_attn_bk': _L3_attn_in['bk'], 'L3_attn_Wv': _L3_attn_in['Wv'], 'L3_attn_bv': _L3_attn_in['bv'], 'L3_attn_Wo': _L3_attn_in['Wo'], 'L3_attn_bo': _L3_attn_in['bo'], 'L3_ffn_w_router': _L3_ffn_in['w_router'], 'L3_ffn_w_gate': _L3_ffn_in['w_gate'], 'L3_ffn_w_up': _L3_ffn_in['w_up'], 'L3_ffn_w_down': _L3_ffn_in['w_down'], 'L3_ffn_amplitudes': _L3_ffn_in['amplitudes'], 'L3_ffn_expert_scale': _L3_ffn_in['expert_scale'], 'L3_ffn_shared_w_gate': _L3_ffn_in['shared_w_gate'], 'L3_ffn_shared_w_up': _L3_ffn_in['shared_w_up'], 'L3_ffn_shared_w_down': _L3_ffn_in['shared_w_down']}
    _x0 = _d['L0_attn_x']
    _d['L0_attn_x'] = jax.random.normal(jax.random.fold_in(jax.random.key(seed), 1), (4, 512, 256), dtype=_x0.dtype)
    del _x0
    return _d

def reference(L0_attn_x, L0_attn_Wq, L0_attn_Wkv, L0_attn_Wp, L0_attn_bp, L0_ffn_W_up, L0_ffn_W_gate, L0_ffn_W_down, L1_attn_w_qkv, L1_attn_b_qkv, L1_attn_w_out, L1_attn_b_out, L1_ffn_gate_w, L1_ffn_base_gate_up, L1_ffn_base_down, L1_ffn_expert_gate_up, L1_ffn_expert_down, L2_attn_key, L2_attn_value, L2_attn_Wqkv, L2_attn_Wproj, L2_attn_bproj, L2_ffn_lut, L2_ffn_gate_idx, L2_ffn_up_idx, L2_ffn_down_idx, L3_attn_Wq, L3_attn_bq, L3_attn_Wk, L3_attn_bk, L3_attn_Wv, L3_attn_bv, L3_attn_Wo, L3_attn_bo, L3_ffn_w_router, L3_ffn_w_gate, L3_ffn_w_up, L3_ffn_w_down, L3_ffn_amplitudes, L3_ffn_expert_scale, L3_ffn_shared_w_gate, L3_ffn_shared_w_up, L3_ffn_shared_w_down):

    def _L0_attn_ref(x, Wq, Wkv, Wp, bp):
        import jax, jax.numpy as jnp
        import numpy as np
        H = 8
        G = 4
        HQ = H * G
        B, N, D = x.shape
        C = D // (H * G)
        scale = float(np.sqrt(HQ))
        q = x @ Wq / scale
        kv = x @ Wkv
        k, v = jnp.split(kv, 2, axis=-1)
        q = q.reshape(B, N, H, G, C).transpose(0, 3, 2, 1, 4)
        k = k.reshape(B, N, H, C).transpose(0, 2, 1, 3)
        v = v.reshape(B, N, H, C).transpose(0, 2, 1, 3)
        sim = jnp.einsum('bghnc,bhsc->bghns', q, k)
        attn = jax.nn.softmax(sim, axis=-1)
        o = jnp.einsum('bghns,bhsc->bghnc', attn, v)
        o = o.transpose(0, 3, 2, 1, 4).reshape(B, N, D)
        return o @ Wp + bp

    def _L0_ffn_ref(x, W_up, W_gate, W_down):
        import jax, jax.numpy as jnp
        import numpy as np
        D_MODEL = 256
        D_EXPERT = 1024
        EPS = 1e-08

        def ternary_quant(w):
            scale = jnp.mean(jnp.abs(w)) + EPS
            q = jnp.clip(jnp.round(w / scale), -1.0, 1.0) * scale
            return w + jax.lax.stop_gradient(q - w)
        wu = ternary_quant(W_up)
        wg = ternary_quant(W_gate)
        wd = ternary_quant(W_down)
        up = jnp.einsum('bsd,ed->bse', x, wu)
        gate = jnp.einsum('bsd,ed->bse', x, wg)
        hidden = jax.nn.silu(up) * gate
        return jnp.einsum('bse,de->bsd', hidden, wd)

    def _L1_attn_ref(hidden_states, w_qkv, b_qkv, w_out, b_out):
        import jax, jax.numpy as jnp
        import numpy as np
        B, S, H = (4, 256, 256)
        Bc, Sc, Hc = hidden_states.shape
        scaling = jnp.sqrt(jnp.asarray(Hc, hidden_states.dtype))
        qkv = jnp.einsum('bsh,oh->bso', hidden_states, w_qkv) + b_qkv
        q, k, v = jnp.split(qkv, 3, axis=-1)
        scores = jnp.einsum('bqh,bkh->bqk', q, k) / scaling
        probs = jax.nn.softmax(scores, axis=-1)
        context = jnp.einsum('bqk,bkh->bqh', probs, v)
        out = jnp.einsum('bsh,oh->bso', context, w_out) + b_out
        return out

    def _L1_ffn_ref(x, gate_w, base_gate_up, base_down, expert_gate_up, expert_down):
        import jax, jax.numpy as jnp
        import numpy as np
        H, I, E, K = (256, 512, 8, 2)
        B, S = (1, 256)

        def _silu_mul(gu):
            d = gu.shape[-1] // 2
            return jax.nn.silu(gu[..., :d]) * gu[..., d:]
        base_y = _silu_mul(x @ base_gate_up) @ base_down
        b, s, h = x.shape
        xf = x.reshape(-1, h)
        n = xf.shape[0]
        n_exp = gate_w.shape[1]
        probs = jax.nn.softmax((xf @ gate_w).astype(jnp.float32), axis=-1)
        w, idx = jax.lax.top_k(probs, K)
        w = (w / w.sum(axis=-1, keepdims=True)).astype(x.dtype)
        comb = jnp.zeros((n, n_exp), x.dtype).at[jnp.arange(n)[:, None], idx].add(w)
        out = jnp.zeros_like(xf)
        for e in range(n_exp):
            y = _silu_mul(xf @ expert_gate_up[e]) @ expert_down[e]
            out = out + comb[:, e:e + 1] * y
        return out.reshape(b, s, h) + base_y

    def _L2_attn_ref(query, key, value, Wqkv, Wproj, bproj):
        import jax, jax.numpy as jnp
        import numpy as np
        B, SQ, H = (2, 256, 256)
        NH = 16
        HN = H // NH
        b, sq, h = query.shape
        nh, hn = (NH, HN)
        norm = 1.0 / jnp.sqrt(jnp.asarray(hn, query.dtype))
        x = jnp.transpose(query, (1, 0, 2)).reshape(sq * b, h)
        mixed = x @ Wqkv.T
        mixed = mixed.reshape(sq, b, nh, 3, hn)
        q = mixed[..., 0, :]
        k = mixed[..., 1, :]
        v = mixed[..., 2, :]
        q = q.reshape(sq, b * nh, hn).transpose(1, 0, 2)
        k = k.reshape(sq, b * nh, hn).transpose(1, 0, 2)
        v = v.reshape(sq, b * nh, hn).transpose(1, 0, 2)
        attn = jnp.einsum('gqd,gkd->gqk', q, k) * norm
        attn = jax.nn.softmax(attn, axis=-1)
        ctx = jnp.einsum('gqk,gkd->gqd', attn, v)
        ctx = ctx.reshape(nh, b, sq, hn)
        ctx = jnp.transpose(ctx, (2, 1, 0, 3)).reshape(sq * b, h)
        out = ctx @ Wproj.T + bproj
        out = out.reshape(sq, b, h)
        return jnp.transpose(out, (1, 0, 2))

    def _L2_ffn_ref(x, lut, gate_idx, up_idx, down_idx):
        import jax, jax.numpy as jnp
        import numpy as np
        HIDDEN = 256
        INTER = 688
        LUT_SIZE = 16

        def _ghost_linear(x, idx, lut):
            w = lut[idx]
            return jnp.einsum('bsh,oh->bso', x, w)
        gate = _ghost_linear(x, gate_idx, lut)
        up = _ghost_linear(x, up_idx, lut)
        h = jax.nn.silu(gate) * up
        return _ghost_linear(h, down_idx, lut)

    def _L3_attn_ref(x, Wq, bq, Wk, bk, Wv, bv, Wo, bo):
        import jax, jax.numpy as jnp
        import numpy as np
        N_EMBD = 256
        N_HEADS = 16
        HEAD_DIM = N_EMBD // N_HEADS
        THETA = 10000.0

        def _rope_tables(seq_len, head_dim):
            inv = 1.0 / THETA ** (jnp.arange(0, head_dim, 2, dtype=jnp.float32) / head_dim)
            pos = jnp.arange(seq_len, dtype=jnp.float32)
            freqs = jnp.outer(pos, inv)
            return (jnp.cos(freqs)[None, :, None, :], jnp.sin(freqs)[None, :, None, :])

        def _apply_rope(t, cos, sin):
            B, S, H, D = t.shape
            tr = t.reshape(B, S, H, D // 2, 2)
            x0, x1 = (tr[..., 0], tr[..., 1])
            r0 = x0 * cos - x1 * sin
            r1 = x0 * sin + x1 * cos
            return jnp.stack([r0, r1], axis=-1).reshape(B, S, H, D)
        B, S, E = x.shape
        H, D = (N_HEADS, HEAD_DIM)
        q = (x @ Wq.T + bq).reshape(B, S, H, D)
        k = (x @ Wk.T + bk).reshape(B, S, H, D)
        v = (x @ Wv.T + bv).reshape(B, S, H, D)
        cos, sin = _rope_tables(S, D)
        q = _apply_rope(q, cos, sin)
        k = _apply_rope(k, cos, sin)
        qk = jnp.einsum('bshd,bstd->bsht', q, k) / jnp.sqrt(jnp.float32(D))
        att = jax.nn.softmax(qk, axis=-1)
        out = jnp.einsum('bsht,bstd->bshd', att, v)
        out = jnp.swapaxes(out, 1, 2).reshape(B, S, E)
        return out @ Wo.T + bo

    def _L3_ffn_ref(x, w_router, w_gate, w_up, w_down, amplitudes, expert_scale, shared_w_gate, shared_w_up, shared_w_down):
        import jax, jax.numpy as jnp
        import numpy as np
        H = 256
        I = 128
        K = 8
        E = 128
        TOPK = 4
        EPS = 1e-08
        B, S, _ = x.shape
        T = B * S
        xt = x.reshape(T, H)
        probs = jax.nn.softmax(xt @ w_router, axis=-1)
        topk_p, topk_idx = jax.lax.top_k(probs, TOPK)
        topk_w = topk_p / (jnp.sum(topk_p, axis=-1, keepdims=True) + EPS)
        gate = (xt @ w_gate).reshape(T, K, I)
        up = (xt @ w_up).reshape(T, K, I)
        basis = jax.nn.silu(gate) * up
        p = amplitudes[..., 0] ** 2 + amplitudes[..., 1] ** 2
        mix = p / (jnp.sum(p, axis=-1, keepdims=True) + EPS)
        mix_sel = mix[topk_idx]
        mixed = jnp.einsum('tek,tki->tei', mix_sel, basis)
        down = jnp.einsum('tei,ih->teh', mixed, w_down)
        coeff = topk_w * expert_scale[topk_idx]
        out = jnp.einsum('teh,te->th', down, coeff)
        shared = jax.nn.silu(xt @ shared_w_gate) * (xt @ shared_w_up) @ shared_w_down
        out = out + shared
        return out.reshape(B, S, H)
    x = L0_attn_x
    x = _layernorm(x + _L0_attn_ref(x, L0_attn_Wq, L0_attn_Wkv, L0_attn_Wp, L0_attn_bp), axis=-1)
    x = _layernorm(x + _L0_ffn_ref(x, L0_ffn_W_up, L0_ffn_W_gate, L0_ffn_W_down), axis=-1)
    x = _layernorm(x + _L1_attn_ref(x, L1_attn_w_qkv, L1_attn_b_qkv, L1_attn_w_out, L1_attn_b_out), axis=-1)
    x = _layernorm(x + _L1_ffn_ref(x, L1_ffn_gate_w, L1_ffn_base_gate_up, L1_ffn_base_down, L1_ffn_expert_gate_up, L1_ffn_expert_down), axis=-1)
    x = _layernorm(x + _L2_attn_ref(x, L2_attn_key, L2_attn_value, L2_attn_Wqkv, L2_attn_Wproj, L2_attn_bproj), axis=-1)
    x = _layernorm(x + _L2_ffn_ref(x, L2_ffn_lut, L2_ffn_gate_idx, L2_ffn_up_idx, L2_ffn_down_idx), axis=-1)
    x = _layernorm(x + _L3_attn_ref(x, L3_attn_Wq, L3_attn_bq, L3_attn_Wk, L3_attn_bk, L3_attn_Wv, L3_attn_bv, L3_attn_Wo, L3_attn_bo), axis=-1)
    x = _layernorm(x + _L3_ffn_ref(x, L3_ffn_w_router, L3_ffn_w_gate, L3_ffn_w_up, L3_ffn_w_down, L3_ffn_amplitudes, L3_ffn_expert_scale, L3_ffn_shared_w_gate, L3_ffn_shared_w_up, L3_ffn_shared_w_down), axis=-1)
    return x

_drawn_inputs = setup_inputs


def setup_inputs(seed=0):
    import zlib

    import numpy as np

    out = dict(_drawn_inputs(seed))
    spreads = {'L0_attn_bp': (0.0, 0.1),
     'L1_attn_b_qkv': (0.0, 0.1),
     'L1_attn_b_out': (0.0, 0.1),
     'L2_attn_bproj': (0.0, 0.1),
     'L3_attn_bq': (0.0, 0.289),
     'L3_attn_bk': (0.0, 0.1),
     'L3_attn_bv': (0.0, 0.1),
     'L3_attn_bo': (0.0, 0.1),
     'L3_ffn_expert_scale': (1.0, 0.6)}
    factors = {'L1_ffn_gate_w': 3.693,
     'L1_ffn_expert_gate_up': 3.172,
     'L1_ffn_expert_down': 3.171,
     'L3_ffn_w_router': 8.0,
     'L3_ffn_w_gate': 8.0,
     'L3_ffn_w_up': 8.0,
     'L3_ffn_w_down': 8.0,
     'L3_ffn_amplitudes': 8.0,
     'L3_ffn_shared_w_gate': 3.41,
     'L3_ffn_shared_w_up': 3.387,
     'L3_ffn_shared_w_down': 3.381}
    for name, (base, spread) in spreads.items():
        noise = np.random.default_rng([zlib.crc32(name.encode()), seed]).standard_normal(out[name].shape)
        drawn = base * np.exp(spread * noise) if base else spread * noise
        out[name] = jnp.asarray(drawn.astype(out[name].dtype))
    for name, factor in factors.items():
        out[name] = (out[name] * factor).astype(out[name].dtype)
    return out
```

```python
from contextlib import ExitStack

import numpy as np
import concourse.bass as bass
import concourse.mybir as mybir

F32 = mybir.dt.float32
F32R = mybir.dt.float32r
I32 = mybir.dt.int32
ACT = mybir.ActivationFunctionType
ALU = mybir.AluOpType
AXX = mybir.AxisListType.X

P = 128
B, S, D = 4, 512, 256
KD = D // P
NT = B * S // P
TPB = S // P
EPS_LN = 1e-5
RAW_COLS = 6144
HI_LO = ((0, 0), (0, 1), (1, 0))


def need(eng, sem, value):
    if isinstance(value, int) and value <= 0:
        return
    eng.wait_ge(sem, value)


class Core:

    def __init__(self, nc, ctx, arrays, out):
        self.nc, self.arrays, self.out = nc, arrays, out
        sb = lambda name, shape, dt=F32: ctx.enter_context(nc.sbuf_tensor(name, shape, dt))
        sem = lambda name: ctx.enter_context(nc.semaphore(name))
        self.X = sb("X", [P, NT, D])
        self.xt_base = nc.sbuf_base
        sb("XT_slab", [P, 2 * KD * NT * P])
        self.XT = [self.lend(f"XT_{n}", [P, KD, NT * P], F32R, i * 4 * KD * NT * P) for i, n in enumerate(("hi", "lo"))]
        self.ident = sb("ident", [P, P])
        self.raw = sb("raw", [P, RAW_COLS])
        self.bias = sb("bias", [P, D])
        self.raw_loaded = sem("raw_loaded")
        self.bias_loaded = sem("bias_loaded")
        self.n_raw = self.n_bias = 0
        self.limbo = []

    def lend(self, name, shape, dt, at):
        assert at + 4 * int(np.prod(shape[1:])) <= 8 * KD * NT * P
        return self.nc.alloc_sbuf_tensor_at(name, shape, dt, offset=self.xt_base + at)

    def load_raw(self, eng, pieces):
        at = 0
        for name, cols in pieces:
            src = self.arrays[name]
            dst = self.raw[0:src.shape[0], at:at + cols]
            if src.dtype != F32:
                dst = dst.bitcast(src.dtype)
            eng.dma_start(dst, src).then_inc(self.raw_loaded, 16)
            self.n_raw += 16
            at += cols

    def load_bias(self, eng, name):
        eng.dma_start(self.bias[:], self.arrays[name].partition_broadcast(P)).then_inc(self.bias_loaded, 16)
        self.n_bias += 16


class Phase:

    def __init__(self, core, tag):
        self.core, self.tag, self.ctx, self.sems = core, tag, ExitStack(), []

    def __enter__(self):
        self.ctx.__enter__()
        return self

    def __exit__(self, *a):
        nc, limbo = self.core.nc, self.core.limbo
        if self.sems:
            for s in self.sems:
                nc.sync.sem_clear(s)
            limbo.append(self.sems)
            if len(limbo) > 2:
                for s in limbo.pop(0):
                    nc.release_semaphore(s)
        return self.ctx.__exit__(*a)

    def sb(self, name, shape, dt=F32):
        return self.ctx.enter_context(self.core.nc.sbuf_tensor(f"{self.tag}_{name}_s", shape, dt))

    def ps(self, name, shape, dt=F32):
        return self.ctx.enter_context(self.core.nc.psum_tensor(f"{self.tag}_{name}", shape, dt))

    def sem(self, name):
        self.sems.append(self.core.nc.alloc_semaphore(f"{self.tag}_{name}"))
        return self.sems[-1]


def split_on(phase, hi, lo, cols, chunk=1024):
    core = phase.core
    w_hi = phase.sem("w_hi")
    w_lo = phase.sem("w_lo")
    starts = list(range(0, cols, chunk))
    loaded = core.n_raw

    def act():
        e = core.nc.scalar
        e.wait_ge(core.raw_loaded, loaded)
        for a in starts:
            b = min(cols, a + chunk)
            e.activation(hi[:, a:b], core.raw[:, a:b], ACT.Copy).then_inc(w_hi, 1)

    def dve():
        e = core.nc.vector
        e.wait_ge(core.raw_loaded, loaded)
        for n, a in enumerate(starts):
            b = min(cols, a + chunk)
            e.wait_ge(w_hi, n + 1)
            e.tensor_tensor(lo[:, a:b], core.raw[:, a:b], hi[:, a:b].bitcast(F32), ALU.subtract).then_inc(w_lo, 1)

    return act, dve, w_lo, len(starts)


class Tail:

    def __init__(self, phase, last=False):
        core = self.core = phase.core
        self.last = last
        self.y = phase.ps("y", [P, 2, 512])
        self.tx = phase.ps("tx", [P, 512]) if not last else None
        self.R = phase.sb("R", [P, 2, D])
        self.xo = phase.sb("xo", [P, 2, D]) if last else None
        self.st = phase.sb("st", [P, 2, 8])
        self.mv = phase.sb("mv", [P, 2, 2])
        self.ve = phase.sb("ve", [P, 2, 1])
        self.half = phase.sb("half", [P, 1])
        self.rstd = phase.sb("rstd", [P, 2, 1])
        s = phase.sem
        self.y_ready = s("y_ready")
        self.summed = s("summed")
        self.stats = s("stats")
        self.moments = s("moments")
        self.var_eps = s("var_eps")
        self.pow_c = s("pow_c")
        self.rstd_ready = s("rstd_ready")
        self.normed = s("normed")
        self.tx_ready = s("tx_ready")
        self.xt_hi = s("xt_hi")
        self.xt_lo = s("xt_lo")
        self.stored = s("stored")

    def pool_setup(self):
        self.core.nc.gpsimd.memset(self.half[:], -0.5).then_inc(self.pow_c, 1)
        self.core.nc.gpsimd.wait_ge(self.pow_c, 1)

    def dve_stats(self, t):
        e, s = self.core.nc.vector, t % 2
        e.wait_ge(self.y_ready, t + 1)
        need(e, self.normed, t - 1)
        e.tensor_tensor(self.R[:, s], self.y[:, s, 0:D], self.core.X[:, t], ALU.add).then_inc(self.summed, 1)
        e.wait_ge(self.summed, t + 1)
        e.bn_stats(self.st[:, s, 0:6], self.R[:, s]).then_inc(self.stats, 1)
        e.wait_ge(self.stats, t + 1)
        e.bn_aggr(self.mv[:, s], self.st[:, s, 0:6]).then_inc(self.moments, 1)
        e.wait_ge(self.moments, t + 1)
        need(e, self.rstd_ready, t - 1)
        e.tensor_scalar(self.ve[:, s], self.mv[:, s, 1:2], EPS_LN, None, ALU.add).then_inc(self.var_eps, 1)

    def pool_rstd(self, t):
        e, s = self.core.nc.gpsimd, t % 2
        e.wait_ge(self.var_eps, t + 1)
        need(e, self.normed, t - 1)
        e.tensor_tensor(self.rstd[:, s], self.ve[:, s], self.half[:], ALU.pow).then_inc(self.rstd_ready, 1)

    def dve_norm(self, t):
        e, s = self.core.nc.vector, t % 2
        e.wait_ge(self.rstd_ready, t + 1)
        if self.last:
            need(e, self.stored, 16 * (t - 1))
            dst = self.xo[:, s]
        else:
            dst = self.core.X[:, t]
        e.tensor_scalar(dst, self.R[:, s], self.mv[:, s, 0:1], self.rstd[:, s, 0:1],
                        ALU.subtract, ALU.mult).then_inc(self.normed, 1)

    def pe_transpose(self, t):
        e = self.core.nc.tensor
        e.wait_ge(self.normed, t + 1)
        need(e, self.xt_lo, t)
        for k in range(KD):
            mm = e.transpose(self.tx[:, k * P:(k + 1) * P], self.core.X[:, t, k * P:(k + 1) * P], self.core.ident[:])
        mm.then_inc(self.tx_ready, 1)

    def act_xt(self, t):
        e = self.core.nc.scalar
        e.wait_ge(self.tx_ready, t + 1)
        src = self.tx[:, 0:D].rearrange("p (k n) -> p k n", k=KD)
        e.activation(self.core.XT[0][:, :, t * P:(t + 1) * P], src, ACT.Copy).then_inc(self.xt_hi, 1)

    def dve_xt(self, t):
        e = self.core.nc.vector
        e.wait_ge(self.xt_hi, t + 1)
        src = self.tx[:, 0:D].rearrange("p (k n) -> p k n", k=KD)
        e.tensor_tensor(self.core.XT[1][:, :, t * P:(t + 1) * P], src,
                        self.core.XT[0][:, :, t * P:(t + 1) * P].bitcast(F32), ALU.subtract).then_inc(self.xt_lo, 1)

    def sync_store(self, t):
        e = self.core.nc.sync
        e.wait_ge(self.normed, t + 1)
        if t:
            e.wait_ge(self.stored, 16 * t)
        e.dma_start(self.core.out[t * P:(t + 1) * P, :], self.xo[:, t % 2]).then_inc(self.stored, 16)


def start_phase(core, next_raw, next_bias):
    nc = core.nc
    with Phase(core, "start") as ph:
        xt = ph.sb("xt", [P, KD, NT * P])
        x_in = ph.sem("x_in")
        xt_in = ph.sem("xt_in")
        zeroed = ph.sem("zeroed")
        made = ph.sem("made")
        hi_done = ph.sem("hi_done")
        lo_done = ph.sem("lo_done")
        with nc.Block() as block:
            @block.sync
            def _(e):
                for k in range(KD):
                    e.dma_start(xt[:, k, :], core.arrays["xT"][k * P:(k + 1) * P, :]).then_inc(xt_in, 16)
                core.load_raw(e, next_raw)
                core.load_bias(e, next_bias)
                e.dma_start(core.X[:], core.arrays["x"].rearrange("(t p) d -> p t d", p=P)).then_inc(x_in, 16)
                e.wait_ge(x_in, 16)

            @block.gpsimd
            def _(e):
                e.memset(core.ident[:], 0.0).then_inc(zeroed, 1)
                e.wait_ge(zeroed, 1)
                e.affine_select(out=core.ident[:], in_=core.ident[:], compare_op=ALU.not_equal, fill=1.0,
                                base=0, pattern=[[-1, P]], channel_multiplier=1).then_inc(made, 1)
                e.wait_ge(made, 1)

            @block.scalar
            def _(e):
                e.wait_ge(xt_in, 16 * KD)
                for k in range(KD):
                    e.activation(core.XT[0][:, k, :], xt[:, k, :], ACT.Copy).then_inc(hi_done, 1)

            @block.vector
            def _(e):
                for k in range(KD):
                    e.wait_ge(hi_done, k + 1)
                    e.tensor_tensor(core.XT[1][:, k, :], xt[:, k, :], core.XT[0][:, k, :].bitcast(F32),
                                    ALU.subtract).then_inc(lo_done, 1)
                e.wait_ge(lo_done, KD)


def projection_phase(core, tag, q, k, v, v_cols, cols, q_scale, next_raw, qk_bias=None, v_bias=None, v_out=None):
    nc = core.nc
    with Phase(core, tag) as ph:
        n_w = KD * cols
        w = [ph.sb("w_hi", [P, n_w], F32R), ph.sb("w_lo", [P, n_w], F32R)]
        wv = [x[:].rearrange("p (k c) -> p k c", k=KD) for x in w]
        act_split, dve_split, w_ready, n_split = split_on(ph, w[0], w[1], n_w)
        fm = ph.ps("fm", [P, 4, 512])
        tm = ph.ps("tm", [P, 2, 512])
        fm_ready = ph.sem("fm_ready")
        fm_hi = ph.sem("fm_hi")
        fm_lo = ph.sem("fm_lo")
        tm_ready = ph.sem("tm_ready")
        tm_hi = ph.sem("tm_hi")
        tm_lo = ph.sem("tm_lo")
        tiles = [(dst, half, m) for m, (dst, half) in enumerate((x, h) for x in (q, k) for h in range(2))]
        two = v_out(1, 0, 0) is not None
        if two:
            vtmp = ph.sb("vtmp", [P, 2, v_cols])
            v_sum = ph.sem("v_sum")
        raw_n, bias_n = core.n_raw, core.n_bias
        with nc.Block() as block:
            @block.sync
            def _(e):
                e.wait_ge(w_ready, n_split)
                core.load_raw(e, next_raw)

            @block.scalar
            def _(e):
                act_split()
                n = 0
                for b in range(B):
                    for dst, half, m in tiles:
                        e.wait_ge(fm_ready, n + 1)
                        scale = q_scale if dst is q else 1.0
                        if qk_bias is None:
                            e.activation(dst[0][:, 2 * b + half, :], fm[:, n % 4, :], ACT.Copy,
                                         scale=scale).then_inc(fm_hi, 1)
                        else:
                            e.activation(dst[0][:, 2 * b + half, :], fm[:, n % 4, :], ACT.Identity,
                                         bias=qk_bias[:, m:m + 1]).then_inc(fm_hi, 1)
                        n += 1

            @block.vector
            def _(e):
                dve_split()
                n = nv = 0
                for b in range(B):
                    for dst, half, m in tiles:
                        e.wait_ge(fm_hi, n + 1)
                        e.scalar_tensor_tensor(
                            out=dst[1][:, 2 * b + half, :], in0=fm[:, n % 4, :],
                            scalar=(q_scale if dst is q else 1.0) if qk_bias is None else qk_bias[:, m:m + 1],
                            in1=dst[0][:, 2 * b + half, :].bitcast(F32),
                            op0=ALU.mult if qk_bias is None else ALU.add, op1=ALU.subtract).then_inc(fm_lo, 1)
                        n += 1
                    for kt in range(TPB):
                        e.wait_ge(tm_ready, nv + 1)
                        src = tm[:, nv % 2, 0:v_cols]
                        d0, d1 = v_out(0, b, kt), v_out(1, b, kt)
                        if len(d0.shape) == 3:
                            src = src.rearrange("p (a c) -> p a c", a=d0.shape[1])
                        if v_bias is not None:
                            vb = v_bias[:] if len(d0.shape) == 2 else v_bias[:].rearrange("p (a c) -> p a c", a=d0.shape[1])
                        if not two:
                            e.tensor_copy(d0, src).then_inc(tm_hi, 1)
                        else:
                            vf = vtmp[:, nv % 2]
                            need(e, tm_lo, nv - 1)
                            e.tensor_tensor(vf, src, vb, ALU.add).then_inc(v_sum, 1)
                            e.wait_ge(v_sum, nv + 1)
                            e.tensor_copy(d0, vf).then_inc(tm_hi, 1)
                            e.wait_ge(tm_hi, nv + 1)
                            e.tensor_tensor(d1, vf, d0.bitcast(F32), ALU.subtract).then_inc(tm_lo, 1)
                        nv += 1

            @block.tensor
            def _(e):
                e.wait_ge(w_ready, n_split)
                n = nv = 0
                for b in range(B):
                    for dst, half, m in tiles:
                        need(e, fm_lo, n - 3)
                        for kk in range(KD):
                            for j, (wi, xi) in enumerate(HI_LO):
                                mm = e.matmul(fm[:, n % 4, :], wv[wi][:, kk, m * P:(m + 1) * P],
                                              core.XT[xi][:, kk, b * S:(b + 1) * S],
                                              start=(kk == 0 and j == 0), stop=(kk == KD - 1 and j == 2))
                        mm.then_inc(fm_ready, 1)
                        n += 1
                    for kt in range(TPB):
                        need(e, v_sum if two else tm_hi, nv - 1)
                        t = b * TPB + kt
                        for kk in range(KD):
                            for j, (xi, wi) in enumerate(HI_LO):
                                mm = e.matmul(tm[:, nv % 2, 0:v_cols], core.XT[xi][:, kk, t * P:(t + 1) * P],
                                              wv[wi][:, kk, 2 * D:2 * D + v_cols],
                                              start=(kk == 0 and j == 0), stop=(kk == KD - 1 and j == 2))
                        mm.then_inc(tm_ready, 1)
                        nv += 1


QUADS = 4


def attention_phase(core, tag, q, k, V, O, heads, hd, o_at, residual_bias, next_raw):
    nc = core.nc
    G = heads
    NS = G
    REP = 4 // G
    NU = B * 2 * QUADS
    with Phase(core, tag) as ph:
        PT = core.lend(f"{tag}_PT", [P, 2, 4, S], F32, 0)
        QA = core.lend(f"{tag}_QA", [P, 4, S], F32R, 16384)
        KR = core.lend(f"{tag}_KR", [P, 2, S], F32, 24576)
        OT = core.lend(f"{tag}_OT", [P, 2, S], F32, 28672)
        KA = ph.sb("KA", [P, 4, G, S], F32R)
        VA = ph.sb("VA", [P, 4, TPB, 32 if G == 4 else 64])
        mask = ph.sb("mask", [P, G])
        MX = ph.sb("MX", [P, 2, 4, G])
        RI = ph.sb("RI", [P, 4, 4])
        SM = ph.ps("SM", [P, 2, S])
        ST = ph.ps("ST", [P, 4, S])
        PV = ph.ps("PV", [P, S])
        MISC = ph.ps("MISC", [P, S])
        q_in = [ph.sem(f"q_in{i}") for i in range(4)]
        k_in = [ph.sem(f"k_in{i}") for i in range(2)]
        mask_in = ph.sem("mask_in")
        zeroed = ph.sem("zeroed")
        ka_ready = ph.sem("ka_ready")
        va_ready = ph.sem("va_ready")
        sm_ready = ph.sem("sm_ready")
        mx_done = ph.sem("mx_done")
        mt_ready = ph.sem("mt_ready")
        m_done = ph.sem("m_done")
        st_ready = ph.sem("st_ready")
        exp_done = ph.sem("exp_done")
        pv_step = ph.sem("pv_step")
        ot_done = ph.sem("ot_done")
        to_ready = ph.sem("to_ready")
        ri_done = ph.sem("ri_done")
        os_done = ph.sem("os_done")
        o_done = ph.sem("o_done")
        bias_done = ph.sem("bias_done")
        seen_free = ph.sem("seen_free")
        zero_v = ph.sem("zero_v")
        bias_n = core.n_bias
        ROWS_M = 96

        def chunk(u, c):
            return [divmod(4 * c + i, G) for i in range(4)]

        def live(u):
            return not isinstance(u, int) or 0 <= u < NU

        def pe_max(e, u, r, c, items=range(4)):
            if not live(u):
                return
            if c == 0 and items[0] == 0:
                e.wait_ge(q_in[r], 12 * (u - r) + 48)
                e.wait_ge(ka_ready, G * u + G)
            for i in items:
                qt, g = chunk(u, c)[i]
                n = u * (4 * G) + (4 * c + i)
                need(e, mx_done, n - 1)
                e.matmul(SM[:, i % 2, :], QA[0:ROWS_M, r, qt * P:(qt + 1) * P], KA[0:ROWS_M, r, g, :],
                         start=True, stop=True).then_inc(sm_ready, 1)

        def dve_max(e, u, r, c, items=range(4)):
            if not live(u):
                return
            if c == 0 and items[0] == 0:
                need(e, mt_ready, u - 1)
            for i in items:
                qt, g = chunk(u, c)[i]
                e.wait_ge(sm_ready, u * (4 * G) + (4 * c + i + 1))
                e.tensor_reduce(MX[:, r % 2, qt, g:g + 1], SM[:, i % 2, :], AXX, ALU.max).then_inc(mx_done, 1)

        def pe_mt(e, u, r):
            if not live(u):
                return
            e.wait_ge(mx_done, u * (4 * G) + 4 * G)
            need(e, o_done, u - 2)
            for qt in range(4):
                mm = e.transpose(MISC[0:G, qt * P:(qt + 1) * P], MX[:, r % 2, qt, :], core.ident[:])
            mm.then_inc(mt_ready, 1)

        def dve_mrow(e, u, r):
            if not live(u):
                return
            e.wait_ge(mt_ready, u + 1)
            e.tensor_scalar(QA[ROWS_M:ROWS_M + G, r, :], MISC[0:G, :], -1.0, None, ALU.mult).then_inc(m_done, 1)

        def pe_scores(e, u, r, s, half):
            if not live(u):
                return
            if s == 0 and half == 0:
                e.wait_ge(m_done, u + 1)
            h = u * (2 * NS) + (2 * s + half)
            need(e, exp_done, h - 1)
            for a in (2 * half, 2 * half + 1):
                g, kt = a // REP, s * REP + a % REP
                mm = e.matmul(ST[:, a, :], KA[:, r, g, kt * P:(kt + 1) * P], QA[:, r, :], start=True, stop=True)
            mm.then_inc(st_ready, 1)

        def act_exp(e, u, s):
            if not live(u):
                return
            step = u * NS + s
            for half in range(2):
                e.wait_ge(st_ready, u * (2 * NS) + (2 * s + half + 1))
                if half == 0:
                    need(e, pv_step, step - 1)
                e.activation(PT[:, s % 2, 2 * half:2 * half + 2, :], ST[:, 2 * half:2 * half + 2, :],
                             ACT.Exp).then_inc(exp_done, 1)

        def pe_pv(e, u, r, s):
            if not live(u):
                return
            step = u * NS + s
            e.wait_ge(exp_done, u * (2 * NS) + (2 * s + 2))
            if s == 0:
                e.wait_ge(va_ready, u + 1)
                need(e, ot_done, u)
            for a in range(4):
                g, kt = a // REP, s * REP + a % REP
                va = VA[:, r, kt, 0:32] if G == 4 else VA[:, r, kt, 32 * g:32 * g + 32]
                mm = e.matmul(PV[32 * a:32 * a + 32, :], va, PT[:, s % 2, a, :], start=(s == 0), stop=(s == NS - 1),
                              tile_position=(0, 32 * a))
            mm.then_inc(pv_step, 1)

        def act_ot(e, u, r):
            if not live(u):
                return
            e.wait_ge(pv_step, u * NS + NS)
            need(e, to_ready, u - 1)
            e.activation(OT[:, r % 2, :], PV[:], ACT.Copy).then_inc(ot_done, 1)

        def pe_to(e, u, r):
            if not live(u):
                return
            e.wait_ge(ot_done, u + 1)
            e.wait_ge(m_done, min(u + 3, NU) if isinstance(u, int) else u + 3)
            need(e, o_done, u)
            for qt in range(4):
                mm = e.transpose(MISC[:, qt * P:(qt + 1) * P], OT[:, r % 2, qt * P:(qt + 1) * P], core.ident[:])
            mm.then_inc(to_ready, 1)

        def dve_out(e, u, r):
            if not live(u):
                return
            e.wait_ge(to_ready, u + 1)
            T = MISC[:].rearrange("p (t a c) -> p t a c", t=4, a=4)
            if G == 4:
                need(e, o_done, u)
                e.reciprocal(RI[:], T[:, :, :, hd]).then_inc(ri_done, 1)
                e.wait_ge(ri_done, u + 1)
                e.tensor_tensor(o_at(u, r), T[:, :, :, 0:hd],
                                RI[:].unsqueeze(3).broadcast_to([P, 4, 4, hd]), ALU.mult).then_inc(o_done, 1)
            else:
                T2 = MISC[:].rearrange("p (t g h c) -> p t g h c", t=4, g=2, h=2)
                need(e, o_done, u)
                e.tensor_copy(OP[:], T2[:, :, :, 0, 0:hd + 1]).then_inc(op_done, 1)
                e.wait_ge(op_done, 2 * u + 1)
                e.tensor_tensor(OP[:], OP[:], T2[:, :, :, 1, 0:hd + 1], ALU.add).then_inc(op_done, 1)
                e.wait_ge(op_done, 2 * u + 2)
                e.reciprocal(RI[:, :, 0:G], OP[:, :, :, hd]).then_inc(ri_done, 1)
                e.wait_ge(ri_done, u + 1)
                for g in range(2):
                    mm = e.tensor_tensor(o_at(u, r, g), OP[:, :, g, 0:hd],
                                         RI[:, :, g:g + 1].broadcast_to([P, 4, hd]), ALU.mult)
                mm.then_inc(o_done, 1)
        if G == 2:
            OP = ph.sb("OP", [P, 4, 2, hd + 1])
            op_done = ph.sem("op_done")

        def run(e, emit):
            for u in range(-2, 3):
                emit(u, u % 4)
            with e.Fori(0, (NU - 8) // 4) as i:
                for c in range(3, 7):
                    emit(4 * i + c, c % 4)
            for u in range(NU - 5, NU + 1):
                emit(u, u % 4)

        with nc.Block() as block:
            @block.sync
            def _(e):
                e.dma_start(mask[:], core.arrays[f"mask{G}"]).then_inc(mask_in, 16)
                core.load_raw(e, next_raw)

                def emit(i, r):
                    u = 4 * i + r
                    need(e, st_ready, (u - 3) * (2 * NS))
                    e.sem_inc(seen_free, 1)
                    for n, part in enumerate((0, 0, 1)):
                        e.dma_start(QA[32 * n:32 * n + 32, r, :].bitcast(F32),
                                    q[part][32 * r:32 * r + 32, bass.ds(i, 1), :].bitcast(F32)
                                    ).then_inc(q_in[r], 16)
                    need(e, ka_ready, (u - 1) * G)
                    e.sem_inc(seen_free, 1)
                    for n, part in enumerate((0, 1, 0)):
                        e.dma_start(KR[32 * n:32 * n + 32, r % 2, :],
                                    k[part][32 * r:32 * r + 32, bass.ds(i, 1), :].bitcast(F32)).then_inc(k_in[r % 2], 16)
                e.wait_ge(zeroed, 1)
                for r in range(4):
                    emit(0, r)
                with e.Fori(1, 8) as i:
                    for r in range(4):
                        emit(i, r)

            @block.gpsimd
            def _(e):
                e.wait_ge(mask_in, 16)
                e.wait_ge(zeroed, 1)
                if residual_bias:
                    e.wait_ge(core.bias_loaded, bias_n)
                    e.tensor_tensor(core.X[:], core.X[:], core.bias[:].unsqueeze(1).broadcast_to([P, NT, D]),
                                    ALU.add).then_inc(bias_done, 1)

                def emit(i, r):
                    u = 4 * i + r
                    e.wait_ge(k_in[r % 2], 96 * i + 48 * (r // 2 + 1))
                    need(e, st_ready, (u - 3) * (2 * NS))
                    for g in range(G):
                        e.tensor_tensor(KA[:, r, g, :], KR[:, r % 2, :], mask[:, g:g + 1].broadcast_to([P, S]),
                                        ALU.mult).then_inc(ka_ready, 1)
                    need(e, pv_step, (u - 3) * NS)
                    if G == 4:
                        e.tensor_copy(VA[:, r, :, 0:hd], V[:, bass.ds(i, 1), :, r * hd:(r + 1) * hd]
                                      ).then_inc(va_ready, 1)
                    else:
                        for g in range(G):
                            mm = e.tensor_copy(VA[:, r, :, 32 * g:32 * g + hd],
                                               V[:, bass.ds(i, 1), :, (2 * r + g) * hd:(2 * r + g + 1) * hd])
                        mm.then_inc(va_ready, 1)
                for r in range(4):
                    emit(0, r)
                with e.Fori(1, 8) as i:
                    for r in range(4):
                        emit(i, r)
                if residual_bias:
                    e.wait_ge(bias_done, 1)

            @block.scalar
            def _(e):
                def emit(u, r):
                    for s in range(NS):
                        act_exp(e, u, s)
                        if s == 0:
                            act_ot(e, u - 1, (r - 1) % 4)
                run(e, emit)

            @block.vector
            def _(e):
                e.memset(QA[ROWS_M:P, :, :].bitcast(F32), 0.0).then_inc(zero_v, 1)
                e.memset(KR[ROWS_M:P, :, :], 1.0).then_inc(zero_v, 1)
                e.memset(VA[:], 0.0).then_inc(zero_v, 1)
                e.wait_ge(zero_v, 3)
                ones = VA[:, :, :, hd:hd + 1] if G == 4 else \
                    VA[:].rearrange("p r t (g c) -> p r t g c", g=2)[:, :, :, :, hd:hd + 1]
                e.memset(ones, 1.0).then_inc(zeroed, 1)

                def emit(u, r):
                    for s in range(NS - 1):
                        dve_max(e, u + 1, (r + 1) % 4, s + 1)
                    dve_mrow(e, u + 1, (r + 1) % 4)
                    dve_max(e, u + 2, (r + 2) % 4, 0, [0, 1])
                    dve_out(e, u - 1, (r - 1) % 4)
                    dve_max(e, u + 2, (r + 2) % 4, 0, [2, 3])
                run(e, emit)
                e.wait_ge(o_done, NU)

            @block.tensor
            def _(e):
                e.wait_ge(zeroed, 1)

                def emit(u, r):
                    r1, r2, rp = (r + 1) % 4, (r + 2) % 4, (r - 1) % 4
                    for s in range(NS - 1):
                        pe_max(e, u + 1, r1, s + 1, [0])
                        pe_scores(e, u, r, s, 0)
                        pe_max(e, u + 1, r1, s + 1, [1])
                        pe_scores(e, u, r, s, 1)
                        pe_max(e, u + 1, r1, s + 1, [2])
                        if s == 0:
                            pe_pv(e, u - 1, rp, NS - 1)
                        else:
                            pe_pv(e, u, r, s - 1)
                        pe_max(e, u + 1, r1, s + 1, [3])
                    pe_scores(e, u, r, NS - 1, 0)
                    pe_scores(e, u, r, NS - 1, 1)
                    pe_mt(e, u + 1, r1)
                    pe_max(e, u + 2, r2, 0, [0])
                    pe_pv(e, u, r, NS - 2)
                    pe_max(e, u + 2, r2, 0, [1])
                    pe_to(e, u - 1, rp)
                    pe_max(e, u + 2, r2, 0, [2, 3])
                run(e, emit)


def output_phase(core, tag, o_tile, next_raw, next_bias=None):
    nc = core.nc
    with Phase(core, tag) as ph:
        w = [ph.sb("w_hi", [P, KD * D], F32R), ph.sb("w_lo", [P, KD * D], F32R)]
        wv = [x[:].rearrange("p (k c) -> p k c", k=KD) for x in w]
        act_split, dve_split, w_ready, n_split = split_on(ph, w[0], w[1], KD * D)
        OT = [ph.sb("OT_hi", [P, 2, D], F32R), ph.sb("OT_lo", [P, 2, D], F32R)]
        TP = ph.ps("TP", [P, 2, 512])
        tail = Tail(ph)
        tp_ready = ph.sem("tp_ready")
        ot_hi = ph.sem("ot_hi")
        ot_lo = ph.sem("ot_lo")
        with nc.Block() as block:
            @block.sync
            def _(e):
                e.wait_ge(w_ready, n_split)
                core.load_raw(e, next_raw)
                if next_bias:
                    core.load_bias(e, next_bias)

            @block.gpsimd
            def _(e):
                tail.pool_setup()
                for t in range(NT):
                    tail.pool_rstd(t)

            @block.tensor
            def _(e):
                for i in range(NT + 3):
                    if i < NT:
                        need(e, ot_lo, i - 1)
                        for k in range(KD):
                            mm = e.transpose(TP[:, i % 2, k * P:(k + 1) * P], o_tile(i, k), core.ident[:])
                        mm.then_inc(tp_ready, 1)
                    t = i - 1
                    if 0 <= t < NT:
                        if t == 0:
                            e.wait_ge(w_ready, n_split)
                        e.wait_ge(ot_lo, t + 1)
                        need(e, tail.summed, t - 1)
                        for k in range(KD):
                            for j, (oi, wi) in enumerate(HI_LO):
                                mm = e.matmul(tail.y[:, t % 2, 0:D], OT[oi][:, t % 2, k * P:(k + 1) * P],
                                              wv[wi][:, k, :], start=(k == 0 and j == 0),
                                              stop=(k == KD - 1 and j == 2))
                        mm.then_inc(tail.y_ready, 1)
                    if 0 <= i - 3 < NT:
                        tail.pe_transpose(i - 3)

            @block.scalar
            def _(e):
                act_split()
                for i in range(NT + 3):
                    if i < NT:
                        e.wait_ge(tp_ready, i + 1)
                        need(e, tail.y_ready, i - 1)
                        e.activation(OT[0][:, i % 2], TP[:, i % 2, 0:D], ACT.Copy).then_inc(ot_hi, 1)
                    if 0 <= i - 3 < NT:
                        tail.act_xt(i - 3)

            @block.vector
            def _(e):
                dve_split()
                for i in range(NT + 3):
                    if i < NT:
                        e.wait_ge(ot_hi, i + 1)
                        e.tensor_tensor(OT[1][:, i % 2], TP[:, i % 2, 0:D], OT[0][:, i % 2].bitcast(F32),
                                        ALU.subtract).then_inc(ot_lo, 1)
                    if 0 <= i - 1 < NT:
                        tail.dve_stats(i - 1)
                    if 0 <= i - 2 < NT:
                        tail.dve_norm(i - 2)
                    if 0 <= i - 3 < NT:
                        tail.dve_xt(i - 3)
                e.wait_ge(tail.xt_lo, NT)


def feed_forward_phase(core, tag, inter, prepare, next_raw, next_bias=None):
    nc = core.nc
    M = [min(P, inter - a) for a in range(0, inter, P)]
    NM = len(M)
    cols = 2 * KD * inter + NM * D
    with Phase(core, tag) as ph:
        w = [ph.sb("w_hi", [P, cols], F32R), ph.sb("w_lo", [P, cols], F32R)]
        up = [x[:, 0:2 * KD * inter].rearrange("p (s k c) -> p s k c", s=2, k=KD) for x in w]
        down = [x[:, 2 * KD * inter:cols].rearrange("p (m c) -> p m c", m=NM) for x in w]
        prepare(core, tag, w, cols)
        H = [ph.sb("H_hi", [P, 2, NM, S], F32R), ph.sb("H_lo", [P, 2, NM, S], F32R)]
        SU = ph.sb("SU", [P, 2, S])
        HF = ph.sb("HF", [P, 2, S])
        UG = ph.ps("UG", [P, 2, 2, S])
        tail = Tail(ph)
        up_ready = ph.sem("up_ready")
        gate_ready = ph.sem("gate_ready")
        silu_done = ph.sem("silu_done")
        h_done = ph.sem("h_done")
        h_hi = ph.sem("h_hi")
        h_lo = ph.sem("h_lo")

        def tail_steps(c):
            return range(c * TPB, (c + 1) * TPB + (2 if c == B - 1 else 0))

        with nc.Block() as block:
            @block.sync
            def _(e):
                core.load_raw(e, next_raw)
                if next_bias:
                    core.load_bias(e, next_bias)

            @block.gpsimd
            def _(e):
                tail.pool_setup()
                for t in range(NT):
                    tail.pool_rstd(t)

            @block.tensor
            def _(e):
                def ups(c):
                    for m, rows in enumerate(M):
                        n = c * NM + m
                        for side, (free, ready) in enumerate(((silu_done, up_ready), (h_done, gate_ready))):
                            need(e, free, n - 1)
                            for k in range(KD):
                                for j, (wi, xi) in enumerate(HI_LO):
                                    mm = e.matmul(UG[0:rows, n % 2, side, :], up[wi][:, side, k, m * P:m * P + rows],
                                                  core.XT[xi][:, k, c * S:(c + 1) * S],
                                                  start=(k == 0 and j == 0), stop=(k == KD - 1 and j == 2))
                            mm.then_inc(ready, 1)

                def downs(c):
                    e.wait_ge(h_lo, (c + 1) * NM)
                    for t in tail_steps(c):
                        if t < NT:
                            need(e, tail.summed, t - 1)
                            a = (t % TPB) * P
                            for m, rows in enumerate(M):
                                for j, (hi, wi) in enumerate(HI_LO):
                                    mm = e.matmul(tail.y[:, t % 2, 0:D], H[hi][0:rows, c % 2, m, a:a + P],
                                                  down[wi][0:rows, m, :],
                                                  start=(m == 0 and j == 0), stop=(m == NM - 1 and j == 2))
                            mm.then_inc(tail.y_ready, 1)
                        if t >= 2:
                            tail.pe_transpose(t - 2)
                ups(0)
                for c in range(B):
                    if c + 1 < B:
                        ups(c + 1)
                    downs(c)

            @block.scalar
            def _(e):
                def hidden(c):
                    for m in range(NM + 1):
                        n = c * NM + m
                        if m < NM:
                            rows = M[m]
                            e.wait_ge(up_ready, n + 1)
                            need(e, h_done, n - 1)
                            e.activation(SU[0:rows, n % 2], UG[0:rows, n % 2, 0, :], ACT.Silu).then_inc(silu_done, 1)
                        if m >= 1:
                            rows = M[m - 1]
                            e.wait_ge(h_done, n)
                            if m == 1 and c >= 2:
                                e.wait_ge(tail.y_ready, (c - 1) * TPB)
                            e.activation(H[0][0:rows, c % 2, m - 1], HF[0:rows, (n - 1) % 2], ACT.Copy).then_inc(h_hi, 1)
                hidden(0)
                for c in range(B):
                    if c + 1 < B:
                        hidden(c + 1)
                    for t in tail_steps(c):
                        if t >= 2:
                            tail.act_xt(t - 2)

            @block.vector
            def _(e):
                def hidden(c):
                    for m in range(NM + 1):
                        n = c * NM + m
                        if m < NM:
                            rows = M[m]
                            e.wait_ge(gate_ready, n + 1)
                            e.wait_ge(silu_done, n + 1)
                            need(e, h_lo, n - 1)
                            need(e, h_hi, n - 1)
                            e.tensor_tensor(HF[0:rows, n % 2], UG[0:rows, n % 2, 1, :], SU[0:rows, n % 2],
                                            ALU.mult).then_inc(h_done, 1)
                        if m >= 1:
                            rows = M[m - 1]
                            e.wait_ge(h_hi, n)
                            e.wait_ge(h_done, n)
                            e.tensor_tensor(H[1][0:rows, c % 2, m - 1], HF[0:rows, (n - 1) % 2],
                                            H[0][0:rows, c % 2, m - 1].bitcast(F32), ALU.subtract).then_inc(h_lo, 1)
                hidden(0)
                for c in range(B):
                    if c + 1 < B:
                        hidden(c + 1)
                    for t in tail_steps(c):
                        if t < NT:
                            tail.dve_stats(t)
                        if 1 <= t and t - 1 < NT:
                            tail.dve_norm(t - 1)
                        if t >= 2:
                            tail.dve_xt(t - 2)
                e.wait_ge(tail.xt_lo, NT)


def prepare_ternary(core, tag, w, cols):
    nc = core.nc
    n_loaded = core.n_raw
    parts = [(0, 2048), (2048, 4096), (4096, 6144)]
    CH = 1024
    with Phase(core, tag + "t") as ph:
        absum = ph.sb("absum", [P, 3])
        ones = ph.sb("ones", [P, P])
        scale = ph.sb("scale", [P, 3])
        inv = ph.sb("inv", [P, 3])
        up_t = ph.sb("above", [P, 2, CH])
        dn_t = ph.sb("below", [P, 2, CH])
        junk = ph.sb("junk", [P, 2048])
        total = ph.ps("total", [P, 3])
        sem = {x: ph.sem(x) for x in ("ones_set", "abs_done", "total_ready", "scaled", "dve", "whole", "hi_done", "lo_done")}
        pieces = [(m, a) for m, (lo, hi) in enumerate(parts) for a in range(lo, hi, CH)]
        with nc.Block() as block:
            @block.scalar
            def _(e):
                e.wait_ge(core.raw_loaded, n_loaded)
                for m, (a, b) in enumerate(parts):
                    need(e, sem["abs_done"], m)
                    e.activation(junk[:], core.raw[:, a:b], ACT.Abs, accum_out=absum[:, m:m + 1]
                                 ).then_inc(sem["abs_done"], 1)
                for n, (m, a) in enumerate(pieces):
                    e.wait_ge(sem["whole"], n + 1)
                    e.activation(w[0][:, a:a + CH], core.raw[:, a:a + CH], ACT.Copy).then_inc(sem["hi_done"], 1)

            @block.tensor
            def _(e):
                e.wait_ge(sem["ones_set"], 1)
                e.wait_ge(sem["abs_done"], 3)
                e.matmul(total[:], ones[:], absum[:], start=True, stop=True).then_inc(sem["total_ready"], 1)

            @block.vector
            def _(e):
                e.memset(ones[:], 1.0).then_inc(sem["ones_set"], 1)
                e.wait_ge(sem["total_ready"], 1)
                e.tensor_scalar(scale[:], total[:], 1.0 / (D * 1024), 1e-8, ALU.mult, ALU.add).then_inc(sem["scaled"], 1)
                e.wait_ge(sem["scaled"], 1)
                e.reciprocal(inv[:], scale[:]).then_inc(sem["scaled"], 1)
                e.wait_ge(sem["scaled"], 2)
                d = 0
                for n, (m, a) in enumerate(pieces):
                    s, raw = n % 2, core.raw[:, a:a + CH]
                    above, below = up_t[:, s], dn_t[:, s]
                    e.tensor_scalar(above, raw, inv[:, m:m + 1], 0.5, ALU.mult, ALU.is_gt).then_inc(sem["dve"], 1)
                    e.tensor_scalar(below, raw, inv[:, m:m + 1], -0.5, ALU.mult, ALU.is_lt).then_inc(sem["dve"], 1)
                    e.wait_ge(sem["dve"], d + 2)
                    e.tensor_tensor(above, above, below, ALU.subtract).then_inc(sem["dve"], 1)
                    e.wait_ge(sem["dve"], d + 3)
                    e.scalar_tensor_tensor(out=above, in0=above, scalar=scale[:, m:m + 1], in1=raw,
                                           op0=ALU.mult, op1=ALU.subtract).then_inc(sem["dve"], 1)
                    d += 4
                    e.wait_ge(sem["dve"], d)
                    e.tensor_tensor(raw, raw, above, ALU.add).then_inc(sem["whole"], 1)
                    e.wait_ge(sem["hi_done"], n + 1)
                    e.tensor_tensor(w[1][:, a:a + CH], raw, w[0][:, a:a + CH].bitcast(F32), ALU.subtract
                                    ).then_inc(sem["lo_done"], 1)
                e.wait_ge(sem["lo_done"], len(pieces))


def wide_attention_phase(core, tag, q, k, v, O, scale, next_raw):
    nc = core.nc
    with Phase(core, tag) as ph:
        SP = ph.ps("scores", [P, 2, S])
        TP = ph.ps("TP", [P, 2, S])
        CP = ph.ps("context", [P, 2, S])
        PR = core.lend(f"{tag}_probs", [P, 2, S], F32, 0)
        PT = [core.lend(f"{tag}_PT_{n}", [P, 2, TPB, P], F32R, 4096 * (i + 1)) for i, n in enumerate(("hi", "lo"))]
        mx = ph.sb("mx", [P, 2, 1])
        nm = ph.sb("nm", [P, 2, 1])
        rs = ph.sb("rs", [P, 2, 1])
        ri = ph.sb("ri", [P, 2, 1])
        s_ready = ph.sem("s_ready")
        mx_done = ph.sem("mx_done")
        nm_done = ph.sem("nm_done")
        exp_done = ph.sem("exp_done")
        ri_done = ph.sem("ri_done")
        p_done = ph.sem("p_done")
        tp_ready = ph.sem("tp_ready")
        pt_hi = ph.sem("pt_hi")
        pt_lo = ph.sem("pt_lo")
        c_ready = ph.sem("c_ready")
        c_done = ph.sem("c_done")
        bias_done = ph.sem("bias_done")
        bias_n = core.n_bias
        with nc.Block() as block:
            @block.sync
            def _(e):
                core.load_raw(e, next_raw)

            @block.gpsimd
            def _(e):
                e.wait_ge(core.bias_loaded, bias_n)
                e.tensor_tensor(core.X[:], core.X[:], core.bias[:].unsqueeze(1).broadcast_to([P, NT, D]),
                                ALU.add).then_inc(bias_done, 1)
                e.wait_ge(bias_done, 1)

            @block.tensor
            def _(e):
                for i in range(NT + 2):
                    if i < NT:
                        b, qt = divmod(i, TPB)
                        need(e, exp_done, i - 1)
                        for h in range(KD):
                            for j, (qi, ki) in enumerate(HI_LO):
                                mm = e.matmul(SP[:, i % 2, :], q[qi][:, 2 * b + h, qt * P:(qt + 1) * P],
                                              k[ki][:, 2 * b + h, :], start=(h == 0 and j == 0),
                                              stop=(h == KD - 1 and j == 2))
                        mm.then_inc(s_ready, 1)
                    t = i - 1
                    if 0 <= t < NT:
                        e.wait_ge(p_done, t + 1)
                        need(e, pt_lo, t - 1)
                        for kt in range(TPB):
                            mm = e.transpose(TP[:, t % 2, kt * P:(kt + 1) * P], PR[:, t % 2, kt * P:(kt + 1) * P],
                                             core.ident[:])
                        mm.then_inc(tp_ready, 1)
                    t = i - 2
                    if 0 <= t < NT:
                        b = t // TPB
                        e.wait_ge(pt_lo, t + 1)
                        need(e, c_done, t - 1)
                        for kt in range(TPB):
                            for j, (pi, vi) in enumerate(HI_LO):
                                mm = e.matmul(CP[:, t % 2, 0:D], PT[pi][:, t % 2, kt, :], v[vi][:, b * TPB + kt, :],
                                              start=(kt == 0 and j == 0), stop=(kt == TPB - 1 and j == 2))
                        mm.then_inc(c_ready, 1)

            @block.scalar
            def _(e):
                for i in range(NT + 2):
                    if i < NT:
                        e.wait_ge(nm_done, i + 1)
                        need(e, tp_ready, i - 1)
                        e.activation(PR[:, i % 2, :], SP[:, i % 2, :], ACT.Exp, bias=nm[:, i % 2], scale=scale,
                                     accum_out=rs[:, i % 2]).then_inc(exp_done, 1)
                    t = i - 1
                    if 0 <= t < NT:
                        e.wait_ge(tp_ready, t + 1)
                        need(e, c_ready, t - 1)
                        e.activation(PT[0][:, t % 2], TP[:, t % 2, :].rearrange("p (t n) -> p t n", t=TPB),
                                     ACT.Copy).then_inc(pt_hi, 1)
                    t = i - 2
                    if 0 <= t < NT:
                        e.wait_ge(c_ready, t + 1)
                        e.activation(O[:, t, :], CP[:, t % 2, 0:D], ACT.Copy).then_inc(c_done, 1)

            @block.vector
            def _(e):
                for i in range(NT + 2):
                    if i < NT:
                        e.wait_ge(s_ready, i + 1)
                        need(e, nm_done, i - 1)
                        e.tensor_reduce(mx[:, i % 2], SP[:, i % 2, :], AXX, ALU.max).then_inc(mx_done, 1)
                        e.wait_ge(mx_done, i + 1)
                        need(e, exp_done, i - 1)
                        e.tensor_scalar(nm[:, i % 2], mx[:, i % 2], -scale, None, ALU.mult).then_inc(nm_done, 1)
                    t = i - 1
                    if 0 <= t < NT:
                        e.wait_ge(exp_done, t + 1)
                        need(e, p_done, t - 1)
                        e.reciprocal(ri[:, t % 2], rs[:, t % 2]).then_inc(ri_done, 1)
                        e.wait_ge(ri_done, t + 1)
                        e.tensor_scalar(PR[:, t % 2, :], PR[:, t % 2, :], ri[:, t % 2], None,
                                        ALU.mult).then_inc(p_done, 1)
                    t = i - 2
                    if 0 <= t < NT:
                        e.wait_ge(pt_hi, t + 1)
                        e.tensor_tensor(PT[1][:, t % 2], TP[:, t % 2, :].rearrange("p (t n) -> p t n", t=TPB),
                                        PT[0][:, t % 2].bitcast(F32), ALU.subtract).then_inc(pt_lo, 1)
                e.wait_ge(pt_lo, NT)


def routing_phase(core, tag, comb, n_exp, n_top, eps=0.0, e_scale=None, after=None):
    nc = core.nc
    n_s = 8 - n_top
    W = n_exp + n_s
    with Phase(core, tag) as ph:
        n_w = KD * n_exp
        w = [ph.sb("w_hi", [P, n_w], F32R), ph.sb("w_lo", [P, n_w], F32R)]
        wv = [x[:].rearrange("p (k c) -> p k c", k=KD) for x in w]
        act_split, dve_split, w_ready, n_split = split_on(ph, w[0], w[1], n_w)
        LG = ph.ps("logits", [P, NT, n_exp])
        mx = ph.sb("mx", [P, NT])
        ex = ph.sb("ex", [P, NT, n_exp])
        sm = ph.sb("sm", [P, NT])
        probs = ph.sb("probs", [P, NT, W])
        top8 = ph.sb("top8", [P, NT, 8])
        vals = ph.sb("vals", [P, NT, 8])
        rest = ph.sb("rest", [P, NT, W])
        ws = ph.sb("ws", [P, NT])
        lg_ready = ph.sem("lg_ready")
        ex_in = ph.sem("ex_in")
        ex_done = ph.sem("ex_done")
        dv = ph.sem("dv")
        es_in = ph.sem("es_in")
        if e_scale:
            es = ph.sb("es", [P, n_exp])
        with nc.Block() as block:
            @block.sync
            def _(e):
                if e_scale:
                    e.dma_start(es[:], core.arrays[e_scale].partition_broadcast(P)).then_inc(es_in, 16)

            @block.tensor
            def _(e):
                e.wait_ge(w_ready, n_split)
                for t in range(NT):
                    for k in range(KD):
                        for j, (xi, wi) in enumerate(HI_LO):
                            mm = e.matmul(LG[:, t, :], core.XT[xi][:, k, t * P:(t + 1) * P], wv[wi][:, k, :],
                                          start=(k == 0 and j == 0), stop=(k == KD - 1 and j == 2))
                mm.then_inc(lg_ready, 1)

            @block.scalar
            def _(e):
                act_split()
                e.wait_ge(ex_in, 1)
                e.activation(ex[:], ex[:], ACT.Exp).then_inc(ex_done, 1)

            @block.vector
            def _(e):
                dve_split()
                for j in range(n_s):
                    e.memset(probs[:, :, n_exp + j:n_exp + j + 1], -1.0 - j).then_inc(dv, 1)
                    e.memset(vals[:, :, n_top + j:n_top + j + 1], -1.0 - j).then_inc(dv, 1)
                c = 2 * n_s
                e.wait_ge(lg_ready, 1)
                e.tensor_reduce(mx[:], LG[:], AXX, ALU.max).then_inc(dv, 1)
                c += 1
                e.wait_ge(dv, c)
                e.tensor_tensor(ex[:], LG[:], mx[:].unsqueeze(2).broadcast_to([P, NT, n_exp]),
                                ALU.subtract).then_inc(ex_in, 1)
                e.wait_ge(ex_done, 1)
                e.tensor_reduce(sm[:], ex[:], AXX, ALU.add).then_inc(dv, 1)
                c += 1
                e.wait_ge(dv, c)
                e.reciprocal(ws[:], sm[:]).then_inc(dv, 1)
                c += 1
                e.wait_ge(dv, c)
                e.tensor_tensor(probs[:, :, 0:n_exp], ex[:], ws[:].unsqueeze(2).broadcast_to([P, NT, n_exp]),
                                ALU.mult).then_inc(dv, 1)
                c += 1
                e.wait_ge(dv, c)
                for t in range(NT):
                    e.max(top8[:, t, :], probs[:, t, 0:n_exp]).then_inc(dv, 1)
                c += NT
                e.wait_ge(dv, c)
                e.tensor_copy(vals[:, :, 0:n_top], top8[:, :, 0:n_top]).then_inc(dv, 1)
                e.tensor_reduce(sm[:], top8[:, :, 0:n_top], AXX, ALU.add).then_inc(dv, 1)
                c += 2
                e.wait_ge(dv, c)
                for t in range(NT):
                    e.match_replace(out=rest[:, t, :], in_to_replace=vals[:, t, :], in_values=probs[:, t, :],
                                    imm_value=0.0).then_inc(dv, 1)
                if eps:
                    e.tensor_scalar(sm[:], sm[:], eps, None, ALU.add).then_inc(dv, 1)
                    c += 1
                    e.wait_ge(dv, c + NT)
                e.reciprocal(ws[:], sm[:]).then_inc(dv, 1)
                c += NT + 1
                e.wait_ge(dv, c)
                e.tensor_tensor(ex[:], probs[:, :, 0:n_exp], rest[:, :, 0:n_exp], ALU.subtract).then_inc(dv, 1)
                c += 1
                e.wait_ge(dv, c)
                if e_scale:
                    e.tensor_tensor(ex[:], ex[:], ws[:].unsqueeze(2).broadcast_to([P, NT, n_exp]),
                                    ALU.mult).then_inc(dv, 1)
                    c += 1
                    e.wait_ge(dv, c)
                    e.wait_ge(es_in, 16)
                    e.tensor_tensor(comb, ex[:], es[:].unsqueeze(1).broadcast_to([P, NT, n_exp]),
                                    ALU.mult).then_inc(dv, 1)
                else:
                    e.tensor_tensor(comb, ex[:], ws[:].unsqueeze(2).broadcast_to([P, NT, n_exp]),
                                    ALU.mult).then_inc(dv, 1)
                c += 1
                e.wait_ge(dv, c)


def experts_phase(core, tag, comb, n_exp, inter, next_raw, table, indices, looked_up):
    nc = core.nc
    N_LUT = 16
    LK_COLS = sum(cols for _, cols in indices)
    LK_W = LK_COLS // (n_exp * B // 2)
    assert LK_W * n_exp * B // 2 == LK_COLS
    NM = inter // P
    GU, DN = KD * 2 * inter, NM * D
    NG = n_exp * B
    with Phase(core, tag) as ph:
        rawe = ph.sb("rawe", [P, GU + DN])
        w = [ph.sb("w_hi", [P, 2, GU + DN], F32R), ph.sb("w_lo", [P, 2, GU + DN], F32R)]
        up = [x[:, :, 0:GU].rearrange("p e (k c) -> p e k c", k=KD) for x in w]
        down = [x[:, :, GU:GU + DN].rearrange("p e (m c) -> p e m c", m=NM) for x in w]
        H = [ph.sb("H_hi", [P, 2, NM, S], F32R), ph.sb("H_lo", [P, 2, NM, S], F32R)]
        SU = ph.sb("SU", [P, 2, S])
        HF = ph.sb("HF", [P, 2, S])
        lut = ph.sb("lut", [P, N_LUT])
        LK = ph.sb("looked_up", [P, LK_COLS])
        idx = ph.sb("idx", [P, LK_W])
        term = ph.sb("term", [P, 2, LK_W])
        total = ph.sb("total", [P, LK_W])
        lk_in = ph.sem("lk_in")
        lk = ph.sem("lk")
        lk_out = ph.sem("lk_out")
        UG = ph.ps("UG", [P, 2, 2, S])
        Y = ph.ps("Y", [P, TPB, S])
        rawe_in = ph.sem("rawe_in")
        rawe_free = ph.sem("rawe_free")
        whole = ph.sem("whole")
        up_ready = ph.sem("up_ready")
        gate_ready = ph.sem("gate_ready")
        silu_done = ph.sem("silu_done")
        h_done = ph.sem("h_done")
        h_hi = ph.sem("h_hi")
        h_lo = ph.sem("h_lo")
        y_ready = ph.sem("y_ready")
        added = ph.sem("added")
        src_gu, src_dn = core.arrays[tag + "_gu"], core.arrays[tag + "_dn"]

        def run(e, emit, at_first=None):
            for g in range(3):
                emit(g, g % 8)
            loops = (NG - 1 - 3) // 8
            with e.Fori(0, loops) as i:
                for c in range(3, 11):
                    emit(8 * i + c, c % 8)
            for g in range(3 + 8 * loops, NG):
                emit(g, g % 8)

        with nc.Block() as block:
            @block.sync
            def _(e):
                core.load_raw(e, next_raw)

                def load(x):
                    e.dma_start(rawe[:, 0:GU], src_gu[bass.ds(x, 1), :, :].rearrange("e p c -> (e p) c")).then_inc(rawe_in, 16)
                    e.dma_start(rawe[:, GU:GU + DN], src_dn[bass.ds(x, 1), :, :].rearrange("e p c -> (e p) c")).then_inc(rawe_in, 16)
                load(0)
                e.dma_start(lut[:], core.arrays[table].partition_broadcast(P)).then_inc(lk_in, 16)
                at = 0
                for name, cols in indices:
                    e.dma_start(LK[:, at:at + cols].bitcast(I32), core.arrays[name]).then_inc(lk_in, 16)
                    at += cols
                for x in range(1, n_exp):
                    e.wait_ge(rawe_free, x)
                    load(x)
                e.wait_ge(lk, N_LUT * NG)
                e.dma_start(core.arrays[looked_up], LK[:]).then_inc(lk_out, 16)
                e.wait_ge(lk_out, 16)

            @block.gpsimd
            def _(e):
                for x in range(n_exp):
                    e.wait_ge(rawe_in, 32 * (x + 1))
                    need(e, y_ready, NT * (x - 1))
                    e.tensor_copy(w[0][:, x % 2, :], rawe[:]).then_inc(whole, 1)
                    e.wait_ge(whole, x + 1)
                    e.tensor_tensor(w[1][:, x % 2, :], rawe[:], w[0][:, x % 2, :].bitcast(F32),
                                    ALU.subtract).then_inc(rawe_free, 1)

            @block.tensor
            def _(e):
                def ups(g, c):
                    x, ch = (c // 4) % 2, c % 4
                    if ch == 0:
                        e.wait_ge(rawe_free, (g - c) // 4 + (c // 4 + 1))
                    for m in range(NM):
                        n = NM * g + m
                        for side, (free, ready) in enumerate(((silu_done, up_ready), (h_done, gate_ready))):
                            need(e, free, n - 1)
                            for k in range(KD):
                                for j, (wi, xi) in enumerate(HI_LO):
                                    a = side * inter + m * P
                                    mm = e.matmul(UG[:, m % 2, side, :], up[wi][:, x, k, a:a + P],
                                                  core.XT[xi][:, k, ch * S:(ch + 1) * S],
                                                  start=(k == 0 and j == 0), stop=(k == KD - 1 and j == 2))
                            mm.then_inc(ready, 1)

                def downs(g, c):
                    x, ch = (c // 4) % 2, c % 4
                    e.wait_ge(h_lo, NM * g + NM)
                    for tt in range(TPB):
                        need(e, added, TPB * g + (tt - 3))
                        for m in range(NM):
                            for j, (hi, wi) in enumerate(HI_LO):
                                mm = e.matmul(Y[:, tt, 0:D], H[hi][:, c % 2, m, tt * P:(tt + 1) * P],
                                              down[wi][:, x, m, :], start=(m == 0 and j == 0),
                                              stop=(m == NM - 1 and j == 2))
                        mm.then_inc(y_ready, 1)

                def emit(g, c):
                    if not isinstance(g, int) or g + 1 < NG:
                        ups(g + 1, (c + 1) % 8)
                    downs(g, c)
                ups(0, 0)
                run(e, emit)

            @block.scalar
            def _(e):
                def hidden(g, c):
                    for m in range(NM + 1):
                        n = NM * g + m
                        if m < NM:
                            e.wait_ge(up_ready, n + 1)
                            need(e, h_done, n - 1)
                            e.activation(SU[:, m % 2], UG[:, m % 2, 0, :], ACT.Silu).then_inc(silu_done, 1)
                        if m >= 1:
                            e.wait_ge(h_done, n)
                            if m == 1:
                                need(e, y_ready, TPB * (g - 1))
                            e.activation(H[0][:, c % 2, m - 1], HF[:, (m - 1) % 2], ACT.Copy).then_inc(h_hi, 1)

                def emit(g, c):
                    if not isinstance(g, int) or g + 1 < NG:
                        hidden(g + 1, (c + 1) % 8)
                hidden(0, 0)
                run(e, emit)

            @block.vector
            def _(e):
                def hidden(g, c):
                    for m in range(NM + 1):
                        n = NM * g + m
                        if m < NM:
                            e.wait_ge(gate_ready, n + 1)
                            e.wait_ge(silu_done, n + 1)
                            need(e, h_lo, n - 1)
                            need(e, h_hi, n - 1)
                            e.tensor_tensor(HF[:, m % 2], UG[:, m % 2, 1, :], SU[:, m % 2], ALU.mult).then_inc(h_done, 1)
                        if m >= 1:
                            e.wait_ge(h_hi, n)
                            e.tensor_tensor(H[1][:, c % 2, m - 1], HF[:, (m - 1) % 2],
                                            H[0][:, c % 2, m - 1].bitcast(F32), ALU.subtract).then_inc(h_lo, 1)
                        if m < NM and not (isinstance(g, int) and g == 0):
                            lookup(g - 1, (c - 1) % 8, m)

                def lookup(g, c, m):
                    j = 8 * (c % 2) + 2 * m
                    base = N_LUT * g + 4 * m
                    piece = LK[:, bass.ds(((g - c) // 2 + c // 2) * LK_W, LK_W)]
                    if j == 0:
                        need(e, lk, base)
                        e.tensor_copy(idx[:], piece.bitcast(I32)).then_inc(lk, 1)
                        e.wait_ge(lk, base + 1)
                        e.tensor_scalar(total[:], idx[:], 0.0, lut[:, 0:1], ALU.is_equal, ALU.mult).then_inc(lk, 1)
                        e.tensor_scalar(term[:, 1], idx[:], 1.0, lut[:, 1:2], ALU.is_equal, ALU.mult).then_inc(lk, 1)
                    else:
                        e.wait_ge(lk, base - 1)
                        e.tensor_scalar(term[:, 0], idx[:], float(j), lut[:, j:j + 1],
                                        ALU.is_equal, ALU.mult).then_inc(lk, 1)
                        e.wait_ge(lk, base)
                        e.tensor_scalar(term[:, 1], idx[:], float(j + 1), lut[:, j + 1:j + 2],
                                        ALU.is_equal, ALU.mult).then_inc(lk, 1)
                        e.wait_ge(lk, base + 1)
                        e.tensor_tensor(total[:], total[:], term[:, 0], ALU.add).then_inc(lk, 1)
                    e.wait_ge(lk, base + 3)
                    e.tensor_tensor(piece if j + 2 == N_LUT else total[:], total[:], term[:, 1],
                                    ALU.add).then_inc(lk, 1)

                def emit(g, c):
                    if not isinstance(g, int) or g + 1 < NG:
                        hidden(g + 1, (c + 1) % 8)
                    if isinstance(g, int) and g + 1 == NG:
                        for m in range(NM):
                            lookup(g, c, m)
                    ch = c % 4
                    x = (g - c) // 4 + c // 4
                    for tt in range(TPB):
                        t = ch * TPB + tt
                        e.wait_ge(y_ready, TPB * g + (tt + 1))
                        e.scalar_tensor_tensor(out=core.X[:, t], in0=Y[:, tt, 0:D],
                                               scalar=comb[:, bass.ds(x, 1), t:t + 1].rearrange("p a b -> p (a b)"),
                                               in1=core.X[:, t], op0=ALU.mult, op1=ALU.add).then_inc(added, 1)
                e.wait_ge(lk_in, 16 * (len(indices) + 1))
                hidden(0, 0)
                run(e, emit)
                e.wait_ge(added, NG * TPB)


def prepare_plain(core, tag, w, cols):
    with Phase(core, tag + "s") as ph:
        act_split, dve_split, w_lo, n = split_on(ph, w[0], w[1], cols)
        with core.nc.Block() as block:
            @block.scalar
            def _(e):
                act_split()

            @block.vector
            def _(e):
                dve_split()
                e.wait_ge(w_lo, n)


def head_mixing_phase(core, tag, O, next_raw, next_bias):
    nc = core.nc
    H, HD = 16, 16
    scratch = nc.dram_tensor("l3_mixed", [B, H, S, HD], F32).ap()
    with Phase(core, tag) as ph:
        n_w = KD * 3 * D
        w = [ph.sb("w_hi", [P, n_w], F32R), ph.sb("w_lo", [P, n_w], F32R)]
        wv = [x[:].rearrange("p (k c) -> p k c", k=KD) for x in w]
        act_split, dve_split, w_ready, n_split = split_on(ph, w[0], w[1], n_w)
        bias = ph.sb("bias", [1, 3 * D])
        ones = ph.sb("ones", [1, P])
        trig = ph.sb("trig", [P, 2, TPB, 8])
        QK = ph.sb("QK", [P, 2, 2 * D])
        VV = ph.sb("VV", [P, 4, D])
        RO = ph.sb("RO", [P, 3, 2 * D])
        tmp = ph.sb("tmp", [P, 2, D])
        PRD = ph.sb("PRD", [P, H * H * HD])
        AVP = ph.sb("AVP", [P, 2, H * HD * H])
        SC = ph.sb("SC", [P, 4, H, H])
        mx = ph.sb("mx", [P, 2, H])
        sm = ph.sb("sm", [P, 2, H])
        OO = ph.sb("OO", [P, 2, D])
        qk_ps = ph.ps("qk", [P, 2, 512])
        v_ps = ph.ps("v", [P, 2, 512])
        const_in = ph.sem("const_in")
        ones_set = ph.sem("ones_set")
        qk_ready = ph.sem("qk_ready")
        v_ready = ph.sem("v_ready")
        qk_done = ph.sem("qk_done")
        v_done = ph.sem("v_done")
        rope_a = ph.sem("rope_a")
        ro_done = ph.sem("ro_done")
        prd_done = ph.sem("prd_done")
        sc_done = ph.sem("sc_done")
        mx_done = ph.sem("mx_done")
        sub_done = ph.sem("sub_done")
        exp_done = ph.sem("exp_done")
        sm_done = ph.sem("sm_done")
        rc_done = ph.sem("rc_done")
        a_done = ph.sem("a_done")
        av_done = ph.sem("av_done")
        o_done = ph.sem("o_done")
        stored = [ph.sem(f"stored{i}") for i in range(2)]
        o_in = ph.sem("o_in")
        bias_done = ph.sem("bias_done")
        bias_n = core.n_bias
        with nc.Block() as block:
            @block.sync
            def _(e):
                e.dma_start(bias[:], core.arrays["l3_bqkv"]).then_inc(const_in, 16)
                e.dma_start(trig[:], core.arrays["trig"].rearrange("f (t p) c -> p f t c", p=P)).then_inc(const_in, 16)
                e.wait_ge(w_ready, n_split)
                core.load_raw(e, next_raw)
                for t in range(NT):
                    b, st = divmod(t, TPB)
                    e.wait_ge(o_done, t + 1)
                    e.dma_start(scratch[b, :, st * P:(st + 1) * P, :].rearrange("h s d -> s h d"),
                                OO[:, t % 2, :].rearrange("p (h d) -> p h d", h=H)).then_inc(stored[t % 2], 16)
                    if st == TPB - 1:
                        e.wait_ge(stored[0], 8 * (t + 1))
                        e.wait_ge(stored[1], 8 * (t + 1))
                        e.dma_start(O[:, b * TPB:(b + 1) * TPB, :],
                                    scratch[b].rearrange("h s d -> (h s d)").rearrange("(t p c) -> p t c", p=P, c=D)
                                    ).then_inc(o_in, 16)
                e.wait_ge(o_in, 16 * B)

            @block.tensor
            def _(e):
                e.wait_ge(w_ready, n_split)
                e.wait_ge(const_in, 32)
                e.wait_ge(ones_set, 1)
                for t in range(NT):
                    for ps, lo, hi, free, ready in ((qk_ps, 0, 2 * D, qk_done, qk_ready), (v_ps, 2 * D, 3 * D, v_done, v_ready)):
                        need(e, free, t - 1)
                        out = ps[:, t % 2, 0:hi - lo]
                        e.matmul(out, ones[:], bias[:, lo:hi], start=True, stop=False)
                        for k in range(KD):
                            for j, (xi, wi) in enumerate(HI_LO):
                                mm = e.matmul(out, core.XT[xi][:, k, t * P:(t + 1) * P], wv[wi][:, k, lo:hi],
                                              start=False, stop=(k == KD - 1 and j == 2))
                        mm.then_inc(ready, 1)

            @block.scalar
            def _(e):
                act_split()
                for i in range(NT + 1):
                    if i < NT:
                        e.wait_ge(qk_ready, i + 1)
                        need(e, ro_done, i - 1)
                        e.activation(QK[:, i % 2], qk_ps[:, i % 2, :], ACT.Copy).then_inc(qk_done, 1)
                        e.wait_ge(v_ready, i + 1)
                        need(e, av_done, i - 3)
                        e.activation(VV[:, i % 4], v_ps[:, i % 2, 0:D], ACT.Copy).then_inc(v_done, 1)
                    if i >= 1:
                        t = i - 1
                        e.wait_ge(sub_done, t + 1)
                        e.activation(SC[:, t % 4], SC[:, t % 4], ACT.Exp, scale=HD ** -0.5).then_inc(exp_done, 1)

            @block.gpsimd
            def _(e):
                e.wait_ge(const_in, 32)
                e.wait_ge(core.bias_loaded, bias_n)
                e.tensor_tensor(core.X[:], core.X[:], core.bias[:].unsqueeze(1).broadcast_to([P, NT, D]),
                                ALU.add).then_inc(bias_done, 1)
                n = 0
                for i in range(NT + 3):
                    if i < NT:
                        s, st = i % 2, i % TPB
                        e.wait_ge(qk_done, i + 1)
                        need(e, prd_done, i - 2)
                        x = QK[:, s].rearrange("p (g c r) -> p r g c", c=8, r=2)
                        r = RO[:, i % 3].rearrange("p (g c r) -> p r g c", c=8, r=2)
                        cos = trig[:, 0, st, :].unsqueeze(1).broadcast_to([P, 2 * H, 8])
                        sin = trig[:, 1, st, :].unsqueeze(1).broadcast_to([P, 2 * H, 8])
                        ta = tmp[:, 0].rearrange("p (g c) -> p g c", c=8)
                        tb = tmp[:, 1].rearrange("p (g c) -> p g c", c=8)
                        for half, (fa, fb, op) in enumerate(((cos, sin, ALU.subtract), (sin, cos, ALU.add))):
                            e.tensor_tensor(ta, x[:, 0], fa, ALU.mult).then_inc(rope_a, 1)
                            e.tensor_tensor(tb, x[:, 1], fb, ALU.mult).then_inc(rope_a, 1)
                            n += 2
                            e.wait_ge(rope_a, n)
                            mm = e.tensor_tensor(r[:, half], ta, tb, op)
                            if half == 0:
                                n += 1
                                mm.then_inc(rope_a, 1)
                                e.wait_ge(rope_a, n)
                            else:
                                mm.then_inc(ro_done, 1)
                        e.wait_ge(ro_done, i + 1)
                    t = i - 3
                    if 0 <= t < NT:
                        e.wait_ge(a_done, t + 1)
                        need(e, o_done, t - 1)
                        a = SC[:, t % 4].unsqueeze(2).broadcast_to([P, H, HD, H])
                        v = VV[:, t % 4].rearrange("p (t d) -> p d t", t=H).unsqueeze(1).broadcast_to([P, H, HD, H])
                        e.tensor_tensor(AVP[:, t % 2].rearrange("p (h d t) -> p h d t", h=H, d=HD), a, v,
                                        ALU.mult).then_inc(av_done, 1)
                e.wait_ge(bias_done, 1)

            @block.vector
            def _(e):
                e.memset(ones[:], 1.0).then_inc(ones_set, 1)
                dve_split()
                for i in range(NT + 4):
                    if i < NT:
                        s = i % 2
                        e.wait_ge(ro_done, i + 1)
                        need(e, sc_done, i)
                        qv = RO[:, i % 3, 0:D].rearrange("p (h d) -> p h d", h=H).unsqueeze(2).broadcast_to([P, H, H, HD])
                        kv = RO[:, i % 3, D:2 * D].rearrange("p (t d) -> p t d", t=H).unsqueeze(1).broadcast_to([P, H, H, HD])
                        e.tensor_tensor(PRD[:].rearrange("p (h t d) -> p h t d", h=H, t=H), qv, kv,
                                        ALU.mult).then_inc(prd_done, 1)
                        e.wait_ge(prd_done, i + 1)
                        need(e, av_done, i - 3)
                        e.tensor_reduce(SC[:, i % 4], PRD[:].rearrange("p (h t d) -> p h t d", h=H, t=H), AXX,
                                        ALU.add).then_inc(sc_done, 1)
                        e.wait_ge(sc_done, i + 1)
                        need(e, a_done, i - 1)
                        e.tensor_reduce(mx[:, s], SC[:, i % 4], AXX, ALU.max).then_inc(mx_done, 1)
                        e.wait_ge(mx_done, i + 1)
                        e.tensor_tensor(SC[:, i % 4], SC[:, i % 4], mx[:, s].unsqueeze(2).broadcast_to([P, H, H]),
                                        ALU.subtract).then_inc(sub_done, 1)
                    t = i - 4
                    if 0 <= t < NT:
                        e.wait_ge(av_done, t + 1)
                        need(e, stored[t % 2], 16 * (t // 2))
                        e.tensor_reduce(OO[:, t % 2].rearrange("p (h d) -> p h d", h=H),
                                        AVP[:, t % 2].rearrange("p (h d t) -> p h d t", h=H, d=HD), AXX,
                                        ALU.add).then_inc(o_done, 1)
                    t = i - 1
                    if 0 <= t < NT:
                        s = t % 2
                        e.wait_ge(exp_done, t + 1)
                        need(e, rc_done, t - 1)
                        e.tensor_reduce(sm[:, s], SC[:, t % 4], AXX, ALU.add).then_inc(sm_done, 1)
                        e.wait_ge(sm_done, t + 1)
                        e.reciprocal(mx[:, s], sm[:, s]).then_inc(rc_done, 1)
                        e.wait_ge(rc_done, t + 1)
                        e.tensor_tensor(SC[:, t % 4], SC[:, t % 4], mx[:, s].unsqueeze(2).broadcast_to([P, H, H]),
                                        ALU.mult).then_inc(a_done, 1)


def mixture_weights_phase(core, tag, comb, C, next_raw):
    nc = core.nc
    K = 8
    with Phase(core, tag) as ph:
        amp = ph.sb("amp", [P, K, 2])
        sq = ph.sb("sq", [P, K, 2])
        p8 = ph.sb("p8", [P, K])
        s1 = ph.sb("s1", [P, 2])
        mix = ph.sb("mix", [P, K])
        CT = ph.sb("CT", [P, 2, P])
        TP = ph.ps("TP", [P, 2, 512])
        CP = ph.ps("CP", [P, NT, K])
        amp_in = ph.sem("amp_in")
        dv = ph.sem("dv")
        tp_ready = ph.sem("tp_ready")
        ct_done = ph.sem("ct_done")
        c_ready = ph.sem("c_ready")
        c_done = ph.sem("c_done")
        with nc.Block() as block:
            @block.sync
            def _(e):
                e.dma_start(amp[:], core.arrays["l3_amp"]).then_inc(amp_in, 16)
                core.load_raw(e, next_raw)

            @block.tensor
            def _(e):
                for i in range(NT + 1):
                    if i < NT:
                        need(e, ct_done, i - 1)
                        e.transpose(TP[:, i % 2, 0:P], comb[:, i, :], core.ident[:]).then_inc(tp_ready, 1)
                    if i >= 1:
                        if i == 1:
                            e.wait_ge(dv, 6)
                        e.wait_ge(ct_done, i)
                        e.matmul(CP[:, i - 1, :], CT[:, (i - 1) % 2, :], mix[:], start=True, stop=True).then_inc(c_ready, 1)

            @block.scalar
            def _(e):
                for i in range(NT):
                    e.wait_ge(tp_ready, i + 1)
                    need(e, c_ready, i - 1)
                    e.activation(CT[:, i % 2, :], TP[:, i % 2, 0:P], ACT.Copy).then_inc(ct_done, 1)

            @block.vector
            def _(e):
                e.wait_ge(amp_in, 16)
                e.tensor_tensor(sq[:], amp[:], amp[:], ALU.mult).then_inc(dv, 1)
                e.wait_ge(dv, 1)
                e.tensor_reduce(p8[:], sq[:], AXX, ALU.add).then_inc(dv, 1)
                e.wait_ge(dv, 2)
                e.tensor_reduce(s1[:, 0:1], p8[:], AXX, ALU.add).then_inc(dv, 1)
                e.wait_ge(dv, 3)
                e.tensor_scalar(s1[:, 1:2], s1[:, 0:1], 1e-8, None, ALU.add).then_inc(dv, 1)
                e.wait_ge(dv, 4)
                e.reciprocal(s1[:, 0:1], s1[:, 1:2]).then_inc(dv, 1)
                e.wait_ge(dv, 5)
                e.tensor_scalar(mix[:], p8[:], s1[:, 0:1], None, ALU.mult).then_inc(dv, 1)
                e.wait_ge(c_ready, NT)
                e.tensor_copy(C[:], CP[:]).then_inc(c_done, 1)
                e.wait_ge(c_done, 1)


def mixture_phase(core, tag, C):
    nc = core.nc
    K, I = 8, 128
    NG, NSH = KD * K * I, KD * 2 * I
    cols = 2 * NG + 2 * NSH + 3 * D
    with Phase(core, tag) as ph:
        w = [ph.sb("w_hi", [P, cols], F32R), ph.sb("w_lo", [P, cols], F32R)]
        main = [x[:, 0:2 * NG].rearrange("p (s k c) -> p s k c", s=2, k=KD) for x in w]
        shared = [x[:, 2 * NG:2 * NG + 2 * NSH].rearrange("p (s k c) -> p s k c", s=2, k=KD) for x in w]
        down = [x[:, 2 * NG + 2 * NSH:cols].rearrange("p (m c) -> p m c", m=3) for x in w]
        act_split, dve_split, w_ready, n_split = split_on(ph, w[0], w[1], cols)
        SG = ph.sb("SG", [P, 2, 512])
        T = ph.sb("T", [P, 2, 512])
        MS = ph.sb("MS", [P, 2, 3, P])
        HT = [ph.sb("HT_hi", [P, 2, 3 * P], F32R), ph.sb("HT_lo", [P, 2, 3 * P], F32R)]
        UG = ph.ps("UG", [P, 2, 2, 512])
        TP = ph.ps("TP", [P, 2, 512])
        tail = Tail(ph, last=True)
        ug_ready = ph.sem("ug_ready")
        silu_done = ph.sem("silu_done")
        t_done = ph.sem("t_done")
        acc_done = ph.sem("acc_done")
        tp_ready = ph.sem("tp_ready")
        ht_hi = ph.sem("ht_hi")
        ht_lo = ph.sem("ht_lo")
        with nc.Block() as block:
            @block.sync
            def _(e):
                for t in range(NT):
                    tail.sync_store(t)
                e.wait_ge(tail.stored, 16 * NT)

            @block.gpsimd
            def _(e):
                tail.pool_setup()
                for t in range(NT):
                    tail.pool_rstd(t)

            def pe_t(e, t):
                e.wait_ge(acc_done, K * (t + 1))
                e.wait_ge(t_done, 3 * (t + 1))
                need(e, ht_lo, t - 1)
                for m in range(3):
                    mm = e.transpose(TP[:, t % 2, m * P:(m + 1) * P], MS[:, t % 2, m, :], core.ident[:])
                mm.then_inc(tp_ready, 1)

            def pe_down(e, t):
                e.wait_ge(ht_lo, t + 1)
                need(e, tail.summed, t - 1)
                for m in range(3):
                    for j, (hi, wi) in enumerate(HI_LO):
                        mm = e.matmul(tail.y[:, t % 2, 0:D], HT[hi][:, t % 2, m * P:(m + 1) * P], down[wi][:, m, :],
                                      start=(m == 0 and j == 0), stop=(m == 2 and j == 2))
                mm.then_inc(tail.y_ready, 1)

            @block.tensor
            def _(e):
                e.wait_ge(w_ready, n_split)
                for i in range(NT + 2):
                    if i < NT:
                        for it in range(3):
                            n = 3 * i + it
                            need(e, t_done, n - 1)
                            for side in range(2):
                                N = 512 if it < 2 else 256
                                for k in range(KD):
                                    for j, (xi, wi) in enumerate(HI_LO):
                                        rhs = main[wi][:, side, k, it * 512:(it + 1) * 512] if it < 2 else \
                                            shared[wi][:, side, k, :]
                                        mm = e.matmul(UG[:, n % 2, side, 0:N], core.XT[xi][:, k, i * P:(i + 1) * P], rhs,
                                                      start=(k == 0 and j == 0), stop=(k == KD - 1 and j == 2))
                            mm.then_inc(ug_ready, 1)
                            if it == 0 and 0 <= i - 1 < NT:
                                pe_t(e, i - 1)
                            if it == 1 and 0 <= i - 1 < NT:
                                pe_down(e, i - 1)
                    elif i - 1 < NT:
                        pe_t(e, i - 1)
                        pe_down(e, i - 1)

            @block.scalar
            def _(e):
                act_split()
                for i in range(NT + 1):
                    for it in range(3):
                        if i < NT:
                            n = 3 * i + it
                            N = 512 if it < 2 else 256
                            e.wait_ge(ug_ready, n + 1)
                            need(e, t_done, n - 1)
                            e.activation(SG[:, n % 2, 0:N], UG[:, n % 2, 0, 0:N], ACT.Silu).then_inc(silu_done, 1)
                        if it == 0 and i >= 1:
                            t = i - 1
                            e.wait_ge(tp_ready, t + 1)
                            need(e, tail.y_ready, t - 1)
                            e.activation(HT[0][:, t % 2], TP[:, t % 2, 0:3 * P], ACT.Copy).then_inc(ht_hi, 1)

            @block.vector
            def _(e):
                dve_split()

                def item(i, it):
                    n = 3 * i + it
                    e.wait_ge(silu_done, n + 1)
                    if it == 2:
                        need(e, tp_ready, i - 1)
                        e.tensor_tensor(MS[:, i % 2, 1:3, :].rearrange("p a b -> p (a b)"), SG[:, n % 2, 0:256],
                                        UG[:, n % 2, 1, 0:256], ALU.mult).then_inc(t_done, 1)
                        return
                    need(e, acc_done, K * i + 4 * it - 4)
                    e.tensor_tensor(T[:, it, :], SG[:, n % 2, :], UG[:, n % 2, 1, :], ALU.mult).then_inc(t_done, 1)
                    e.wait_ge(t_done, n + 1)
                    for kk in range(4):
                        k = 4 * it + kk
                        src, c = T[:, it, kk * I:(kk + 1) * I], C[:, i, k:k + 1]
                        if k == 0:
                            need(e, tp_ready, i - 1)
                            e.tensor_scalar(MS[:, i % 2, 0, :], src, c, None, ALU.mult).then_inc(acc_done, 1)
                        else:
                            e.wait_ge(acc_done, K * i + k)
                            e.scalar_tensor_tensor(out=MS[:, i % 2, 0, :], in0=src, scalar=c, in1=MS[:, i % 2, 0, :],
                                                   op0=ALU.mult, op1=ALU.add).then_inc(acc_done, 1)

                for i in range(NT + 2):
                    if i < NT:
                        item(i, 0)
                    if 0 <= i - 1 < NT:
                        t = i - 1
                        e.wait_ge(ht_hi, t + 1)
                        e.tensor_tensor(HT[1][:, t % 2], TP[:, t % 2, 0:3 * P], HT[0][:, t % 2].bitcast(F32),
                                        ALU.subtract).then_inc(ht_lo, 1)
                    if i < NT:
                        item(i, 1)
                        item(i, 2)
                    if 0 <= i - 1 < NT:
                        tail.dve_stats(i - 1)
                    if 0 <= i - 2 < NT:
                        tail.dve_norm(i - 2)
                e.wait_ge(tail.normed, NT)


def program(nc, arrays, out, upto=99):
    with ExitStack() as ctx:
        core = Core(nc, ctx, arrays, out)
        arrays["l2_weights"] = nc.dram_tensor("l2_weights", [P, 4288], F32).ap()
        start_phase(core, [("l0_qkv", 1152)], "l0_bp")
        with Phase(core, "l0") as big:
            q = [big.sb("q_hi", [P, 8, S], F32R), big.sb("q_lo", [P, 8, S], F32R)]
            k = [big.sb("k_hi", [P, 8, S], F32R), big.sb("k_lo", [P, 8, S], F32R)]
            V = big.sb("V", [P, 8, TPB, 32])
            projection_phase(core, "l0p", q, k, V, 64, 576, 32 ** -0.5, [("l0_wp", 512)],
                             v_out=lambda part, b, kt: None if part else V[:, 2 * b:2 * b + 2, kt, :])
            O = core.XTF = big.sb("O", [P, 8, TPB, P])
            attention_phase(core, "l0a", q, k, V, O, 4, 8,
                            lambda u, r: O[:, bass.ds((u - r) // 4, 1), :, 32 * r:32 * r + 32].rearrange(
                                "p i t (a c) -> p (i t) a c", a=4), True, [])
            output_phase(core, "l0o", lambda t, kk: O[:, 2 * (t // TPB) + kk, t % TPB, :], [("l0_up", 2048), ("l0_gate", 2048), ("l0_down", 2048)])
        if upto == 0:
            return dump_phase(core)
        feed_forward_phase(core, "l0f", 1024, prepare_ternary, [("l1_qkv", 1536)], "l1_bo")
        if upto == 1:
            return dump_phase(core)
        with Phase(core, "l1") as big:
            q = [big.sb("q_hi", [P, 8, S], F32R), big.sb("q_lo", [P, 8, S], F32R)]
            k = [big.sb("k_hi", [P, 8, S], F32R), big.sb("k_lo", [P, 8, S], F32R)]
            v = [big.sb("v_hi", [P, NT, D], F32R), big.sb("v_lo", [P, NT, D], F32R)]
            O = big.sb("O", [P, NT, D])
            bqk, bv = load_biases(core, big, "l1_bqk", "l1_bv")
            projection_phase(core, "l1p", q, k, v, D, 768, 1.0, [("l1_wo", 512)], qk_bias=bqk, v_bias=bv,
                             v_out=lambda part, b, kt: v[part][:, b * TPB + kt, :])
            wide_attention_phase(core, "l1a", q, k, v, O, 1.0 / 16, [])
            output_phase(core, "l1o", lambda t, kk: O[:, t, kk * P:(kk + 1) * P], [("l1_router", 16)])
        if upto == 2:
            return dump_phase(core)
        with Phase(core, "l1m") as big:
            comb = big.sb("comb", [P, 8, NT])
            routing_phase(core, "l1r", comb[:].rearrange("p e t -> p t e"), 8, 2)
            experts_phase(core, "l1e", comb, 8, 512, [("l1_base_gu", 2048), ("l1_base_dn", 1024)],
                          "l2_lut", [("l2_gate", 1376), ("l2_up", 1376), ("l2_down", 1536)], "l2_weights")
        feed_forward_phase(core, "l1f", 512, prepare_plain, [("l2_qkv", 1536)], "l2_bo")
        if upto == 3:
            return dump_phase(core)
        with Phase(core, "l2") as big:
            O = big.sb("O", [P, B, TPB, D])
            with Phase(core, "l2x") as inner:
                q = [inner.sb("q_hi", [P, 8, S], F32R), inner.sb("q_lo", [P, 8, S], F32R)]
                k = [inner.sb("k_hi", [P, 8, S], F32R), inner.sb("k_lo", [P, 8, S], F32R)]
                V = inner.sb("V", [P, 8, TPB, P])
                projection_phase(core, "l2p", q, k, V, D, 768, 16 ** -0.5, [("l2_wo", 512)],
                                 v_out=lambda part, b, kt: None if part else V[:, 2 * b:2 * b + 2, kt, :])

                def o_at(u, r, g):
                    nh = 2 * ((u - r) // 4) + r // 2
                    return O[:, (2 * r + g) % 4, :, bass.ds(nh * 16, 16)]
                attention_phase(core, "l2a", q, k, V, O, 2, 16, o_at, True, [])
            output_phase(core, "l2o", lambda t, kk: O[:, t // TPB, t % TPB, kk * P:(kk + 1) * P],
                         [("l2_weights", 4288)])
        if upto == 4:
            return dump_phase(core)
        feed_forward_phase(core, "l2f", 688, prepare_plain, [("l3_qkv", 1536)], "l3_bo")
        if upto == 5:
            return dump_phase(core)
        with Phase(core, "l3") as big:
            O = big.sb("O", [P, NT, D])
            head_mixing_phase(core, "l3a", O, [("l3_wo", 512)], None)
            output_phase(core, "l3o", lambda t, kk: O[:, t, kk * P:(kk + 1) * P], [("l3_router", 256)])
        if upto == 6:
            return dump_phase(core)
        with Phase(core, "l3m") as big:
            C = big.sb("C", [P, NT, 8])
            with Phase(core, "l3c") as inner:
                comb = inner.sb("comb", [P, NT, P])
                routing_phase(core, "l3r", comb[:], 128, 4, 1e-8, "l3_escale")
                mixture_weights_phase(core, "l3w", comb, C,
                                      [("l3_gate", 2048), ("l3_up", 2048), ("l3_sgate", 512), ("l3_sup", 512),
                                       ("l3_down", 256), ("l3_sdown", 512)])
            mixture_phase(core, "l3f", C)


def load_biases(core, big, qk_name, v_name):
    bqk = big.sb("bqk", [P, 4])
    bv = big.sb("bv", [P, D])
    done = big.sem("bias_in")
    with core.nc.Block() as block:
        @block.sync
        def _(e):
            e.dma_start(bqk[:], core.arrays[qk_name]).then_inc(done, 16)
            e.dma_start(bv[:], core.arrays[v_name].partition_broadcast(P)).then_inc(done, 16)
            e.wait_ge(done, 32)
    return bqk, bv


def dump_phase(core):
    nc = core.nc
    with Phase(core, "dump") as ph:
        done = ph.sem("done")
        with nc.Block() as block:
            @block.sync
            def _(e):
                e.dma_start(core.out.rearrange("(t p) d -> p t d", p=P), core.X[:]).then_inc(done, 16)
                e.wait_ge(done, 16)


def by_partition(w):
    return np.ascontiguousarray(np.moveaxis(w.reshape((w.shape[0] // P, P) + w.shape[1:]), 0, 1)).reshape(P, -1)


def head_mask(G):
    m = np.zeros((P, G), np.float32)
    for row in range(96):
        m[row, (row % 32) // (32 // G)] = 1
    for g in range(G):
        m[96 + g, g] = 1
    return m


def layout(inp):
    a = {}
    x = np.asarray(inp["L0_attn_x"]).reshape(NT * P, D)
    a["x"], a["xT"] = x, np.ascontiguousarray(x.T)
    wkv = np.asarray(inp["L0_attn_Wkv"])
    wk = np.repeat(wkv[:, :64].reshape(D, 8, 1, 8), 4, axis=2).reshape(D, D)
    a["l0_qkv"] = by_partition(np.concatenate([np.asarray(inp["L0_attn_Wq"]), wk, wkv[:, 64:]], axis=1))
    a["l0_wp"] = by_partition(np.asarray(inp["L0_attn_Wp"]))
    a["l0_up"] = by_partition(np.ascontiguousarray(np.asarray(inp["L0_ffn_W_up"]).T))
    a["l0_gate"] = by_partition(np.ascontiguousarray(np.asarray(inp["L0_ffn_W_gate"]).T))
    a["l0_down"] = by_partition(np.ascontiguousarray(np.asarray(inp["L0_ffn_W_down"]).T))
    a["l1_qkv"] = by_partition(np.ascontiguousarray(np.asarray(inp["L1_attn_w_qkv"]).T))
    b = np.asarray(inp["L1_attn_b_qkv"])
    a["l1_bqk"], a["l1_bv"] = by_partition(b[:512]), b[512:]
    a["l1_wo"] = by_partition(np.ascontiguousarray(np.asarray(inp["L1_attn_w_out"]).T))
    a["l1_bo"] = np.asarray(inp["L1_attn_b_out"])
    a["l1_router"] = by_partition(np.asarray(inp["L1_ffn_gate_w"]))
    gu = np.asarray(inp["L1_ffn_expert_gate_up"])
    a["l1e_gu"] = np.stack([by_partition(g) for g in gu])
    a["l1e_dn"] = np.stack([by_partition(g) for g in np.asarray(inp["L1_ffn_expert_down"])])
    g = np.asarray(inp["L1_ffn_base_gate_up"])
    a["l1_base_gu"] = np.concatenate([by_partition(g[:, :512]), by_partition(g[:, 512:])], axis=1)
    a["l1_base_dn"] = by_partition(np.asarray(inp["L1_ffn_base_down"]))
    w = np.asarray(inp["L2_attn_Wqkv"]).T.reshape(D, 16, 3, 16)
    a["l2_qkv"] = by_partition(np.concatenate([w[:, :, i].reshape(D, D) for i in range(3)], axis=1))
    a["l2_wo"] = by_partition(np.ascontiguousarray(np.asarray(inp["L2_attn_Wproj"]).T))
    a["l2_bo"] = np.asarray(inp["L2_attn_bproj"])
    a["l2_gate"] = by_partition(np.ascontiguousarray(np.asarray(inp["L2_ffn_gate_idx"]).T))
    a["l2_up"] = by_partition(np.ascontiguousarray(np.asarray(inp["L2_ffn_up_idx"]).T))
    dn = np.zeros((768, D), np.asarray(inp["L2_ffn_down_idx"]).dtype)
    dn[:688] = np.asarray(inp["L2_ffn_down_idx"]).T
    a["l2_down"] = by_partition(dn)
    a["l2_lut"] = np.asarray(inp["L2_ffn_lut"])
    f = {k: np.asarray(v) for k, v in inp.items() if k.startswith("L3")}
    a["l3_qkv"] = by_partition(np.concatenate([f[f"L3_attn_W{c}"].T for c in "qkv"], axis=1))
    a["l3_bqkv"] = np.concatenate([f[f"L3_attn_b{c}"] for c in "qkv"]).reshape(1, -1)
    a["l3_wo"] = by_partition(np.ascontiguousarray(f["L3_attn_Wo"].T))
    a["l3_bo"] = f["L3_attn_bo"]
    a["l3_router"] = by_partition(f["L3_ffn_w_router"])
    a["l3_escale"] = f["L3_ffn_expert_scale"]
    a["l3_amp"] = f["L3_ffn_amplitudes"]
    for name, key in (("gate", "w_gate"), ("up", "w_up"), ("sgate", "shared_w_gate"), ("sup", "shared_w_up"),
                      ("down", "w_down"), ("sdown", "shared_w_down")):
        a[f"l3_{name}"] = by_partition(f[f"L3_ffn_{key}"])
    freqs = np.outer(np.arange(S, dtype=np.float32),
                     (1.0 / 10000.0 ** (np.arange(0, 16, 2, dtype=np.float32) / 16)).astype(np.float32))
    a["trig"] = np.stack([np.cos(freqs), np.sin(freqs)]).astype(np.float32)
    a["l0_bp"] = np.asarray(inp["L0_attn_bp"])
    a["mask4"], a["mask2"] = head_mask(4), head_mask(2)
    return a


def kernel(**inputs):
    import concourse.bacc as _bacc
    from concourse.bass_utils import run_bass_kernel_spmd as _run

    nc = _bacc.Bacc("TRN2", target_bir_lowering=False, num_devices=1)
    arrays = {name: np.ascontiguousarray(a) for name, a in layout(inputs).items()}
    handles = {name: nc.dram_tensor(name, a.shape, mybir.dt.from_np(a.dtype), kind="ExternalInput").ap()
               for name, a in arrays.items()}
    out = nc.dram_tensor("out", (NT * P, D), F32, kind="ExternalOutput").ap()
    program(nc, handles, out)
    r = _run(nc, [arrays], core_ids=[0])
    return r.results[0]["out"].reshape(B, S, D)
```

```python
from contextlib import ExitStack

import numpy as np
import concourse.bass as bass
import concourse.mybir as mybir

F32 = mybir.dt.float32
F32R = mybir.dt.float32r
I32 = mybir.dt.int32
ACT = mybir.ActivationFunctionType
ALU = mybir.AluOpType
AXX = mybir.AxisListType.X

P = 128
B, S, D = 4, 512, 256
KD = D // P
NT = B * S // P
TPB = S // P
EPS_LN = 1e-5
RAW_COLS = 6144
HI_LO = ((0, 0), (0, 1), (1, 0))


STEP, LAST = "M0 S0 S1 M1 M2 P M3", "S0 M0 S1 MT M1 P M2 M3 TO"
STEP2, LAST2 = "M0 S0 S1 M1 M2 P M3", "S0 M0 S1 MT M1 P M2 M3 TO"


def need(eng, sem, value):
    if isinstance(value, int) and value <= 0:
        return
    eng.wait_ge(sem, value)


class Core:

    def __init__(self, nc, ctx, arrays, out):
        self.nc, self.arrays, self.out = nc, arrays, out
        sb = lambda name, shape, dt=F32: ctx.enter_context(nc.sbuf_tensor(name, shape, dt))
        sem = lambda name: ctx.enter_context(nc.semaphore(name))
        self.X = sb("X", [P, NT, D])
        self.xt_base = nc.sbuf_base
        sb("XT_slab", [P, 2 * KD * NT * P])
        self.XT = [self.lend(f"XT_{n}", [P, KD, NT * P], F32R, i * 4 * KD * NT * P) for i, n in enumerate(("hi", "lo"))]
        self.ident = sb("ident", [P, P])
        self.raw = sb("raw", [P, RAW_COLS])
        self.bias = sb("bias", [P, D])
        self.raw_loaded = sem("raw_loaded")
        self.bias_loaded = sem("bias_loaded")
        self.n_raw = self.n_bias = 0
        self.limbo = []

    def lend(self, name, shape, dt, at):
        assert at + 4 * int(np.prod(shape[1:])) <= 8 * KD * NT * P
        return self.nc.alloc_sbuf_tensor_at(name, shape, dt, offset=self.xt_base + at)

    def load_raw(self, eng, pieces):
        at = 0
        for name, cols in pieces:
            src = self.arrays[name]
            dst = self.raw[0:src.shape[0], at:at + cols]
            if src.dtype != F32:
                dst = dst.bitcast(src.dtype)
            eng.dma_start(dst, src).then_inc(self.raw_loaded, 16)
            self.n_raw += 16
            at += cols

    def load_bias(self, eng, name):
        eng.dma_start(self.bias[:], self.arrays[name].partition_broadcast(P)).then_inc(self.bias_loaded, 16)
        self.n_bias += 16


class Phase:

    def __init__(self, core, tag):
        self.core, self.tag, self.ctx, self.sems = core, tag, ExitStack(), []

    def __enter__(self):
        self.ctx.__enter__()
        return self

    def __exit__(self, *a):
        nc, limbo = self.core.nc, self.core.limbo
        if self.sems:
            for s in self.sems:
                nc.sync.sem_clear(s)
            limbo.append(self.sems)
            if len(limbo) > 2:
                for s in limbo.pop(0):
                    nc.release_semaphore(s)
        return self.ctx.__exit__(*a)

    def sb(self, name, shape, dt=F32):
        return self.ctx.enter_context(self.core.nc.sbuf_tensor(f"{self.tag}_{name}_s", shape, dt))

    def ps(self, name, shape, dt=F32):
        return self.ctx.enter_context(self.core.nc.psum_tensor(f"{self.tag}_{name}", shape, dt))

    def sem(self, name):
        self.sems.append(self.core.nc.alloc_semaphore(f"{self.tag}_{name}"))
        return self.sems[-1]


def split_on(phase, hi, lo, cols, chunk=1024):
    core = phase.core
    w_hi = phase.sem("w_hi")
    w_lo = phase.sem("w_lo")
    starts = list(range(0, cols, chunk))
    loaded = core.n_raw

    def act():
        e = core.nc.scalar
        e.wait_ge(core.raw_loaded, loaded)
        for a in starts:
            b = min(cols, a + chunk)
            e.activation(hi[:, a:b], core.raw[:, a:b], ACT.Copy).then_inc(w_hi, 1)

    def dve():
        e = core.nc.vector
        e.wait_ge(core.raw_loaded, loaded)
        for n, a in enumerate(starts):
            b = min(cols, a + chunk)
            e.wait_ge(w_hi, n + 1)
            e.tensor_tensor(lo[:, a:b], core.raw[:, a:b], hi[:, a:b].bitcast(F32), ALU.subtract).then_inc(w_lo, 1)

    return act, dve, w_lo, len(starts)


class Tail:

    def __init__(self, phase, last=False, y_scale=None):
        core = self.core = phase.core
        self.y_scale = y_scale
        self.last = last
        self.y = phase.ps("y", [P, 2, 512])
        self.tx = phase.ps("tx", [P, 512]) if not last else None
        self.R = phase.sb("R", [P, 2, D])
        self.xo = phase.sb("xo", [P, 2, D]) if last else None
        self.st = phase.sb("st", [P, 2, 8])
        self.mv = phase.sb("mv", [P, 2, 2])
        self.ve = phase.sb("ve", [P, 2, 1])
        self.half = phase.sb("half", [P, 1])
        self.rstd = phase.sb("rstd", [P, 2, 1])
        s = phase.sem
        self.y_ready = s("y_ready")
        self.summed = s("summed")
        self.stats = s("stats")
        self.moments = s("moments")
        self.var_eps = s("var_eps")
        self.pow_c = s("pow_c")
        self.rstd_ready = s("rstd_ready")
        self.normed = s("normed")
        self.tx_ready = s("tx_ready")
        self.xt_hi = s("xt_hi")
        self.xt_lo = s("xt_lo")
        self.stored = s("stored")

    def pool_setup(self):
        self.core.nc.gpsimd.memset(self.half[:], -0.5).then_inc(self.pow_c, 1)
        self.core.nc.gpsimd.wait_ge(self.pow_c, 1)

    def dve_stats(self, t):
        e, s = self.core.nc.vector, t % 2
        e.wait_ge(self.y_ready, t + 1)
        need(e, self.normed, t - 1)
        if self.y_scale is None:
            e.tensor_tensor(self.R[:, s], self.y[:, s, 0:D], self.core.X[:, t], ALU.add).then_inc(self.summed, 1)
        else:
            e.scalar_tensor_tensor(out=self.R[:, s], in0=self.y[:, s, 0:D], scalar=self.y_scale,
                                   in1=self.core.X[:, t], op0=ALU.mult, op1=ALU.add).then_inc(self.summed, 1)
        e.wait_ge(self.summed, t + 1)
        e.bn_stats(self.st[:, s, 0:6], self.R[:, s]).then_inc(self.stats, 1)
        e.wait_ge(self.stats, t + 1)
        e.bn_aggr(self.mv[:, s], self.st[:, s, 0:6]).then_inc(self.moments, 1)
        e.wait_ge(self.moments, t + 1)
        need(e, self.rstd_ready, t - 1)
        e.tensor_scalar(self.ve[:, s], self.mv[:, s, 1:2], EPS_LN, None, ALU.add).then_inc(self.var_eps, 1)

    def pool_rstd(self, t):
        e, s = self.core.nc.gpsimd, t % 2
        e.wait_ge(self.var_eps, t + 1)
        need(e, self.normed, t - 1)
        e.tensor_tensor(self.rstd[:, s], self.ve[:, s], self.half[:], ALU.pow).then_inc(self.rstd_ready, 1)

    def dve_norm(self, t):
        e, s = self.core.nc.vector, t % 2
        e.wait_ge(self.rstd_ready, t + 1)
        if self.last:
            need(e, self.stored, 16 * (t - 1))
            dst = self.xo[:, s]
        else:
            dst = self.core.X[:, t]
        e.tensor_scalar(dst, self.R[:, s], self.mv[:, s, 0:1], self.rstd[:, s, 0:1],
                        ALU.subtract, ALU.mult).then_inc(self.normed, 1)

    def pe_transpose(self, t):
        e = self.core.nc.tensor
        e.wait_ge(self.normed, t + 1)
        need(e, self.xt_lo, t)
        for k in range(KD):
            mm = e.transpose(self.tx[:, k * P:(k + 1) * P], self.core.X[:, t, k * P:(k + 1) * P], self.core.ident[:])
        mm.then_inc(self.tx_ready, 1)

    def act_xt(self, t):
        e = self.core.nc.scalar
        e.wait_ge(self.tx_ready, t + 1)
        src = self.tx[:, 0:D].rearrange("p (k n) -> p k n", k=KD)
        e.activation(self.core.XT[0][:, :, t * P:(t + 1) * P], src, ACT.Copy).then_inc(self.xt_hi, 1)

    def dve_xt(self, t):
        e = self.core.nc.vector
        e.wait_ge(self.xt_hi, t + 1)
        src = self.tx[:, 0:D].rearrange("p (k n) -> p k n", k=KD)
        e.tensor_tensor(self.core.XT[1][:, :, t * P:(t + 1) * P], src,
                        self.core.XT[0][:, :, t * P:(t + 1) * P].bitcast(F32), ALU.subtract).then_inc(self.xt_lo, 1)

    def sync_store(self, t):
        e = self.core.nc.sync
        e.wait_ge(self.normed, t + 1)
        if t:
            e.wait_ge(self.stored, 16 * t)
        e.dma_start(self.core.out[t * P:(t + 1) * P, :], self.xo[:, t % 2]).then_inc(self.stored, 16)


def start_phase(core, next_raw, next_bias):
    nc = core.nc
    with Phase(core, "start") as ph:
        xt = ph.sb("xt", [P, KD, NT * P])
        x_in = ph.sem("x_in")
        xt_in = ph.sem("xt_in")
        zeroed = ph.sem("zeroed")
        made = ph.sem("made")
        hi_done = ph.sem("hi_done")
        lo_done = ph.sem("lo_done")
        with nc.Block() as block:
            @block.sync
            def _(e):
                for k in range(KD):
                    e.dma_start(xt[:, k, :], core.arrays["xT"][k * P:(k + 1) * P, :]).then_inc(xt_in, 16)
                core.load_raw(e, next_raw)
                core.load_bias(e, next_bias)
                e.dma_start(core.X[:], core.arrays["x"].rearrange("(t p) d -> p t d", p=P)).then_inc(x_in, 16)
                e.wait_ge(x_in, 16)

            @block.gpsimd
            def _(e):
                e.memset(core.ident[:], 0.0).then_inc(zeroed, 1)
                e.wait_ge(zeroed, 1)
                e.affine_select(out=core.ident[:], in_=core.ident[:], compare_op=ALU.not_equal, fill=1.0,
                                base=0, pattern=[[-1, P]], channel_multiplier=1).then_inc(made, 1)
                e.wait_ge(made, 1)

            @block.scalar
            def _(e):
                e.wait_ge(xt_in, 16 * KD)
                for k in range(KD):
                    e.activation(core.XT[0][:, k, :], xt[:, k, :], ACT.Copy).then_inc(hi_done, 1)

            @block.vector
            def _(e):
                for k in range(KD):
                    e.wait_ge(hi_done, k + 1)
                    e.tensor_tensor(core.XT[1][:, k, :], xt[:, k, :], core.XT[0][:, k, :].bitcast(F32),
                                    ALU.subtract).then_inc(lo_done, 1)
                e.wait_ge(lo_done, KD)


def projection_phase(core, tag, q, k, v, v_cols, cols, q_scale, next_raw, qk_bias=None, v_bias=None, v_out=None):
    nc = core.nc
    with Phase(core, tag) as ph:
        n_w = KD * cols
        w = [ph.sb("w_hi", [P, n_w], F32R), ph.sb("w_lo", [P, n_w], F32R)]
        wv = [x[:].rearrange("p (k c) -> p k c", k=KD) for x in w]
        act_split, dve_split, w_ready, n_split = split_on(ph, w[0], w[1], n_w)
        fm = ph.ps("fm", [P, 4, 512])
        tm = ph.ps("tm", [P, 2, 512])
        fm_ready = ph.sem("fm_ready")
        fm_hi = ph.sem("fm_hi")
        fm_lo = ph.sem("fm_lo")
        tm_ready = ph.sem("tm_ready")
        tm_hi = ph.sem("tm_hi")
        tm_lo = ph.sem("tm_lo")
        tiles = [(dst, half, m) for m, (dst, half) in enumerate((x, h) for x in (q, k) for h in range(2))]
        two = v_out(1, 0, 0) is not None
        if two:
            vtmp = ph.sb("vtmp", [P, 2, v_cols])
            v_sum = ph.sem("v_sum")
        raw_n, bias_n = core.n_raw, core.n_bias
        with nc.Block() as block:
            @block.sync
            def _(e):
                e.wait_ge(w_ready, n_split)
                core.load_raw(e, next_raw)

            @block.scalar
            def _(e):
                act_split()
                n = 0
                for b in range(B):
                    for dst, half, m in tiles:
                        e.wait_ge(fm_ready, n + 1)
                        scale = q_scale if dst is q else 1.0
                        if qk_bias is None:
                            e.activation(dst[0][:, 2 * b + half, :], fm[:, n % 4, :], ACT.Copy,
                                         scale=scale).then_inc(fm_hi, 1)
                        else:
                            e.activation(dst[0][:, 2 * b + half, :], fm[:, n % 4, :], ACT.Identity,
                                         bias=qk_bias[:, m:m + 1]).then_inc(fm_hi, 1)
                        n += 1

            @block.vector
            def _(e):
                dve_split()
                n = nv = 0
                for b in range(B):
                    for dst, half, m in tiles:
                        e.wait_ge(fm_hi, n + 1)
                        e.scalar_tensor_tensor(
                            out=dst[1][:, 2 * b + half, :], in0=fm[:, n % 4, :],
                            scalar=(q_scale if dst is q else 1.0) if qk_bias is None else qk_bias[:, m:m + 1],
                            in1=dst[0][:, 2 * b + half, :].bitcast(F32),
                            op0=ALU.mult if qk_bias is None else ALU.add, op1=ALU.subtract).then_inc(fm_lo, 1)
                        n += 1
                    for kt in range(TPB):
                        e.wait_ge(tm_ready, nv + 1)
                        src = tm[:, nv % 2, 0:v_cols]
                        d0, d1 = v_out(0, b, kt), v_out(1, b, kt)
                        if len(d0.shape) == 3:
                            src = src.rearrange("p (a c) -> p a c", a=d0.shape[1])
                        if v_bias is not None:
                            vb = v_bias[:] if len(d0.shape) == 2 else v_bias[:].rearrange("p (a c) -> p a c", a=d0.shape[1])
                        if not two:
                            e.tensor_copy(d0, src).then_inc(tm_hi, 1)
                        else:
                            vf = vtmp[:, nv % 2]
                            need(e, tm_lo, nv - 1)
                            e.tensor_tensor(vf, src, vb, ALU.add).then_inc(v_sum, 1)
                            e.wait_ge(v_sum, nv + 1)
                            e.tensor_copy(d0, vf).then_inc(tm_hi, 1)
                            e.wait_ge(tm_hi, nv + 1)
                            e.tensor_tensor(d1, vf, d0.bitcast(F32), ALU.subtract).then_inc(tm_lo, 1)
                        nv += 1

            @block.tensor
            def _(e):
                e.wait_ge(w_ready, n_split)
                n = nv = 0
                for b in range(B):
                    for dst, half, m in tiles:
                        need(e, fm_lo, n - 3)
                        for kk in range(KD):
                            for j, (wi, xi) in enumerate(HI_LO):
                                mm = e.matmul(fm[:, n % 4, :], wv[wi][:, kk, m * P:(m + 1) * P],
                                              core.XT[xi][:, kk, b * S:(b + 1) * S],
                                              start=(kk == 0 and j == 0), stop=(kk == KD - 1 and j == 2))
                        mm.then_inc(fm_ready, 1)
                        n += 1
                    for kt in range(TPB):
                        need(e, v_sum if two else tm_hi, nv - 1)
                        t = b * TPB + kt
                        for kk in range(KD):
                            for j, (xi, wi) in enumerate(HI_LO):
                                mm = e.matmul(tm[:, nv % 2, 0:v_cols], core.XT[xi][:, kk, t * P:(t + 1) * P],
                                              wv[wi][:, kk, 2 * D:2 * D + v_cols],
                                              start=(kk == 0 and j == 0), stop=(kk == KD - 1 and j == 2))
                        mm.then_inc(tm_ready, 1)
                        nv += 1


QUADS = 4


def attention_phase(core, tag, q, k, V, O, heads, hd, o_at, residual_bias, next_raw):
    nc = core.nc
    G = heads
    NS = G
    REP = 4 // G
    NU = B * 2 * QUADS
    RING = 3
    UNROLL = 4 if G == 4 else 12
    ring_order = [("max", 1, i) for i in range(4, 4 * G)] + [
        ("mt", 1, 0) if x == "MT" else ("to", -1, 0) if x == "TO" else ("max", 2, int(x[1]))
        for x in (LAST if G == 4 else LAST2).split() if x[0] == "M" or x == "TO"]
    filled = [(kind, u + du, i) for u in range(-2, NU + 1) for kind, du, i in ring_order if 0 <= u + du < NU]
    number = {item: n for n, item in enumerate(filled)}
    assert UNROLL * len(ring_order) % RING == 0
    with Phase(core, tag) as ph:
        PT = core.lend(f"{tag}_PT", [P, 2, 4, S], F32, 0)
        QA = core.lend(f"{tag}_QA", [P, 4, S], F32R, 16384)
        KR = core.lend(f"{tag}_KR", [P, 2, S], F32, 24576)
        OT = core.lend(f"{tag}_OT", [P, 2, S], F32, 28672)
        KA = ph.sb("KA", [P, 4, G, S], F32R)
        VA = ph.sb("VA", [P, 4, TPB, 32 if G == 4 else 64])
        mask = ph.sb("mask", [P, G])
        MX = ph.sb("MX", [P, 2, 4, G])
        RI = ph.sb("RI", [P, 4, 4])
        SM = ph.ps("SM", [P, RING, S])
        ST = ph.ps("ST", [P, 4, S])
        PV = ph.ps("PV", [P, S])
        q_in = [ph.sem(f"q_in{i}") for i in range(4)]
        k_in = [ph.sem(f"k_in{i}") for i in range(2)]
        mask_in = ph.sem("mask_in")
        zeroed = ph.sem("zeroed")
        ka_ready = ph.sem("ka_ready")
        va_ready = ph.sem("va_ready")
        sm_ready = ph.sem("sm_ready")
        mx_done = ph.sem("mx_done")
        mt_ready = ph.sem("mt_ready")
        m_done = ph.sem("m_done")
        st_ready = ph.sem("st_ready")
        exp_done = ph.sem("exp_done")
        pv_step = ph.sem("pv_step")
        ot_done = ph.sem("ot_done")
        to_ready = ph.sem("to_ready")
        ri_done = ph.sem("ri_done")
        os_done = ph.sem("os_done")
        o_done = ph.sem("o_done")
        bias_done = ph.sem("bias_done")
        seen_free = ph.sem("seen_free")
        zero_v = ph.sem("zero_v")
        bias_n = core.n_bias
        ROWS_M = 96

        def slot(kind, cu, i=0):
            return number[kind, cu, i] % RING

        def claim(e, kind, u, cu, i=0):
            n = number[kind, cu, i]
            if n >= RING:
                was, unit, j = filled[n - RING]
                unit = unit - cu + u
                sem, count = {"max": (mx_done, unit * (4 * G) + (j + 1)), "mt": (m_done, unit + 1),
                              "to": (o_done, unit + 1)}[was]
                e.wait_ge(sem, count)
            return SM[:, n % RING, :]

        def chunk(u, c):
            return [divmod(4 * c + i, G) for i in range(4)]

        def live(u):
            return not isinstance(u, int) or 0 <= u < NU

        def pe_max(e, u, cu, c, items=range(4)):
            if not live(u):
                return
            r = cu % 4
            if c == 0 and items[0] == 0:
                e.wait_ge(q_in[r], 12 * (u - r) + 48)
                e.wait_ge(ka_ready, G * u + G)
            for i in items:
                qt, g = chunk(u, c)[i]
                e.matmul(claim(e, "max", u, cu, 4 * c + i), QA[0:ROWS_M, r, qt * P:(qt + 1) * P], KA[0:ROWS_M, r, g, :],
                         start=True, stop=True).then_inc(sm_ready, 1)

        def dve_max(e, u, cu, c, items=range(4)):
            if not live(u):
                return
            r = cu % 4
            if c == 0 and items[0] == 0:
                need(e, mt_ready, u - 1)
            for i in items:
                qt, g = chunk(u, c)[i]
                e.wait_ge(sm_ready, u * (4 * G) + (4 * c + i + 1))
                e.tensor_reduce(MX[:, r % 2, qt, g:g + 1], SM[:, slot("max", cu, 4 * c + i), :], AXX, ALU.max).then_inc(mx_done, 1)

        def pe_mt(e, u, cu):
            if not live(u):
                return
            r = cu % 4
            e.wait_ge(mx_done, u * (4 * G) + 4 * G)
            maxima = claim(e, "mt", u, cu)
            for qt in range(4):
                mm = e.transpose(maxima[0:G, qt * P:(qt + 1) * P], MX[:, r % 2, qt, :], core.ident[:])
            mm.then_inc(mt_ready, 1)

        def dve_mrow(e, u, cu):
            if not live(u):
                return
            r = cu % 4
            e.wait_ge(mt_ready, u + 1)
            e.tensor_scalar(QA[ROWS_M:ROWS_M + G, r, :], SM[0:G, slot("mt", cu), :], -1.0, None, ALU.mult).then_inc(m_done, 1)

        def pe_scores(e, u, r, s, half):
            if not live(u):
                return
            if s == 0 and half == 0:
                e.wait_ge(m_done, u + 1)
            h = u * (2 * NS) + (2 * s + half)
            need(e, exp_done, h - 1)
            for a in (2 * half, 2 * half + 1):
                g, kt = a // REP, s * REP + a % REP
                mm = e.matmul(ST[:, a, :], KA[:, r, g, kt * P:(kt + 1) * P], QA[:, r, :], start=True, stop=True)
            mm.then_inc(st_ready, 1)

        def act_exp(e, u, s):
            if not live(u):
                return
            step = u * NS + s
            for half in range(2):
                e.wait_ge(st_ready, u * (2 * NS) + (2 * s + half + 1))
                if half == 0:
                    need(e, pv_step, step - 1)
                e.activation(PT[:, s % 2, 2 * half:2 * half + 2, :], ST[:, 2 * half:2 * half + 2, :],
                             ACT.Exp).then_inc(exp_done, 1)

        def pe_pv(e, u, r, s):
            if not live(u):
                return
            step = u * NS + s
            e.wait_ge(exp_done, u * (2 * NS) + (2 * s + 2))
            if s == 0:
                e.wait_ge(va_ready, u + 1)
                need(e, ot_done, u)
            for a in range(4):
                g, kt = a // REP, s * REP + a % REP
                va = VA[:, r, kt, 0:32] if G == 4 else VA[:, r, kt, 32 * g:32 * g + 32]
                mm = e.matmul(PV[32 * a:32 * a + 32, :], va, PT[:, s % 2, a, :], start=(s == 0), stop=(s == NS - 1),
                              tile_position=(0, 32 * a))
            mm.then_inc(pv_step, 1)

        def act_ot(e, u, r):
            if not live(u):
                return
            e.wait_ge(pv_step, u * NS + NS)
            need(e, to_ready, u - 1)
            e.activation(OT[:, r % 2, :], PV[:], ACT.Copy).then_inc(ot_done, 1)

        def pe_to(e, u, cu):
            if not live(u):
                return
            r = cu % 4
            e.wait_ge(ot_done, u + 1)
            out = claim(e, "to", u, cu)
            for qt in range(4):
                mm = e.transpose(out[:, qt * P:(qt + 1) * P], OT[:, r % 2, qt * P:(qt + 1) * P], core.ident[:])
            mm.then_inc(to_ready, 1)

        def dve_out(e, u, cu):
            if not live(u):
                return
            r = cu % 4
            out = SM[:, slot("to", cu), :]
            e.wait_ge(to_ready, u + 1)
            T = out.rearrange("p (t a c) -> p t a c", t=4, a=4)
            if G == 4:
                need(e, o_done, u)
                e.reciprocal(RI[:], T[:, :, :, hd]).then_inc(ri_done, 1)
                e.wait_ge(ri_done, u + 1)
                e.tensor_tensor(o_at(u, r), T[:, :, :, 0:hd],
                                RI[:].unsqueeze(3).broadcast_to([P, 4, 4, hd]), ALU.mult).then_inc(o_done, 1)
            else:
                T2 = out.rearrange("p (t g h c) -> p t g h c", t=4, g=2, h=2)
                need(e, o_done, u)
                e.tensor_copy(OP[:], T2[:, :, :, 0, 0:hd + 1]).then_inc(op_done, 1)
                e.wait_ge(op_done, 2 * u + 1)
                e.tensor_tensor(OP[:], OP[:], T2[:, :, :, 1, 0:hd + 1], ALU.add).then_inc(op_done, 1)
                e.wait_ge(op_done, 2 * u + 2)
                e.reciprocal(RI[:, :, 0:G], OP[:, :, :, hd]).then_inc(ri_done, 1)
                e.wait_ge(ri_done, u + 1)
                for g in range(2):
                    mm = e.tensor_tensor(o_at(u, r, g), OP[:, :, g, 0:hd],
                                         RI[:, :, g:g + 1].broadcast_to([P, 4, hd]), ALU.mult)
                mm.then_inc(o_done, 1)
        if G == 2:
            OP = ph.sb("OP", [P, 4, 2, hd + 1])
            op_done = ph.sem("op_done")

        def run(e, emit):
            rounds = (NU - 8) // UNROLL
            for u in range(-2, 3):
                emit(u, u)
            with e.Fori(0, rounds) as i:
                for c in range(3, 3 + UNROLL):
                    emit(UNROLL * i + c, c)
            for u in range(3 + UNROLL * rounds, NU + 1):
                emit(u, u)

        with nc.Block() as block:
            @block.sync
            def _(e):
                e.dma_start(mask[:], core.arrays[f"mask{G}"]).then_inc(mask_in, 16)
                core.load_raw(e, next_raw)

                def emit(i, r):
                    u = 4 * i + r
                    need(e, st_ready, (u - 3) * (2 * NS))
                    e.sem_inc(seen_free, 1)
                    for n, part in enumerate((0, 0, 1)):
                        e.dma_start(QA[32 * n:32 * n + 32, r, :].bitcast(F32),
                                    q[part][32 * r:32 * r + 32, bass.ds(i, 1), :].bitcast(F32)
                                    ).then_inc(q_in[r], 16)
                    need(e, ka_ready, (u - 1) * G)
                    e.sem_inc(seen_free, 1)
                    for n, part in enumerate((0, 1, 0)):
                        e.dma_start(KR[32 * n:32 * n + 32, r % 2, :],
                                    k[part][32 * r:32 * r + 32, bass.ds(i, 1), :].bitcast(F32)).then_inc(k_in[r % 2], 16)
                e.wait_ge(zeroed, 1)
                for r in range(4):
                    emit(0, r)
                with e.Fori(1, 8) as i:
                    for r in range(4):
                        emit(i, r)

            @block.gpsimd
            def _(e):
                e.wait_ge(mask_in, 16)
                e.wait_ge(zeroed, 1)
                if residual_bias:
                    e.wait_ge(core.bias_loaded, bias_n)
                    e.tensor_tensor(core.X[:], core.X[:], core.bias[:].unsqueeze(1).broadcast_to([P, NT, D]),
                                    ALU.add).then_inc(bias_done, 1)

                def emit(i, r):
                    u = 4 * i + r
                    e.wait_ge(k_in[r % 2], 96 * i + 48 * (r // 2 + 1))
                    need(e, st_ready, (u - 3) * (2 * NS))
                    for g in range(G):
                        e.tensor_tensor(KA[:, r, g, :], KR[:, r % 2, :], mask[:, g:g + 1].broadcast_to([P, S]),
                                        ALU.mult).then_inc(ka_ready, 1)
                    need(e, pv_step, (u - 3) * NS)
                    if G == 4:
                        e.tensor_copy(VA[:, r, :, 0:hd], V[:, bass.ds(i, 1), :, r * hd:(r + 1) * hd]
                                      ).then_inc(va_ready, 1)
                    else:
                        for g in range(G):
                            mm = e.tensor_copy(VA[:, r, :, 32 * g:32 * g + hd],
                                               V[:, bass.ds(i, 1), :, (2 * r + g) * hd:(2 * r + g + 1) * hd])
                        mm.then_inc(va_ready, 1)
                for r in range(4):
                    emit(0, r)
                with e.Fori(1, 8) as i:
                    for r in range(4):
                        emit(i, r)
                if residual_bias:
                    e.wait_ge(bias_done, 1)

            @block.scalar
            def _(e):
                def emit(u, c):
                    for s in range(NS):
                        act_exp(e, u, s)
                        if s == 0:
                            act_ot(e, u - 1, (c - 1) % 4)
                run(e, emit)

            @block.vector
            def _(e):
                e.memset(QA[ROWS_M:P, :, :].bitcast(F32), 0.0).then_inc(zero_v, 1)
                e.memset(KR[ROWS_M:P, :, :], 1.0).then_inc(zero_v, 1)
                e.memset(VA[:], 0.0).then_inc(zero_v, 1)
                e.wait_ge(zero_v, 3)
                ones = VA[:, :, :, hd:hd + 1] if G == 4 else \
                    VA[:].rearrange("p r t (g c) -> p r t g c", g=2)[:, :, :, :, hd:hd + 1]
                e.memset(ones, 1.0).then_inc(zeroed, 1)

                def emit(u, c):
                    for kind, du, n in ring_order:
                        if kind == "max":
                            dve_max(e, u + du, c + du, n // 4, [n % 4])
                        elif kind == "mt":
                            dve_mrow(e, u + du, c + du)
                        else:
                            dve_out(e, u + du, c + du)
                run(e, emit)
                e.wait_ge(o_done, NU)

            @block.tensor
            def _(e):
                e.wait_ge(zeroed, 1)

                def emit(u, c):
                    r, rp = c % 4, (c - 1) % 4
                    for s in range(NS - 1):
                        for x in (STEP if G == 4 else STEP2).split():
                            if x[0] == "M":
                                pe_max(e, u + 1, c + 1, s + 1, [int(x[1])])
                            elif x[0] == "S":
                                pe_scores(e, u, r, s, int(x[1]))
                            elif s == 0:
                                pe_pv(e, u - 1, rp, NS - 1)
                            else:
                                pe_pv(e, u, r, s - 1)
                    for x in (LAST if G == 4 else LAST2).split():
                        if x == "MT":
                            pe_mt(e, u + 1, c + 1)
                        elif x == "TO":
                            pe_to(e, u - 1, c - 1)
                        elif x == "P":
                            pe_pv(e, u, r, NS - 2)
                        elif x[0] == "M":
                            pe_max(e, u + 2, c + 2, 0, [int(x[1])])
                        else:
                            pe_scores(e, u, r, NS - 1, int(x[1]))
                run(e, emit)


def output_phase(core, tag, o_tile, next_raw, next_bias=None):
    nc = core.nc
    with Phase(core, tag) as ph:
        w = [ph.sb("w_hi", [P, KD * D], F32R), ph.sb("w_lo", [P, KD * D], F32R)]
        wv = [x[:].rearrange("p (k c) -> p k c", k=KD) for x in w]
        act_split, dve_split, w_ready, n_split = split_on(ph, w[0], w[1], KD * D)
        OT = [ph.sb("OT_hi", [P, 2, D], F32R), ph.sb("OT_lo", [P, 2, D], F32R)]
        TP = ph.ps("TP", [P, 2, 512])
        tail = Tail(ph)
        tp_ready = ph.sem("tp_ready")
        ot_hi = ph.sem("ot_hi")
        ot_lo = ph.sem("ot_lo")
        with nc.Block() as block:
            @block.sync
            def _(e):
                e.wait_ge(w_ready, n_split)
                core.load_raw(e, next_raw)
                if next_bias:
                    core.load_bias(e, next_bias)

            @block.gpsimd
            def _(e):
                tail.pool_setup()
                for t in range(NT):
                    tail.pool_rstd(t)

            @block.tensor
            def _(e):
                for i in range(NT + 3):
                    if i < NT:
                        need(e, ot_lo, i - 1)
                        for k in range(KD):
                            mm = e.transpose(TP[:, i % 2, k * P:(k + 1) * P], o_tile(i, k), core.ident[:])
                        mm.then_inc(tp_ready, 1)
                    t = i - 1
                    if 0 <= t < NT:
                        if t == 0:
                            e.wait_ge(w_ready, n_split)
                        e.wait_ge(ot_lo, t + 1)
                        need(e, tail.summed, t - 1)
                        for k in range(KD):
                            for j, (oi, wi) in enumerate(HI_LO):
                                mm = e.matmul(tail.y[:, t % 2, 0:D], OT[oi][:, t % 2, k * P:(k + 1) * P],
                                              wv[wi][:, k, :], start=(k == 0 and j == 0),
                                              stop=(k == KD - 1 and j == 2))
                        mm.then_inc(tail.y_ready, 1)
                    if 0 <= i - 3 < NT:
                        tail.pe_transpose(i - 3)

            @block.scalar
            def _(e):
                act_split()
                for i in range(NT + 3):
                    if i < NT:
                        e.wait_ge(tp_ready, i + 1)
                        need(e, tail.y_ready, i - 1)
                        e.activation(OT[0][:, i % 2], TP[:, i % 2, 0:D], ACT.Copy).then_inc(ot_hi, 1)
                    if 0 <= i - 3 < NT:
                        tail.act_xt(i - 3)

            @block.vector
            def _(e):
                dve_split()
                for i in range(NT + 3):
                    if i < NT:
                        e.wait_ge(ot_hi, i + 1)
                        e.tensor_tensor(OT[1][:, i % 2], TP[:, i % 2, 0:D], OT[0][:, i % 2].bitcast(F32),
                                        ALU.subtract).then_inc(ot_lo, 1)
                    if 0 <= i - 1 < NT:
                        tail.dve_stats(i - 1)
                    if 0 <= i - 2 < NT:
                        tail.dve_norm(i - 2)
                    if 0 <= i - 3 < NT:
                        tail.dve_xt(i - 3)
                e.wait_ge(tail.xt_lo, NT)


def feed_forward_phase(core, tag, inter, next_raw, next_bias=None, ternary=False):
    nc = core.nc
    M = [min(P, inter - a) for a in range(0, inter, P)]
    NM = len(M)
    cols = 2 * KD * inter + NM * D
    with Phase(core, tag) as ph:
        w = [ph.sb("w_hi", [P, cols], F32R)] + ([] if ternary else [ph.sb("w_lo", [P, cols], F32R)])
        parts_wx = [(wi, xi) for wi, xi in HI_LO if wi < len(w)]
        parts_hw = [(hi, wi) for hi, wi in HI_LO if wi < len(w)]
        up = [x[:, 0:2 * KD * inter].rearrange("p (s k c) -> p s k c", s=2, k=KD) for x in w]
        down = [x[:, 2 * KD * inter:cols].rearrange("p (m c) -> p m c", m=NM) for x in w]
        if ternary:
            scale = ph.sb("scale", [P, 4])
            prepare_ternary(core, tag, w[0], scale)
        else:
            prepare_plain(core, tag, w, cols)
        H = [ph.sb("H_hi", [P, 2, NM, S], F32R), ph.sb("H_lo", [P, 2, NM, S], F32R)]
        SU = ph.sb("SU", [P, 2, S])
        HF = ph.sb("HF", [P, 2, S])
        UG = ph.ps("UG", [P, 2, 2, S])
        tail = Tail(ph, y_scale=scale[:, 3:4] if ternary else None)
        up_ready = ph.sem("up_ready")
        gate_ready = ph.sem("gate_ready")
        silu_done = ph.sem("silu_done")
        h_done = ph.sem("h_done")
        h_hi = ph.sem("h_hi")
        h_lo = ph.sem("h_lo")

        def tail_steps(c):
            return range(c * TPB, (c + 1) * TPB + (2 if c == B - 1 else 0))

        with nc.Block() as block:
            @block.sync
            def _(e):
                core.load_raw(e, next_raw)
                if next_bias:
                    core.load_bias(e, next_bias)

            @block.gpsimd
            def _(e):
                tail.pool_setup()
                for t in range(NT):
                    tail.pool_rstd(t)

            @block.tensor
            def _(e):
                def ups(c):
                    for m, rows in enumerate(M):
                        n = c * NM + m
                        for side, (free, ready) in enumerate(((silu_done, up_ready), (h_done, gate_ready))):
                            need(e, free, n - 1)
                            for k in range(KD):
                                for j, (wi, xi) in enumerate(parts_wx):
                                    mm = e.matmul(UG[0:rows, n % 2, side, :], up[wi][:, side, k, m * P:m * P + rows],
                                                  core.XT[xi][:, k, c * S:(c + 1) * S],
                                                  start=(k == 0 and j == 0),
                                                  stop=(k == KD - 1 and j == len(parts_wx) - 1))
                            mm.then_inc(ready, 1)

                def downs(c):
                    e.wait_ge(h_lo, (c + 1) * NM)
                    for t in tail_steps(c):
                        if t < NT:
                            need(e, tail.summed, t - 1)
                            a = (t % TPB) * P
                            for m, rows in enumerate(M):
                                for j, (hi, wi) in enumerate(parts_hw):
                                    mm = e.matmul(tail.y[:, t % 2, 0:D], H[hi][0:rows, c % 2, m, a:a + P],
                                                  down[wi][0:rows, m, :],
                                                  start=(m == 0 and j == 0),
                                                  stop=(m == NM - 1 and j == len(parts_hw) - 1))
                            mm.then_inc(tail.y_ready, 1)
                        if t >= 2:
                            tail.pe_transpose(t - 2)
                ups(0)
                for c in range(B):
                    if c + 1 < B:
                        ups(c + 1)
                    downs(c)

            @block.scalar
            def _(e):
                def hidden(c):
                    for m in range(NM + 1):
                        n = c * NM + m
                        if m < NM:
                            rows = M[m]
                            e.wait_ge(up_ready, n + 1)
                            need(e, h_done, n - 1)
                            e.activation(SU[0:rows, n % 2], UG[0:rows, n % 2, 0, :], ACT.Silu,
                                         scale=scale[0:rows, 0:1] if ternary else 1.0).then_inc(silu_done, 1)
                        if m >= 1:
                            rows = M[m - 1]
                            e.wait_ge(h_done, n)
                            if m == 1 and c >= 2:
                                e.wait_ge(tail.y_ready, (c - 1) * TPB)
                            e.activation(H[0][0:rows, c % 2, m - 1], HF[0:rows, (n - 1) % 2], ACT.Copy).then_inc(h_hi, 1)
                hidden(0)
                for c in range(B):
                    if c + 1 < B:
                        hidden(c + 1)
                    for t in tail_steps(c):
                        if t >= 2:
                            tail.act_xt(t - 2)

            @block.vector
            def _(e):
                def hidden(c):
                    for m in range(NM + 1):
                        n = c * NM + m
                        if m < NM:
                            rows = M[m]
                            e.wait_ge(gate_ready, n + 1)
                            e.wait_ge(silu_done, n + 1)
                            need(e, h_lo, n - 1)
                            need(e, h_hi, n - 1)
                            e.tensor_tensor(HF[0:rows, n % 2], UG[0:rows, n % 2, 1, :], SU[0:rows, n % 2],
                                            ALU.mult).then_inc(h_done, 1)
                        if m >= 1:
                            rows = M[m - 1]
                            e.wait_ge(h_hi, n)
                            e.wait_ge(h_done, n)
                            e.tensor_tensor(H[1][0:rows, c % 2, m - 1], HF[0:rows, (n - 1) % 2],
                                            H[0][0:rows, c % 2, m - 1].bitcast(F32), ALU.subtract).then_inc(h_lo, 1)
                hidden(0)
                for c in range(B):
                    if c + 1 < B:
                        hidden(c + 1)
                    for t in tail_steps(c):
                        if t < NT:
                            tail.dve_stats(t)
                        if 1 <= t and t - 1 < NT:
                            tail.dve_norm(t - 1)
                        if t >= 2:
                            tail.dve_xt(t - 2)
                e.wait_ge(tail.xt_lo, NT)


def prepare_ternary(core, tag, signs, scale):
    nc = core.nc
    n_loaded = core.n_raw
    parts = [(0, 2048), (2048, 4096), (4096, 6144)]
    CH = 1024
    with Phase(core, tag + "t") as ph:
        absum = ph.sb("absum", [P, 3])
        ones = ph.sb("ones", [P, P])
        half = ph.sb("half", [P, 2, 3])
        below = ph.sb("below", [P, 2, CH])
        junk = ph.sb("junk", [P, 2048])
        total = ph.ps("total", [P, 3])
        sem = {x: ph.sem(x) for x in ("ones_set", "abs_done", "total_ready", "scaled", "below_done", "signs_done")}
        pieces = [(m, a) for m, (lo, hi) in enumerate(parts) for a in range(lo, hi, CH)]
        with nc.Block() as block:
            @block.scalar
            def _(e):
                e.wait_ge(core.raw_loaded, n_loaded)
                for m, (a, b) in enumerate(parts):
                    need(e, sem["abs_done"], m)
                    e.activation(junk[:], core.raw[:, a:b], ACT.Abs, accum_out=absum[:, m:m + 1]
                                 ).then_inc(sem["abs_done"], 1)

            @block.tensor
            def _(e):
                e.wait_ge(sem["ones_set"], 1)
                e.wait_ge(sem["abs_done"], 3)
                e.matmul(total[:], ones[:], absum[:], start=True, stop=True).then_inc(sem["total_ready"], 1)

            @block.vector
            def _(e):
                e.memset(ones[:], 1.0).then_inc(sem["ones_set"], 1)
                e.wait_ge(sem["total_ready"], 1)
                e.tensor_scalar(scale[:, 0:3], total[:], 1.0 / (D * 1024), 1e-8, ALU.mult, ALU.add
                                ).then_inc(sem["scaled"], 1)
                e.wait_ge(sem["scaled"], 1)
                e.tensor_scalar(half[:, 0, :], scale[:, 0:3], 0.5, None, ALU.mult).then_inc(sem["scaled"], 1)
                e.tensor_scalar(half[:, 1, :], scale[:, 0:3], -0.5, None, ALU.mult).then_inc(sem["scaled"], 1)
                e.tensor_tensor(scale[:, 3:4], scale[:, 1:2], scale[:, 2:3], ALU.mult).then_inc(sem["scaled"], 1)
                e.wait_ge(sem["scaled"], 4)
                for n in range(len(pieces) + 1):
                    if n < len(pieces):
                        m, a = pieces[n]
                        need(e, sem["signs_done"], n - 1)
                        e.tensor_scalar(below[:, n % 2], core.raw[:, a:a + CH], half[:, 1, m:m + 1], None,
                                        ALU.is_lt).then_inc(sem["below_done"], 1)
                    if n >= 1:
                        m, a = pieces[n - 1]
                        e.wait_ge(sem["below_done"], n)
                        e.scalar_tensor_tensor(out=signs[:, a:a + CH], in0=core.raw[:, a:a + CH],
                                               scalar=half[:, 0, m:m + 1], in1=below[:, (n - 1) % 2],
                                               op0=ALU.is_gt, op1=ALU.subtract).then_inc(sem["signs_done"], 1)
                e.wait_ge(sem["signs_done"], len(pieces))


def wide_attention_phase(core, tag, q, k, v, O, scale, next_raw):
    nc = core.nc
    with Phase(core, tag) as ph:
        SP = ph.ps("scores", [P, 3, S])
        TP = ph.ps("TP", [P, 2, S])
        CP = ph.ps("context", [P, 2, S])
        PR = core.lend(f"{tag}_probs", [P, 3, S], F32, 0)
        PT = [core.lend(f"{tag}_PT_{n}", [P, 2, TPB, P], F32R, 6144 + 4096 * i) for i, n in enumerate(("hi", "lo"))]
        mx = ph.sb("mx", [P, 3, 1])
        nm = ph.sb("nm", [P, 3, 1])
        rs = ph.sb("rs", [P, 3, 1])
        ri = ph.sb("ri", [P, 3, 1])
        s_ready = ph.sem("s_ready")
        mx_done = ph.sem("mx_done")
        nm_done = ph.sem("nm_done")
        exp_done = ph.sem("exp_done")
        ri_done = ph.sem("ri_done")
        p_done = ph.sem("p_done")
        tp_ready = ph.sem("tp_ready")
        pt_hi = ph.sem("pt_hi")
        pt_lo = ph.sem("pt_lo")
        c_ready = ph.sem("c_ready")
        c_done = ph.sem("c_done")
        bias_done = ph.sem("bias_done")
        bias_n = core.n_bias
        with nc.Block() as block:
            @block.sync
            def _(e):
                core.load_raw(e, next_raw)

            @block.gpsimd
            def _(e):
                e.wait_ge(core.bias_loaded, bias_n)
                e.tensor_tensor(core.X[:], core.X[:], core.bias[:].unsqueeze(1).broadcast_to([P, NT, D]),
                                ALU.add).then_inc(bias_done, 1)
                e.wait_ge(bias_done, 1)

            @block.tensor
            def _(e):
                for i in range(NT + 3):
                    if i < NT:
                        b, qt = divmod(i, TPB)
                        need(e, exp_done, i - 2)
                        for h in range(KD):
                            for j, (qi, ki) in enumerate(HI_LO):
                                mm = e.matmul(SP[:, i % 3, :], q[qi][:, 2 * b + h, qt * P:(qt + 1) * P],
                                              k[ki][:, 2 * b + h, :], start=(h == 0 and j == 0),
                                              stop=(h == KD - 1 and j == 2))
                        mm.then_inc(s_ready, 1)
                    t = i - 2
                    if 0 <= t < NT:
                        e.wait_ge(p_done, t + 1)
                        need(e, pt_lo, t - 1)
                        for kt in range(TPB):
                            mm = e.transpose(TP[:, t % 2, kt * P:(kt + 1) * P], PR[:, t % 3, kt * P:(kt + 1) * P],
                                             core.ident[:])
                        mm.then_inc(tp_ready, 1)
                    t = i - 3
                    if 0 <= t < NT:
                        b = t // TPB
                        e.wait_ge(pt_lo, t + 1)
                        need(e, c_done, t - 1)
                        for kt in range(TPB):
                            for j, (pi, vi) in enumerate(HI_LO):
                                mm = e.matmul(CP[:, t % 2, 0:D], PT[pi][:, t % 2, kt, :], v[vi][:, b * TPB + kt, :],
                                              start=(kt == 0 and j == 0), stop=(kt == TPB - 1 and j == 2))
                        mm.then_inc(c_ready, 1)

            @block.scalar
            def _(e):
                for i in range(NT + 3):
                    if i < NT:
                        e.wait_ge(nm_done, i + 1)
                        need(e, tp_ready, i - 2)
                        e.activation(PR[:, i % 3, :], SP[:, i % 3, :], ACT.Exp, bias=nm[:, i % 3], scale=scale,
                                     accum_out=rs[:, i % 3]).then_inc(exp_done, 1)
                    t = i - 2
                    if 0 <= t < NT:
                        e.wait_ge(tp_ready, t + 1)
                        need(e, c_ready, t - 1)
                        e.activation(PT[0][:, t % 2], TP[:, t % 2, :].rearrange("p (t n) -> p t n", t=TPB),
                                     ACT.Copy).then_inc(pt_hi, 1)
                    t = i - 3
                    if 0 <= t < NT:
                        e.wait_ge(c_ready, t + 1)
                        e.activation(O[:, t, :], CP[:, t % 2, 0:D], ACT.Copy).then_inc(c_done, 1)

            @block.vector
            def _(e):
                for i in range(NT + 3):
                    if i < NT:
                        e.wait_ge(s_ready, i + 1)
                        need(e, nm_done, i - 2)
                        e.tensor_reduce(mx[:, i % 3], SP[:, i % 3, :], AXX, ALU.max).then_inc(mx_done, 1)
                        e.wait_ge(mx_done, i + 1)
                        need(e, exp_done, i - 2)
                        e.tensor_scalar(nm[:, i % 3], mx[:, i % 3], -scale, None, ALU.mult).then_inc(nm_done, 1)
                    t = i - 1
                    if 0 <= t < NT:
                        e.wait_ge(exp_done, t + 1)
                        need(e, p_done, t - 2)
                        e.reciprocal(ri[:, t % 3], rs[:, t % 3]).then_inc(ri_done, 1)
                        e.wait_ge(ri_done, t + 1)
                        e.tensor_scalar(PR[:, t % 3, :], PR[:, t % 3, :], ri[:, t % 3], None,
                                        ALU.mult).then_inc(p_done, 1)
                    t = i - 2
                    if 0 <= t < NT:
                        e.wait_ge(pt_hi, t + 1)
                        e.tensor_tensor(PT[1][:, t % 2], TP[:, t % 2, :].rearrange("p (t n) -> p t n", t=TPB),
                                        PT[0][:, t % 2].bitcast(F32), ALU.subtract).then_inc(pt_lo, 1)
                e.wait_ge(pt_lo, NT)


def routing_phase(core, tag, comb, n_exp, n_top, eps=0.0, e_scale=None, next_raw=()):
    nc = core.nc
    n_s = 8 - n_top
    W = n_exp + n_s
    with Phase(core, tag) as ph:
        n_w = KD * n_exp
        w = [ph.sb("w_hi", [P, n_w], F32R), ph.sb("w_lo", [P, n_w], F32R)]
        wv = [x[:].rearrange("p (k c) -> p k c", k=KD) for x in w]
        act_split, dve_split, w_ready, n_split = split_on(ph, w[0], w[1], n_w)
        LG = ph.ps("logits", [P, NT, n_exp])
        mx = ph.sb("mx", [P, NT])
        ex = ph.sb("ex", [P, NT, n_exp])
        sm = ph.sb("sm", [P, NT])
        probs = ph.sb("probs", [P, NT, W])
        top8 = ph.sb("top8", [P, NT, 8])
        vals = ph.sb("vals", [P, NT, 8])
        rest = ph.sb("rest", [P, NT, W])
        ws = ph.sb("ws", [P, NT])
        lg_ready = ph.sem("lg_ready")
        ex_in = ph.sem("ex_in")
        ex_done = ph.sem("ex_done")
        dv = ph.sem("dv")
        es_in = ph.sem("es_in")
        if e_scale:
            es = ph.sb("es", [P, n_exp])
        with nc.Block() as block:
            @block.sync
            def _(e):
                if e_scale:
                    e.dma_start(es[:], core.arrays[e_scale].partition_broadcast(P)).then_inc(es_in, 16)
                if next_raw:
                    e.wait_ge(w_ready, n_split)
                    core.load_raw(e, next_raw)

            @block.tensor
            def _(e):
                e.wait_ge(w_ready, n_split)
                for t in range(NT):
                    for k in range(KD):
                        for j, (xi, wi) in enumerate(HI_LO):
                            mm = e.matmul(LG[:, t, :], core.XT[xi][:, k, t * P:(t + 1) * P], wv[wi][:, k, :],
                                          start=(k == 0 and j == 0), stop=(k == KD - 1 and j == 2))
                mm.then_inc(lg_ready, 1)

            @block.scalar
            def _(e):
                act_split()
                e.wait_ge(ex_in, 1)
                e.activation(ex[:], ex[:], ACT.Exp).then_inc(ex_done, 1)

            @block.vector
            def _(e):
                dve_split()
                for j in range(n_s):
                    e.memset(probs[:, :, n_exp + j:n_exp + j + 1], -1.0 - j).then_inc(dv, 1)
                    e.memset(vals[:, :, n_top + j:n_top + j + 1], -1.0 - j).then_inc(dv, 1)
                c = 2 * n_s
                e.wait_ge(lg_ready, 1)
                e.tensor_reduce(mx[:], LG[:], AXX, ALU.max).then_inc(dv, 1)
                c += 1
                e.wait_ge(dv, c)
                e.tensor_tensor(ex[:], LG[:], mx[:].unsqueeze(2).broadcast_to([P, NT, n_exp]),
                                ALU.subtract).then_inc(ex_in, 1)
                e.wait_ge(ex_done, 1)
                e.tensor_reduce(sm[:], ex[:], AXX, ALU.add).then_inc(dv, 1)
                c += 1
                e.wait_ge(dv, c)
                e.reciprocal(ws[:], sm[:]).then_inc(dv, 1)
                c += 1
                e.wait_ge(dv, c)
                e.tensor_tensor(probs[:, :, 0:n_exp], ex[:], ws[:].unsqueeze(2).broadcast_to([P, NT, n_exp]),
                                ALU.mult).then_inc(dv, 1)
                c += 1
                e.wait_ge(dv, c)
                for t in range(NT):
                    e.max(top8[:, t, :], probs[:, t, 0:n_exp]).then_inc(dv, 1)
                c += NT
                e.wait_ge(dv, c)
                e.tensor_copy(vals[:, :, 0:n_top], top8[:, :, 0:n_top]).then_inc(dv, 1)
                e.tensor_reduce(sm[:], top8[:, :, 0:n_top], AXX, ALU.add).then_inc(dv, 1)
                c += 2
                e.wait_ge(dv, c)
                for t in range(NT):
                    e.match_replace(out=rest[:, t, :], in_to_replace=vals[:, t, :], in_values=probs[:, t, :],
                                    imm_value=0.0).then_inc(dv, 1)
                if eps:
                    e.tensor_scalar(sm[:], sm[:], eps, None, ALU.add).then_inc(dv, 1)
                    c += 1
                    e.wait_ge(dv, c + NT)
                e.reciprocal(ws[:], sm[:]).then_inc(dv, 1)
                c += NT + 1
                e.wait_ge(dv, c)
                e.tensor_tensor(ex[:], probs[:, :, 0:n_exp], rest[:, :, 0:n_exp], ALU.subtract).then_inc(dv, 1)
                c += 1
                e.wait_ge(dv, c)
                if e_scale:
                    e.tensor_tensor(ex[:], ex[:], ws[:].unsqueeze(2).broadcast_to([P, NT, n_exp]),
                                    ALU.mult).then_inc(dv, 1)
                    c += 1
                    e.wait_ge(dv, c)
                    e.wait_ge(es_in, 16)
                    e.tensor_tensor(comb, ex[:], es[:].unsqueeze(1).broadcast_to([P, NT, n_exp]),
                                    ALU.mult).then_inc(dv, 1)
                else:
                    e.tensor_tensor(comb, ex[:], ws[:].unsqueeze(2).broadcast_to([P, NT, n_exp]),
                                    ALU.mult).then_inc(dv, 1)
                c += 1
                e.wait_ge(dv, c)


def experts_phase(core, tag, comb, n_exp, inter, next_raw, table, indices, looked_up):
    nc = core.nc
    N_LUT = 16
    LK_COLS = sum(cols for _, cols in indices)
    LK_W = LK_COLS // (n_exp * B // 2)
    assert LK_W * n_exp * B // 2 == LK_COLS
    NM = inter // P
    GU, DN = KD * 2 * inter, NM * D
    NG = n_exp * B
    with Phase(core, tag) as ph:
        rawe = ph.sb("rawe", [P, GU + DN])
        w = [ph.sb("w_hi", [P, 2, GU + DN], F32R), ph.sb("w_lo", [P, 2, GU + DN], F32R)]
        up = [x[:, :, 0:GU].rearrange("p e (k c) -> p e k c", k=KD) for x in w]
        down = [x[:, :, GU:GU + DN].rearrange("p e (m c) -> p e m c", m=NM) for x in w]
        H = [ph.sb("H_hi", [P, 2, NM, S], F32R), ph.sb("H_lo", [P, 2, NM, S], F32R)]
        SU = ph.sb("SU", [P, 2, S])
        HF = ph.sb("HF", [P, 2, S])
        lut = ph.sb("lut", [P, N_LUT])
        LK = ph.sb("looked_up", [P, LK_COLS])
        idx = ph.sb("idx", [P, LK_W])
        term = ph.sb("term", [P, 2, LK_W])
        total = ph.sb("total", [P, LK_W])
        lk_in = ph.sem("lk_in")
        lk = ph.sem("lk")
        lk_out = ph.sem("lk_out")
        UG = ph.ps("UG", [P, 2, 2, S])
        Y = ph.ps("Y", [P, TPB, S])
        act_split, dve_split, w_ready, n_split = split_on(ph, w[0][:, 0, :], w[1][:, 0, :], GU + DN)
        rawe_in = ph.sem("rawe_in")
        rawe_free = ph.sem("rawe_free")
        whole = ph.sem("whole")
        up_ready = ph.sem("up_ready")
        gate_ready = ph.sem("gate_ready")
        silu_done = ph.sem("silu_done")
        h_done = ph.sem("h_done")
        h_hi = ph.sem("h_hi")
        h_lo = ph.sem("h_lo")
        y_ready = ph.sem("y_ready")
        added = ph.sem("added")
        src_gu, src_dn = core.arrays[tag + "_gu"], core.arrays[tag + "_dn"]

        def run(e, emit, at_first=None):
            for g in range(3):
                emit(g, g % 8)
            loops = (NG - 1 - 3) // 8
            with e.Fori(0, loops) as i:
                for c in range(3, 11):
                    emit(8 * i + c, c % 8)
            for g in range(3 + 8 * loops, NG):
                emit(g, g % 8)

        with nc.Block() as block:
            @block.sync
            def _(e):
                def load(x):
                    e.dma_start(rawe[:, 0:GU], src_gu[bass.ds(x, 1), :, :].rearrange("e p c -> (e p) c")).then_inc(rawe_in, 16)
                    e.dma_start(rawe[:, GU:GU + DN], src_dn[bass.ds(x, 1), :, :].rearrange("e p c -> (e p) c")).then_inc(rawe_in, 16)
                load(1)
                e.dma_start(lut[:], core.arrays[table].partition_broadcast(P)).then_inc(lk_in, 16)
                at = 0
                for name, cols in indices:
                    e.dma_start(LK[:, at:at + cols].bitcast(I32), core.arrays[name]).then_inc(lk_in, 16)
                    at += cols
                e.wait_ge(w_ready, n_split)
                core.load_raw(e, next_raw)
                for x in range(2, n_exp):
                    e.wait_ge(rawe_free, x - 1)
                    load(x)
                e.wait_ge(lk, N_LUT * NG)
                e.dma_start(core.arrays[looked_up], LK[:]).then_inc(lk_out, 16)
                e.wait_ge(lk_out, 16)

            @block.gpsimd
            def _(e):
                for x in range(1, n_exp):
                    e.wait_ge(rawe_in, 32 * x)
                    need(e, y_ready, NT * (x - 1))
                    e.tensor_copy(w[0][:, x % 2, :], rawe[:]).then_inc(whole, 1)
                    e.wait_ge(whole, x)
                    e.tensor_tensor(w[1][:, x % 2, :], rawe[:], w[0][:, x % 2, :].bitcast(F32),
                                    ALU.subtract).then_inc(rawe_free, 1)

            @block.tensor
            def _(e):
                def ups(g, c):
                    x, ch = (c // 4) % 2, c % 4
                    if ch == 0:
                        if isinstance(g, int) and g == 0:
                            e.wait_ge(w_ready, n_split)
                        else:
                            e.wait_ge(rawe_free, (g - c) // 4 + c // 4)
                    for m in range(NM):
                        n = NM * g + m
                        for side, (free, ready) in enumerate(((silu_done, up_ready), (h_done, gate_ready))):
                            need(e, free, n - 1)
                            for k in range(KD):
                                for j, (wi, xi) in enumerate(HI_LO):
                                    a = side * inter + m * P
                                    mm = e.matmul(UG[:, m % 2, side, :], up[wi][:, x, k, a:a + P],
                                                  core.XT[xi][:, k, ch * S:(ch + 1) * S],
                                                  start=(k == 0 and j == 0), stop=(k == KD - 1 and j == 2))
                            mm.then_inc(ready, 1)

                def downs(g, c):
                    x, ch = (c // 4) % 2, c % 4
                    e.wait_ge(h_lo, NM * g + NM)
                    for tt in range(TPB):
                        need(e, added, TPB * g + (tt - 3))
                        for m in range(NM):
                            for j, (hi, wi) in enumerate(HI_LO):
                                mm = e.matmul(Y[:, tt, 0:D], H[hi][:, c % 2, m, tt * P:(tt + 1) * P],
                                              down[wi][:, x, m, :], start=(m == 0 and j == 0),
                                              stop=(m == NM - 1 and j == 2))
                        mm.then_inc(y_ready, 1)

                def emit(g, c):
                    if not isinstance(g, int) or g + 1 < NG:
                        ups(g + 1, (c + 1) % 8)
                    downs(g, c)
                ups(0, 0)
                run(e, emit)

            @block.scalar
            def _(e):
                def hidden(g, c):
                    for m in range(NM + 1):
                        n = NM * g + m
                        if m < NM:
                            e.wait_ge(up_ready, n + 1)
                            need(e, h_done, n - 1)
                            e.activation(SU[:, m % 2], UG[:, m % 2, 0, :], ACT.Silu).then_inc(silu_done, 1)
                        if m >= 1:
                            e.wait_ge(h_done, n)
                            if m == 1:
                                need(e, y_ready, TPB * (g - 1))
                            e.activation(H[0][:, c % 2, m - 1], HF[:, (m - 1) % 2], ACT.Copy).then_inc(h_hi, 1)

                def emit(g, c):
                    if not isinstance(g, int) or g + 1 < NG:
                        hidden(g + 1, (c + 1) % 8)
                act_split()
                hidden(0, 0)
                run(e, emit)

            @block.vector
            def _(e):
                def hidden(g, c):
                    for m in range(NM + 1):
                        n = NM * g + m
                        if m < NM:
                            e.wait_ge(gate_ready, n + 1)
                            e.wait_ge(silu_done, n + 1)
                            need(e, h_lo, n - 1)
                            need(e, h_hi, n - 1)
                            e.tensor_tensor(HF[:, m % 2], UG[:, m % 2, 1, :], SU[:, m % 2], ALU.mult).then_inc(h_done, 1)
                        if m >= 1:
                            e.wait_ge(h_hi, n)
                            e.tensor_tensor(H[1][:, c % 2, m - 1], HF[:, (m - 1) % 2],
                                            H[0][:, c % 2, m - 1].bitcast(F32), ALU.subtract).then_inc(h_lo, 1)
                        if m < NM and not (isinstance(g, int) and g == 0):
                            lookup(g - 1, (c - 1) % 8, m)

                def lookup(g, c, m):
                    j = 8 * (c % 2) + 2 * m
                    base = N_LUT * g + 4 * m
                    piece = LK[:, bass.ds(((g - c) // 2 + c // 2) * LK_W, LK_W)]
                    if j == 0:
                        need(e, lk, base)
                        e.tensor_copy(idx[:], piece.bitcast(I32)).then_inc(lk, 1)
                        e.wait_ge(lk, base + 1)
                        e.tensor_scalar(total[:], idx[:], 0.0, lut[:, 0:1], ALU.is_equal, ALU.mult).then_inc(lk, 1)
                        e.tensor_scalar(term[:, 1], idx[:], 1.0, lut[:, 1:2], ALU.is_equal, ALU.mult).then_inc(lk, 1)
                    else:
                        e.wait_ge(lk, base - 1)
                        e.tensor_scalar(term[:, 0], idx[:], float(j), lut[:, j:j + 1],
                                        ALU.is_equal, ALU.mult).then_inc(lk, 1)
                        e.wait_ge(lk, base)
                        e.tensor_scalar(term[:, 1], idx[:], float(j + 1), lut[:, j + 1:j + 2],
                                        ALU.is_equal, ALU.mult).then_inc(lk, 1)
                        e.wait_ge(lk, base + 1)
                        e.tensor_tensor(total[:], total[:], term[:, 0], ALU.add).then_inc(lk, 1)
                    e.wait_ge(lk, base + 3)
                    e.tensor_tensor(piece if j + 2 == N_LUT else total[:], total[:], term[:, 1],
                                    ALU.add).then_inc(lk, 1)

                def emit(g, c):
                    if not isinstance(g, int) or g + 1 < NG:
                        hidden(g + 1, (c + 1) % 8)
                    if isinstance(g, int) and g + 1 == NG:
                        for m in range(NM):
                            lookup(g, c, m)
                    ch = c % 4
                    x = (g - c) // 4 + c // 4
                    for tt in range(TPB):
                        t = ch * TPB + tt
                        e.wait_ge(y_ready, TPB * g + (tt + 1))
                        e.scalar_tensor_tensor(out=core.X[:, t], in0=Y[:, tt, 0:D],
                                               scalar=comb[:, bass.ds(x, 1), t:t + 1].rearrange("p a b -> p (a b)"),
                                               in1=core.X[:, t], op0=ALU.mult, op1=ALU.add).then_inc(added, 1)
                dve_split()
                e.wait_ge(lk_in, 16 * (len(indices) + 1))
                hidden(0, 0)
                run(e, emit)
                e.wait_ge(added, NG * TPB)


def prepare_plain(core, tag, w, cols):
    with Phase(core, tag + "s") as ph:
        act_split, dve_split, w_lo, n = split_on(ph, w[0], w[1], cols)
        with core.nc.Block() as block:
            @block.scalar
            def _(e):
                act_split()

            @block.vector
            def _(e):
                dve_split()
                e.wait_ge(w_lo, n)


def head_mixing_phase(core, tag, O, next_raw, next_bias):
    nc = core.nc
    H, HD = 16, 16
    scratch = nc.dram_tensor("l3_mixed", [B, H, S, HD], F32).ap()
    with Phase(core, tag) as ph:
        n_w = KD * 3 * D
        w = [ph.sb("w_hi", [P, n_w], F32R), ph.sb("w_lo", [P, n_w], F32R)]
        wv = [x[:].rearrange("p (k c) -> p k c", k=KD) for x in w]
        act_split, dve_split, w_ready, n_split = split_on(ph, w[0], w[1], n_w)
        bias = ph.sb("bias", [1, 3 * D])
        ones = ph.sb("ones", [1, P])
        trig = ph.sb("trig", [P, 2, TPB, 8])
        NB = 6
        RT = ph.sb("RT", [P, 2, 2, 2 * D])
        VV = ph.sb("VV", [P, NB, D])
        RO = ph.sb("RO", [P, 3, 2 * D])
        PRD = ph.sb("PRD", [P, 2, HD, H * H])
        AVP = ph.sb("AVP", [P, 2, H * HD * H])
        SC = ph.sb("SC", [P, NB, H, H])
        mx = ph.sb("mx", [P, 2, H])
        sm = ph.sb("sm", [P, 2, H])
        OO = ph.sb("OO", [P, 2, D])
        qk_ps = ph.ps("qk", [P, 2, 512])
        v_ps = ph.ps("v", [P, 2, 512])
        sc_ps = ph.ps("sc", [P, 2, 512])
        const_in = ph.sem("const_in")
        ones_set = ph.sem("ones_set")
        qk_ready = ph.sem("qk_ready")
        v_ready = ph.sem("v_ready")
        rt_done = ph.sem("rt_done")
        v_done = ph.sem("v_done")
        ro_done = ph.sem("ro_done")
        prd_done = ph.sem("prd_done")
        sc_ready = ph.sem("sc_ready")
        mx_done = ph.sem("mx_done")
        sub_done = ph.sem("sub_done")
        exp_done = ph.sem("exp_done")
        sm_done = ph.sem("sm_done")
        rc_done = ph.sem("rc_done")
        a_done = ph.sem("a_done")
        av_done = ph.sem("av_done")
        av_rest = ph.sem("av_rest")
        o_done = ph.sem("o_done")
        stored = [ph.sem(f"stored{i}") for i in range(2)]
        o_in = ph.sem("o_in")
        bias_done = ph.sem("bias_done")
        bias_n = core.n_bias

        def av_product(e, t, lo, hi):
            shape = [P, hi - lo, HD, H]
            a = SC[:, t % NB, lo:hi].unsqueeze(2).broadcast_to(shape)
            v = VV[:, t % NB].rearrange("p (t d) -> p d t", t=H).unsqueeze(1).broadcast_to(shape)
            out = AVP[:, t % 2].rearrange("p (h d t) -> p h d t", h=H, d=HD)[:, lo:hi]
            return e.tensor_tensor(out, a, v, ALU.mult)

        def pool_heads(t):
            return 15 if t < NT - 4 else 6
        with nc.Block() as block:
            @block.sync
            def _(e):
                e.dma_start(bias[:], core.arrays["l3_bqkv"]).then_inc(const_in, 16)
                e.dma_start(trig[:], core.arrays["trig"].rearrange("f (t p) c -> p f t c", p=P)).then_inc(const_in, 16)
                e.wait_ge(w_ready, n_split)
                core.load_raw(e, next_raw)
                for t in range(NT):
                    b, st = divmod(t, TPB)
                    e.wait_ge(o_done, t + 1)
                    e.dma_start(scratch[b, :, st * P:(st + 1) * P, :].rearrange("h s d -> s h d"),
                                OO[:, t % 2, :].rearrange("p (h d) -> p h d", h=H)).then_inc(stored[t % 2], 16)
                    if st == TPB - 1:
                        e.wait_ge(stored[0], 8 * (t + 1))
                        e.wait_ge(stored[1], 8 * (t + 1))
                        e.dma_start(O[:, b * TPB:(b + 1) * TPB, :],
                                    scratch[b].rearrange("h s d -> (h s d)").rearrange("(t p c) -> p t c", p=P, c=D)
                                    ).then_inc(o_in, 16)
                e.wait_ge(o_in, 16 * B)

            @block.tensor
            def _(e):
                e.wait_ge(w_ready, n_split)
                e.wait_ge(const_in, 32)
                e.wait_ge(ones_set, 1)
                for i in range(NT + 2):
                    t = i
                    for ps, lo, hi, free, ready in ((qk_ps, 0, 2 * D, rt_done, qk_ready),
                                                    (v_ps, 2 * D, 3 * D, v_done, v_ready)) if i < NT else ():
                        need(e, free, t - 1)
                        out = ps[:, t % 2, 0:hi - lo]
                        e.matmul(out, ones[:], bias[:, lo:hi], start=True, stop=False)
                        for k in range(KD):
                            for j, (xi, wi) in enumerate(HI_LO):
                                mm = e.matmul(out, core.XT[xi][:, k, t * P:(t + 1) * P], wv[wi][:, k, lo:hi],
                                              start=False, stop=(k == KD - 1 and j == 2))
                        mm.then_inc(ready, 1)

                    t = i - 2
                    if 0 <= t < NT:
                        e.wait_ge(prd_done, t + 1)
                        need(e, sub_done, t - 1)
                        for d in range(HD):
                            mm = e.matmul(sc_ps[:, t % 2, 0:H * H], core.ident[:], PRD[:, t % 2, d, :],
                                          start=(d == 0), stop=(d == HD - 1))
                        mm.then_inc(sc_ready, 1)

            @block.scalar
            def _(e):
                act_split()
                e.wait_ge(const_in, 32)
                for i in range(NT + 2):
                    if i < NT:
                        s, st = i % 2, i % TPB
                        e.wait_ge(qk_ready, i + 1)
                        need(e, ro_done, i - 1)
                        x = qk_ps[:, s, :].rearrange("p (g c r) -> p c g r", c=8, r=2)
                        for f in range(2):
                            r = RT[:, s, f, :].rearrange("p (g c r) -> p c g r", c=8, r=2)
                            for c in range(8):
                                mm = e.activation(r[:, c], x[:, c], ACT.Identity, scale=trig[:, f, st, c:c + 1])
                        mm.then_inc(rt_done, 1)
                        e.wait_ge(v_ready, i + 1)
                        need(e, av_done, i - (NB - 1))
                        need(e, av_rest, i - (NB - 1))
                        e.activation(VV[:, i % NB], v_ps[:, i % 2, 0:D], ACT.Copy).then_inc(v_done, 1)
                    t = i - 2
                    if 0 <= t < NT:
                        e.wait_ge(sub_done, t + 1)
                        e.activation(SC[:, t % NB], SC[:, t % NB], ACT.Exp, scale=HD ** -0.5).then_inc(exp_done, 1)

            @block.gpsimd
            def _(e):
                e.wait_ge(core.bias_loaded, bias_n)
                e.tensor_tensor(core.X[:], core.X[:], core.bias[:].unsqueeze(1).broadcast_to([P, NT, D]),
                                ALU.add).then_inc(bias_done, 1)
                for i in range(NT + 4):
                    if i < NT:
                        e.wait_ge(rt_done, i + 1)
                        need(e, prd_done, i - 2)
                        tc = RT[:, i % 2, 0, :].rearrange("p (g r) -> p r g", r=2)
                        ts = RT[:, i % 2, 1, :].rearrange("p (g r) -> p r g", r=2)
                        r = RO[:, i % 3].rearrange("p (g r) -> p r g", r=2)
                        e.tensor_tensor(r[:, 0], tc[:, 0], ts[:, 1], ALU.subtract)
                        e.tensor_tensor(r[:, 1], ts[:, 0], tc[:, 1], ALU.add).then_inc(ro_done, 1)
                    t = i - 4
                    if 0 <= t < NT:
                        e.wait_ge(a_done, t + 1)
                        need(e, o_done, t - 1)
                        av_product(e, t, 0, pool_heads(t)).then_inc(av_done, 1)
                e.wait_ge(bias_done, 1)

            @block.vector
            def _(e):
                e.memset(ones[:], 1.0).then_inc(ones_set, 1)
                dve_split()
                for i in range(NT + 5):
                    if i < NT:
                        e.wait_ge(ro_done, i + 1)
                        need(e, sc_ready, i - 1)
                        qv = RO[:, i % 3, 0:D].rearrange("p (h d) -> p d h", h=H).unsqueeze(3).broadcast_to([P, HD, H, H])
                        kv = RO[:, i % 3, D:2 * D].rearrange("p (t d) -> p d t", t=H).unsqueeze(2).broadcast_to([P, HD, H, H])
                        e.tensor_tensor(PRD[:, i % 2].rearrange("p d (h t) -> p d h t", h=H), qv, kv,
                                        ALU.mult).then_inc(prd_done, 1)
                    t = i - 2
                    if 0 <= t < NT:
                        s = t % 2
                        e.wait_ge(exp_done, t + 1)
                        need(e, rc_done, t - 1)
                        e.tensor_reduce(sm[:, s], SC[:, t % NB], AXX, ALU.add).then_inc(sm_done, 1)
                        e.wait_ge(sm_done, t + 1)
                        e.reciprocal(mx[:, s], sm[:, s]).then_inc(rc_done, 1)
                        e.wait_ge(rc_done, t + 1)
                        e.tensor_tensor(SC[:, t % NB], SC[:, t % NB], mx[:, s].unsqueeze(2).broadcast_to([P, H, H]),
                                        ALU.mult).then_inc(a_done, 1)
                    t = i - 1
                    if 0 <= t < NT:
                        s = t % 2
                        sc = sc_ps[:, s, 0:H * H].rearrange("p (h t) -> p h t", h=H)
                        e.wait_ge(sc_ready, t + 1)
                        need(e, a_done, t - 1)
                        e.tensor_reduce(mx[:, s], sc, AXX, ALU.max).then_inc(mx_done, 1)
                        e.wait_ge(mx_done, t + 1)
                        need(e, av_done, t - (NB - 1))
                        need(e, av_rest, t - (NB - 1))
                        e.tensor_tensor(SC[:, t % NB], sc, mx[:, s].unsqueeze(2).broadcast_to([P, H, H]),
                                        ALU.subtract).then_inc(sub_done, 1)
                    t = i - 4
                    if 0 <= t < NT:
                        e.wait_ge(a_done, t + 1)
                        need(e, o_done, t - 1)
                        av_product(e, t, pool_heads(t), H).then_inc(av_rest, 1)
                    t = i - 5
                    if 0 <= t < NT:
                        e.wait_ge(av_done, t + 1)
                        e.wait_ge(av_rest, t + 1)
                        need(e, stored[t % 2], 16 * (t // 2))
                        e.tensor_reduce(OO[:, t % 2].rearrange("p (h d) -> p h d", h=H),
                                        AVP[:, t % 2].rearrange("p (h d t) -> p h d t", h=H, d=HD), AXX,
                                        ALU.add).then_inc(o_done, 1)


def mixture_weights_phase(core, tag, comb, C, next_raw):
    nc = core.nc
    K = 8
    with Phase(core, tag) as ph:
        amp = ph.sb("amp", [P, K, 2])
        sq = ph.sb("sq", [P, K, 2])
        p8 = ph.sb("p8", [P, K])
        s1 = ph.sb("s1", [P, 2])
        mix = ph.sb("mix", [P, K])
        CT = ph.sb("CT", [P, 2, P])
        TP = ph.ps("TP", [P, 2, 512])
        CP = ph.ps("CP", [P, NT, K])
        amp_in = ph.sem("amp_in")
        dv = ph.sem("dv")
        tp_ready = ph.sem("tp_ready")
        ct_done = ph.sem("ct_done")
        c_ready = ph.sem("c_ready")
        c_done = ph.sem("c_done")
        with nc.Block() as block:
            @block.sync
            def _(e):
                e.dma_start(amp[:], core.arrays["l3_amp"]).then_inc(amp_in, 16)
                core.load_raw(e, next_raw)

            @block.tensor
            def _(e):
                for i in range(NT + 1):
                    if i < NT:
                        need(e, ct_done, i - 1)
                        e.transpose(TP[:, i % 2, 0:P], comb[:, i, :], core.ident[:]).then_inc(tp_ready, 1)
                    if i >= 1:
                        if i == 1:
                            e.wait_ge(dv, 6)
                        e.wait_ge(ct_done, i)
                        e.matmul(CP[:, i - 1, :], CT[:, (i - 1) % 2, :], mix[:], start=True, stop=True).then_inc(c_ready, 1)

            @block.scalar
            def _(e):
                for i in range(NT):
                    e.wait_ge(tp_ready, i + 1)
                    need(e, c_ready, i - 1)
                    e.activation(CT[:, i % 2, :], TP[:, i % 2, 0:P], ACT.Copy).then_inc(ct_done, 1)

            @block.vector
            def _(e):
                e.wait_ge(amp_in, 16)
                e.tensor_tensor(sq[:], amp[:], amp[:], ALU.mult).then_inc(dv, 1)
                e.wait_ge(dv, 1)
                e.tensor_reduce(p8[:], sq[:], AXX, ALU.add).then_inc(dv, 1)
                e.wait_ge(dv, 2)
                e.tensor_reduce(s1[:, 0:1], p8[:], AXX, ALU.add).then_inc(dv, 1)
                e.wait_ge(dv, 3)
                e.tensor_scalar(s1[:, 1:2], s1[:, 0:1], 1e-8, None, ALU.add).then_inc(dv, 1)
                e.wait_ge(dv, 4)
                e.reciprocal(s1[:, 0:1], s1[:, 1:2]).then_inc(dv, 1)
                e.wait_ge(dv, 5)
                e.tensor_scalar(mix[:], p8[:], s1[:, 0:1], None, ALU.mult).then_inc(dv, 1)
                e.wait_ge(c_ready, NT)
                e.tensor_copy(C[:], CP[:]).then_inc(c_done, 1)
                e.wait_ge(c_done, 1)


def mixture_phase(core, tag, C):
    nc = core.nc
    K, I = 8, 128
    NG, NSH = KD * K * I, KD * 2 * I
    cols = 2 * NG + 2 * NSH + 3 * D
    with Phase(core, tag) as ph:
        w = [ph.sb("w_hi", [P, cols], F32R), ph.sb("w_lo", [P, cols], F32R)]
        main = [x[:, 0:2 * NG].rearrange("p (s k c) -> p s k c", s=2, k=KD) for x in w]
        shared = [x[:, 2 * NG:2 * NG + 2 * NSH].rearrange("p (s k c) -> p s k c", s=2, k=KD) for x in w]
        down = [x[:, 2 * NG + 2 * NSH:cols].rearrange("p (m c) -> p m c", m=3) for x in w]
        act_split, dve_split, w_ready, n_split = split_on(ph, w[0], w[1], cols)
        SG = ph.sb("SG", [P, 2, 512])
        T = ph.sb("T", [P, 2, 512])
        MS = ph.sb("MS", [P, 2, 3, P])
        HT = [ph.sb("HT_hi", [P, 2, 3 * P], F32R), ph.sb("HT_lo", [P, 2, 3 * P], F32R)]
        UG = ph.ps("UG", [P, 2, 2, 512])
        TP = ph.ps("TP", [P, 2, 512])
        tail = Tail(ph, last=True)
        ug_ready = ph.sem("ug_ready")
        silu_done = ph.sem("silu_done")
        t_done = ph.sem("t_done")
        acc_done = ph.sem("acc_done")
        tp_ready = ph.sem("tp_ready")
        ht_hi = ph.sem("ht_hi")
        ht_lo = ph.sem("ht_lo")
        with nc.Block() as block:
            @block.sync
            def _(e):
                for t in range(NT):
                    tail.sync_store(t)
                e.wait_ge(tail.stored, 16 * NT)

            @block.gpsimd
            def _(e):
                tail.pool_setup()
                for t in range(NT):
                    tail.pool_rstd(t)

            def pe_t(e, t):
                e.wait_ge(acc_done, K * (t + 1))
                e.wait_ge(t_done, 3 * (t + 1))
                need(e, ht_lo, t - 1)
                for m in range(3):
                    mm = e.transpose(TP[:, t % 2, m * P:(m + 1) * P], MS[:, t % 2, m, :], core.ident[:])
                mm.then_inc(tp_ready, 1)

            def pe_down(e, t):
                e.wait_ge(ht_lo, t + 1)
                need(e, tail.summed, t - 1)
                for m in range(3):
                    for j, (hi, wi) in enumerate(HI_LO):
                        mm = e.matmul(tail.y[:, t % 2, 0:D], HT[hi][:, t % 2, m * P:(m + 1) * P], down[wi][:, m, :],
                                      start=(m == 0 and j == 0), stop=(m == 2 and j == 2))
                mm.then_inc(tail.y_ready, 1)

            @block.tensor
            def _(e):
                e.wait_ge(w_ready, n_split)
                for i in range(NT + 2):
                    if i < NT:
                        for it in range(3):
                            n = 3 * i + it
                            need(e, t_done, n - 1)
                            for side in range(2):
                                N = 512 if it < 2 else 256
                                for k in range(KD):
                                    for j, (xi, wi) in enumerate(HI_LO):
                                        rhs = main[wi][:, side, k, it * 512:(it + 1) * 512] if it < 2 else \
                                            shared[wi][:, side, k, :]
                                        mm = e.matmul(UG[:, n % 2, side, 0:N], core.XT[xi][:, k, i * P:(i + 1) * P], rhs,
                                                      start=(k == 0 and j == 0), stop=(k == KD - 1 and j == 2))
                            mm.then_inc(ug_ready, 1)
                            if it == 0 and 0 <= i - 1 < NT:
                                pe_t(e, i - 1)
                            if it == 1 and 0 <= i - 1 < NT:
                                pe_down(e, i - 1)
                    elif i - 1 < NT:
                        pe_t(e, i - 1)
                        pe_down(e, i - 1)

            @block.scalar
            def _(e):
                act_split()
                for i in range(NT + 1):
                    for it in range(3):
                        if i < NT:
                            n = 3 * i + it
                            N = 512 if it < 2 else 256
                            e.wait_ge(ug_ready, n + 1)
                            need(e, t_done, n - 1)
                            e.activation(SG[:, n % 2, 0:N], UG[:, n % 2, 0, 0:N], ACT.Silu).then_inc(silu_done, 1)
                        if it == 0 and i >= 1:
                            t = i - 1
                            e.wait_ge(tp_ready, t + 1)
                            need(e, tail.y_ready, t - 1)
                            e.activation(HT[0][:, t % 2], TP[:, t % 2, 0:3 * P], ACT.Copy).then_inc(ht_hi, 1)

            @block.vector
            def _(e):
                dve_split()

                def item(i, it):
                    n = 3 * i + it
                    e.wait_ge(silu_done, n + 1)
                    if it == 2:
                        need(e, tp_ready, i - 1)
                        e.tensor_tensor(MS[:, i % 2, 1:3, :].rearrange("p a b -> p (a b)"), SG[:, n % 2, 0:256],
                                        UG[:, n % 2, 1, 0:256], ALU.mult).then_inc(t_done, 1)
                        return
                    need(e, acc_done, K * i + 4 * it - 4)
                    e.tensor_tensor(T[:, it, :], SG[:, n % 2, :], UG[:, n % 2, 1, :], ALU.mult).then_inc(t_done, 1)
                    e.wait_ge(t_done, n + 1)
                    for kk in range(4):
                        k = 4 * it + kk
                        src, c = T[:, it, kk * I:(kk + 1) * I], C[:, i, k:k + 1]
                        if k == 0:
                            need(e, tp_ready, i - 1)
                            e.tensor_scalar(MS[:, i % 2, 0, :], src, c, None, ALU.mult).then_inc(acc_done, 1)
                        else:
                            e.wait_ge(acc_done, K * i + k)
                            e.scalar_tensor_tensor(out=MS[:, i % 2, 0, :], in0=src, scalar=c, in1=MS[:, i % 2, 0, :],
                                                   op0=ALU.mult, op1=ALU.add).then_inc(acc_done, 1)

                for i in range(NT + 2):
                    if i < NT:
                        item(i, 0)
                    if 0 <= i - 1 < NT:
                        t = i - 1
                        e.wait_ge(ht_hi, t + 1)
                        e.tensor_tensor(HT[1][:, t % 2], TP[:, t % 2, 0:3 * P], HT[0][:, t % 2].bitcast(F32),
                                        ALU.subtract).then_inc(ht_lo, 1)
                    if i < NT:
                        item(i, 1)
                        item(i, 2)
                    if 0 <= i - 1 < NT:
                        tail.dve_stats(i - 1)
                    if 0 <= i - 2 < NT:
                        tail.dve_norm(i - 2)
                e.wait_ge(tail.normed, NT)


def program(nc, arrays, out, upto=99):
    with ExitStack() as ctx:
        core = Core(nc, ctx, arrays, out)
        arrays["l1e_gu0"], arrays["l1e_dn0"] = arrays["l1e_gu"][0], arrays["l1e_dn"][0]
        arrays["l2_weights"] = nc.dram_tensor("l2_weights", [P, 4288], F32).ap()
        start_phase(core, [("l0_qkv", 1152)], "l0_bp")
        with Phase(core, "l0") as big:
            q = [big.sb("q_hi", [P, 8, S], F32R), big.sb("q_lo", [P, 8, S], F32R)]
            k = [big.sb("k_hi", [P, 8, S], F32R), big.sb("k_lo", [P, 8, S], F32R)]
            V = big.sb("V", [P, 8, TPB, 32])
            projection_phase(core, "l0p", q, k, V, 64, 576, 32 ** -0.5, [("l0_wp", 512)],
                             v_out=lambda part, b, kt: None if part else V[:, 2 * b:2 * b + 2, kt, :])
            O = core.XTF = big.sb("O", [P, 8, TPB, P])
            attention_phase(core, "l0a", q, k, V, O, 4, 8,
                            lambda u, r: O[:, bass.ds((u - r) // 4, 1), :, 32 * r:32 * r + 32].rearrange(
                                "p i t (a c) -> p (i t) a c", a=4), True, [])
            output_phase(core, "l0o", lambda t, kk: O[:, 2 * (t // TPB) + kk, t % TPB, :], [("l0_up", 2048), ("l0_gate", 2048), ("l0_down", 2048)])
        if upto == 0:
            return dump_phase(core)
        feed_forward_phase(core, "l0f", 1024, [("l1_qkv", 1536)], "l1_bo", ternary=True)
        if upto == 1:
            return dump_phase(core)
        with Phase(core, "l1") as big:
            q = [big.sb("q_hi", [P, 8, S], F32R), big.sb("q_lo", [P, 8, S], F32R)]
            k = [big.sb("k_hi", [P, 8, S], F32R), big.sb("k_lo", [P, 8, S], F32R)]
            v = [big.sb("v_hi", [P, NT, D], F32R), big.sb("v_lo", [P, NT, D], F32R)]
            O = big.sb("O", [P, NT, D])
            bqk, bv = load_biases(core, big, "l1_bqk", "l1_bv")
            projection_phase(core, "l1p", q, k, v, D, 768, 1.0, [("l1_wo", 512)], qk_bias=bqk, v_bias=bv,
                             v_out=lambda part, b, kt: v[part][:, b * TPB + kt, :])
            wide_attention_phase(core, "l1a", q, k, v, O, 1.0 / 16, [])
            output_phase(core, "l1o", lambda t, kk: O[:, t, kk * P:(kk + 1) * P], [("l1_router", 16)])
        if upto == 2:
            return dump_phase(core)
        with Phase(core, "l1m") as big:
            comb = big.sb("comb", [P, 8, NT])
            routing_phase(core, "l1r", comb[:].rearrange("p e t -> p t e"), 8, 2,
                          next_raw=[("l1e_gu0", 2048), ("l1e_dn0", 1024)])
            experts_phase(core, "l1e", comb, 8, 512, [("l1_base_gu", 2048), ("l1_base_dn", 1024)],
                          "l2_lut", [("l2_gate", 1376), ("l2_up", 1376), ("l2_down", 1536)], "l2_weights")
        feed_forward_phase(core, "l1f", 512, [("l2_qkv", 1536)], "l2_bo")
        if upto == 3:
            return dump_phase(core)
        with Phase(core, "l2") as big:
            O = big.sb("O", [P, B, TPB, D])
            with Phase(core, "l2x") as inner:
                q = [inner.sb("q_hi", [P, 8, S], F32R), inner.sb("q_lo", [P, 8, S], F32R)]
                k = [inner.sb("k_hi", [P, 8, S], F32R), inner.sb("k_lo", [P, 8, S], F32R)]
                V = inner.sb("V", [P, 8, TPB, P])
                projection_phase(core, "l2p", q, k, V, D, 768, 16 ** -0.5, [("l2_wo", 512)],
                                 v_out=lambda part, b, kt: None if part else V[:, 2 * b:2 * b + 2, kt, :])

                def o_at(u, r, g):
                    nh = 2 * ((u - r) // 4) + r // 2
                    return O[:, (2 * r + g) % 4, :, bass.ds(nh * 16, 16)]
                attention_phase(core, "l2a", q, k, V, O, 2, 16, o_at, True, [])
            output_phase(core, "l2o", lambda t, kk: O[:, t // TPB, t % TPB, kk * P:(kk + 1) * P],
                         [("l2_weights", 4288)])
        if upto == 4:
            return dump_phase(core)
        feed_forward_phase(core, "l2f", 688, [("l3_qkv", 1536)], "l3_bo")
        if upto == 5:
            return dump_phase(core)
        with Phase(core, "l3") as big:
            O = big.sb("O", [P, NT, D])
            head_mixing_phase(core, "l3a", O, [("l3_wo", 512)], None)
            output_phase(core, "l3o", lambda t, kk: O[:, t, kk * P:(kk + 1) * P], [("l3_router", 256)])
        if upto == 6:
            return dump_phase(core)
        with Phase(core, "l3m") as big:
            C = big.sb("C", [P, NT, 8])
            with Phase(core, "l3c") as inner:
                comb = inner.sb("comb", [P, NT, P])
                routing_phase(core, "l3r", comb[:], 128, 4, 1e-8, "l3_escale")
                mixture_weights_phase(core, "l3w", comb, C,
                                      [("l3_gate", 2048), ("l3_up", 2048), ("l3_sgate", 512), ("l3_sup", 512),
                                       ("l3_down", 256), ("l3_sdown", 512)])
            mixture_phase(core, "l3f", C)


def load_biases(core, big, qk_name, v_name):
    bqk = big.sb("bqk", [P, 4])
    bv = big.sb("bv", [P, D])
    done = big.sem("bias_in")
    with core.nc.Block() as block:
        @block.sync
        def _(e):
            e.dma_start(bqk[:], core.arrays[qk_name]).then_inc(done, 16)
            e.dma_start(bv[:], core.arrays[v_name].partition_broadcast(P)).then_inc(done, 16)
            e.wait_ge(done, 32)
    return bqk, bv


def dump_phase(core):
    nc = core.nc
    with Phase(core, "dump") as ph:
        done = ph.sem("done")
        with nc.Block() as block:
            @block.sync
            def _(e):
                e.dma_start(core.out.rearrange("(t p) d -> p t d", p=P), core.X[:]).then_inc(done, 16)
                e.wait_ge(done, 16)


def by_partition(w):
    return np.ascontiguousarray(np.moveaxis(w.reshape((w.shape[0] // P, P) + w.shape[1:]), 0, 1)).reshape(P, -1)


def head_mask(G):
    m = np.zeros((P, G), np.float32)
    for row in range(96):
        m[row, (row % 32) // (32 // G)] = 1
    for g in range(G):
        m[96 + g, g] = 1
    return m


def layout(inp):
    a = {}
    x = np.asarray(inp["L0_attn_x"]).reshape(NT * P, D)
    a["x"], a["xT"] = x, np.ascontiguousarray(x.T)
    wkv = np.asarray(inp["L0_attn_Wkv"])
    wk = np.repeat(wkv[:, :64].reshape(D, 8, 1, 8), 4, axis=2).reshape(D, D)
    a["l0_qkv"] = by_partition(np.concatenate([np.asarray(inp["L0_attn_Wq"]), wk, wkv[:, 64:]], axis=1))
    a["l0_wp"] = by_partition(np.asarray(inp["L0_attn_Wp"]))
    a["l0_up"] = by_partition(np.ascontiguousarray(np.asarray(inp["L0_ffn_W_up"]).T))
    a["l0_gate"] = by_partition(np.ascontiguousarray(np.asarray(inp["L0_ffn_W_gate"]).T))
    a["l0_down"] = by_partition(np.ascontiguousarray(np.asarray(inp["L0_ffn_W_down"]).T))
    a["l1_qkv"] = by_partition(np.ascontiguousarray(np.asarray(inp["L1_attn_w_qkv"]).T))
    b = np.asarray(inp["L1_attn_b_qkv"])
    a["l1_bqk"], a["l1_bv"] = by_partition(b[:512]), b[512:]
    a["l1_wo"] = by_partition(np.ascontiguousarray(np.asarray(inp["L1_attn_w_out"]).T))
    a["l1_bo"] = np.asarray(inp["L1_attn_b_out"])
    a["l1_router"] = by_partition(np.asarray(inp["L1_ffn_gate_w"]))
    gu = np.asarray(inp["L1_ffn_expert_gate_up"])
    a["l1e_gu"] = np.stack([by_partition(g) for g in gu])
    a["l1e_dn"] = np.stack([by_partition(g) for g in np.asarray(inp["L1_ffn_expert_down"])])
    g = np.asarray(inp["L1_ffn_base_gate_up"])
    a["l1_base_gu"] = np.concatenate([by_partition(g[:, :512]), by_partition(g[:, 512:])], axis=1)
    a["l1_base_dn"] = by_partition(np.asarray(inp["L1_ffn_base_down"]))
    w = np.asarray(inp["L2_attn_Wqkv"]).T.reshape(D, 16, 3, 16)
    a["l2_qkv"] = by_partition(np.concatenate([w[:, :, i].reshape(D, D) for i in range(3)], axis=1))
    a["l2_wo"] = by_partition(np.ascontiguousarray(np.asarray(inp["L2_attn_Wproj"]).T))
    a["l2_bo"] = np.asarray(inp["L2_attn_bproj"])
    a["l2_gate"] = by_partition(np.ascontiguousarray(np.asarray(inp["L2_ffn_gate_idx"]).T))
    a["l2_up"] = by_partition(np.ascontiguousarray(np.asarray(inp["L2_ffn_up_idx"]).T))
    dn = np.zeros((768, D), np.asarray(inp["L2_ffn_down_idx"]).dtype)
    dn[:688] = np.asarray(inp["L2_ffn_down_idx"]).T
    a["l2_down"] = by_partition(dn)
    a["l2_lut"] = np.asarray(inp["L2_ffn_lut"])
    f = {k: np.asarray(v) for k, v in inp.items() if k.startswith("L3")}
    a["l3_qkv"] = by_partition(np.concatenate([f[f"L3_attn_W{c}"].T for c in "qkv"], axis=1))
    a["l3_bqkv"] = np.concatenate([f[f"L3_attn_b{c}"] for c in "qkv"]).reshape(1, -1)
    a["l3_wo"] = by_partition(np.ascontiguousarray(f["L3_attn_Wo"].T))
    a["l3_bo"] = f["L3_attn_bo"]
    a["l3_router"] = by_partition(f["L3_ffn_w_router"])
    a["l3_escale"] = f["L3_ffn_expert_scale"]
    a["l3_amp"] = f["L3_ffn_amplitudes"]
    for name, key in (("gate", "w_gate"), ("up", "w_up"), ("sgate", "shared_w_gate"), ("sup", "shared_w_up"),
                      ("down", "w_down"), ("sdown", "shared_w_down")):
        a[f"l3_{name}"] = by_partition(f[f"L3_ffn_{key}"])
    freqs = np.outer(np.arange(S, dtype=np.float32),
                     (1.0 / 10000.0 ** (np.arange(0, 16, 2, dtype=np.float32) / 16)).astype(np.float32))
    a["trig"] = np.stack([np.cos(freqs), np.sin(freqs)]).astype(np.float32)
    a["l0_bp"] = np.asarray(inp["L0_attn_bp"])
    a["mask4"], a["mask2"] = head_mask(4), head_mask(2)
    return a


def kernel(**inputs):
    import concourse.bacc as _bacc
    from concourse.bass_utils import run_bass_kernel_spmd as _run

    nc = _bacc.Bacc("TRN2", target_bir_lowering=False, num_devices=1)
    arrays = {name: np.ascontiguousarray(a) for name, a in layout(inputs).items()}
    handles = {name: nc.dram_tensor(name, a.shape, mybir.dt.from_np(a.dtype), kind="ExternalInput").ap()
               for name, a in arrays.items()}
    out = nc.dram_tensor("out", (NT * P, D), F32, kind="ExternalOutput").ap()
    program(nc, handles, out)
    r = _run(nc, [arrays], core_ids=[0])
    return r.results[0]["out"].reshape(B, S, D)
```

```python
from contextlib import ExitStack

import numpy as np
import concourse.bass as bass
import concourse.mybir as mybir

F32 = mybir.dt.float32
F32R = mybir.dt.float32r
I32 = mybir.dt.int32
ACT = mybir.ActivationFunctionType
ALU = mybir.AluOpType
AXX = mybir.AxisListType.X

P = 128
B, S, D = 4, 512, 256
KD = D // P
NT = B * S // P
TPB = S // P
EPS_LN = 1e-5
RAW_COLS = 6144
HI_LO = ((0, 0), (0, 1), (1, 0))

STEP, LAST = "S0 M0 S1 M1 M2 P M3", "S0 M0 S1 M1 MT TO P M2 M3"
STEP2, LAST2 = "S0 S1 M0 M1 M2 P M3", "S0 M0 MT M1 S1 TO P M2 M3"


def need(eng, sem, value):
    if isinstance(value, int) and value <= 0:
        return
    eng.wait_ge(sem, value)


class Core:

    def __init__(self, nc, ctx, arrays, out):
        self.nc, self.arrays, self.out = nc, arrays, out
        sb = lambda name, shape, dt=F32: ctx.enter_context(nc.sbuf_tensor(name, shape, dt))
        sem = lambda name: ctx.enter_context(nc.semaphore(name))
        self.X = sb("X", [P, NT, D])
        self.xt_base = nc.sbuf_base
        sb("XT_slab", [P, 2 * KD * NT * P])
        self.XT = [self.lend(f"XT_{n}", [P, KD, NT * P], F32R, i * 4 * KD * NT * P) for i, n in enumerate(("hi", "lo"))]
        self.ident = sb("ident", [P, P])
        self.raw = sb("raw", [P, RAW_COLS])
        self.bias = sb("bias", [P, D])
        self.absum = sb("absum", [P, 3])
        self.raw_loaded = sem("raw_loaded")
        self.x_loaded = sem("x_loaded")
        self.bias_loaded = sem("bias_loaded")
        self.n_raw = self.n_bias = 0
        self.limbo = []

    def lend(self, name, shape, dt, at):
        assert at + 4 * int(np.prod(shape[1:])) <= 8 * KD * NT * P
        return self.nc.alloc_sbuf_tensor_at(name, shape, dt, offset=self.xt_base + at)

    def load_raw(self, eng, pieces):
        at = 0
        for name, cols in pieces:
            src = self.arrays[name]
            dst = self.raw[0:src.shape[0], at:at + cols]
            if src.dtype != F32:
                dst = dst.bitcast(src.dtype)
            eng.dma_start(dst, src).then_inc(self.raw_loaded, 16)
            self.n_raw += 16
            at += cols

    def load_bias(self, eng, name):
        eng.dma_start(self.bias[:], self.arrays[name].partition_broadcast(P)).then_inc(self.bias_loaded, 16)
        self.n_bias += 16


class Phase:

    def __init__(self, core, tag):
        self.core, self.tag, self.ctx, self.sems = core, tag, ExitStack(), []

    def __enter__(self):
        self.ctx.__enter__()
        return self

    def __exit__(self, *a):
        nc, limbo = self.core.nc, self.core.limbo
        if self.sems:
            for s in self.sems:
                nc.sync.sem_clear(s)
            limbo.append(self.sems)
            if len(limbo) > 2:
                for s in limbo.pop(0):
                    nc.release_semaphore(s)
        return self.ctx.__exit__(*a)

    def sb(self, name, shape, dt=F32):
        return self.ctx.enter_context(self.core.nc.sbuf_tensor(f"{self.tag}_{name}_s", shape, dt))

    def ps(self, name, shape, dt=F32):
        return self.ctx.enter_context(self.core.nc.psum_tensor(f"{self.tag}_{name}", shape, dt))

    def sem(self, name):
        self.sems.append(self.core.nc.alloc_semaphore(f"{self.tag}_{name}"))
        return self.sems[-1]


def split_on(phase, hi, lo, cols, chunk=1024, at=0, name="w"):
    core = phase.core
    w_hi = phase.sem(f"{name}_hi")
    w_lo = phase.sem(f"{name}_lo")
    starts = list(range(0, cols, chunk))
    loaded = core.n_raw

    def act():
        e = core.nc.scalar
        e.wait_ge(core.raw_loaded, loaded)
        for a in starts:
            b = min(cols, a + chunk)
            e.activation(hi[:, a:b], core.raw[:, at + a:at + b], ACT.Copy).then_inc(w_hi, 1)

    def dve():
        e = core.nc.vector
        e.wait_ge(core.raw_loaded, loaded)
        for n, a in enumerate(starts):
            b = min(cols, a + chunk)
            e.wait_ge(w_hi, n + 1)
            e.tensor_tensor(lo[:, a:b], core.raw[:, at + a:at + b], hi[:, a:b].bitcast(F32), ALU.subtract).then_inc(w_lo, 1)

    return act, dve, w_lo, len(starts)


class Tail:

    def __init__(self, phase, last=False, y_scale=None):
        core = self.core = phase.core
        self.y_scale = y_scale
        self.last = last
        self.y = phase.ps("y", [P, 2, 512])
        self.tx = phase.ps("tx", [P, 2, 512]) if not last else None
        self.R = phase.sb("R", [P, 2, D])
        self.xf = phase.sb("xf", [P, 2, KD, P]) if not last else None
        self.xo = phase.sb("xo", [P, 2, D]) if last else None
        self.st = phase.sb("st", [P, 2, 8])
        self.mv = phase.sb("mv", [P, 2, 2])
        self.ve = phase.sb("ve", [P, 2, 1])
        self.half = phase.sb("half", [P, 1])
        self.rstd = phase.sb("rstd", [P, 2, 1])
        s = phase.sem
        self.y_ready = s("y_ready")
        self.summed = s("summed")
        self.stats = s("stats")
        self.moments = s("moments")
        self.pow_c = s("pow_c")
        self.var_eps = s("var_eps")
        self.rstd_ready = s("rstd_ready")
        self.normed = s("normed")
        self.tx_ready = s("tx_ready")
        self.xt_hi = s("xt_hi")
        self.xt_lo = s("xt_lo")
        self.stored = s("stored")

    def dve_stats(self, t, between=()):
        e, s = self.core.nc.vector, t % 2
        e.wait_ge(self.y_ready, t + 1)
        need(e, self.normed, t - 1)
        if self.y_scale is None:
            e.tensor_tensor(self.R[:, s], self.y[:, s, 0:D], self.core.X[:, t], ALU.add).then_inc(self.summed, 1)
        else:
            e.scalar_tensor_tensor(out=self.R[:, s], in0=self.y[:, s, 0:D], scalar=self.y_scale,
                                   in1=self.core.X[:, t], op0=ALU.mult, op1=ALU.add).then_inc(self.summed, 1)
        if len(between) > 0:
            between[0]()
        e.wait_ge(self.summed, t + 1)
        e.bn_stats(self.st[:, s, 0:6], self.R[:, s]).then_inc(self.stats, 1)
        if len(between) > 1:
            between[1]()
        e.wait_ge(self.stats, t + 1)
        need(e, self.rstd_ready, t - 1)
        e.bn_aggr(self.mv[:, s], self.st[:, s, 0:6]).then_inc(self.moments, 1)

    def pool_rstd(self, t):
        e, s = self.core.nc.gpsimd, t % 2
        e.wait_ge(self.moments, t + 1)
        need(e, self.normed, t - 1)
        e.tensor_scalar(self.ve[:, s], self.mv[:, s, 1:2], EPS_LN, None, ALU.add).then_inc(self.var_eps, 1)
        e.wait_ge(self.var_eps, t + 1)
        e.tensor_tensor(self.rstd[:, s], self.ve[:, s], self.half[:], ALU.pow).then_inc(self.rstd_ready, 1)

    def pool_steps(self):
        self.core.nc.gpsimd.memset(self.half[:], -0.5).then_inc(self.pow_c, 1)
        self.core.nc.gpsimd.wait_ge(self.pow_c, 1)
        for i in range(NT + 2):
            if i < NT:
                self.pool_rstd(i)
            if i >= 2 and not self.last:
                self.pool_xt(i - 2)
        if not self.last:
            self.core.nc.gpsimd.wait_ge(self.xt_lo, NT)

    def dve_norm(self, t):
        e, s = self.core.nc.vector, t % 2
        e.wait_ge(self.rstd_ready, t + 1)
        if self.last:
            need(e, self.stored, 16 * (t - 1))
            dst = self.xo[:, s]
        else:
            dst = self.core.X[:, t]
        e.tensor_scalar(dst, self.R[:, s], self.mv[:, s, 0:1], self.rstd[:, s, 0:1],
                        ALU.subtract, ALU.mult).then_inc(self.normed, 1)

    def pe_transpose(self, t):
        e = self.core.nc.tensor
        e.wait_ge(self.normed, t + 1)
        need(e, self.xt_hi, t - 1)
        for k in range(KD):
            mm = e.transpose(self.tx[:, t % 2, k * P:(k + 1) * P], self.core.X[:, t, k * P:(k + 1) * P], self.core.ident[:])
        mm.then_inc(self.tx_ready, 1)

    def act_xt(self, t):
        e, s = self.core.nc.scalar, t % 2
        e.wait_ge(self.tx_ready, t + 1)
        need(e, self.xt_lo, t - 1)
        src = self.tx[:, s, 0:D].rearrange("p (k n) -> p k n", k=KD)
        e.activation(self.xf[:, s], src, ACT.Copy)
        e.activation(self.core.XT[0][:, :, t * P:(t + 1) * P], src, ACT.Copy).then_inc(self.xt_hi, 1)

    def pool_xt(self, t):
        e = self.core.nc.gpsimd
        e.wait_ge(self.xt_hi, t + 1)
        e.tensor_tensor(self.core.XT[1][:, :, t * P:(t + 1) * P], self.xf[:, t % 2],
                        self.core.XT[0][:, :, t * P:(t + 1) * P].bitcast(F32), ALU.subtract).then_inc(self.xt_lo, 1)

    def sync_store(self, t):
        e = self.core.nc.sync
        e.wait_ge(self.normed, t + 1)
        if t:
            e.wait_ge(self.stored, 16 * t)
        e.dma_start(self.core.out[t * P:(t + 1) * P, :], self.xo[:, t % 2]).then_inc(self.stored, 16)


def start_phase(core, next_raw, next_bias):
    nc = core.nc
    with Phase(core, "start") as ph:
        xt = ph.sb("xt", [P, KD, NT * P])
        xt_in = [ph.sem(f"xt_in{b}") for b in range(B)]
        zeroed = ph.sem("zeroed")
        made = ph.sem("made")
        hi_done = ph.sem("hi_done")
        lo_done = ph.sem("lo_done")
        with nc.Block() as block:
            @block.sync
            def _(e):
                src = core.arrays["xT"].rearrange("(k p) n -> p k n", p=P)
                for b in range(B):
                    e.dma_start(xt[:, :, b * S:(b + 1) * S], src[:, :, b * S:(b + 1) * S]).then_inc(xt_in[b], 16)
                core.load_raw(e, next_raw)
                core.load_bias(e, next_bias)
                e.dma_start(core.X[:], core.arrays["x"].rearrange("(t p) d -> p t d", p=P)).then_inc(core.x_loaded, 16)

            @block.gpsimd
            def _(e):
                e.memset(core.ident[:], 0.0).then_inc(zeroed, 1)
                e.wait_ge(zeroed, 1)
                e.affine_select(out=core.ident[:], in_=core.ident[:], compare_op=ALU.not_equal, fill=1.0,
                                base=0, pattern=[[-1, P]], channel_multiplier=1).then_inc(made, 1)
                e.wait_ge(made, 1)

            @block.scalar
            def _(e):
                for b in range(B):
                    e.wait_ge(xt_in[b], 16)
                    e.activation(core.XT[0][:, :, b * S:(b + 1) * S], xt[:, :, b * S:(b + 1) * S],
                                 ACT.Copy).then_inc(hi_done, 1)

            @block.vector
            def _(e):
                for b in range(B):
                    e.wait_ge(hi_done, b + 1)
                    e.tensor_tensor(core.XT[1][:, :, b * S:(b + 1) * S], xt[:, :, b * S:(b + 1) * S],
                                    core.XT[0][:, :, b * S:(b + 1) * S].bitcast(F32), ALU.subtract).then_inc(lo_done, 1)
                e.wait_ge(lo_done, B)


def projection_phase(core, tag, q, k, v, v_cols, cols, q_scale, next_raw, qk_bias=None, v_bias=None, v_out=None):
    nc = core.nc
    with Phase(core, tag) as ph:
        n_w = KD * cols
        w = [ph.sb("w_hi", [P, n_w], F32R), ph.sb("w_lo", [P, n_w], F32R)]
        wv = [x[:].rearrange("p (k c) -> p k c", k=KD) for x in w]
        act_split, dve_split, w_ready, n_split = split_on(ph, w[0], w[1], n_w)
        fm = ph.ps("fm", [P, 4, 512])
        tm = ph.ps("tm", [P, 2, 512])
        fm_ready = ph.sem("fm_ready")
        fm_hi = ph.sem("fm_hi")
        fm_lo = ph.sem("fm_lo")
        tm_ready = ph.sem("tm_ready")
        tm_hi = ph.sem("tm_hi")
        tm_lo = ph.sem("tm_lo")
        tiles = [(dst, half, m) for m, (dst, half) in enumerate((x, h) for x in (q, k) for h in range(2))]
        two = v_out(1, 0, 0) is not None
        if two:
            vtmp = ph.sb("vtmp", [P, 2, v_cols])
            v_sum = ph.sem("v_sum")
        raw_n, bias_n = core.n_raw, core.n_bias
        with nc.Block() as block:
            @block.sync
            def _(e):
                e.wait_ge(w_ready, n_split)
                core.load_raw(e, next_raw)

            @block.scalar
            def _(e):
                act_split()
                n = 0
                for b in range(B):
                    for dst, half, m in tiles:
                        e.wait_ge(fm_ready, n + 1)
                        scale = q_scale if dst is q else 1.0
                        if qk_bias is None:
                            e.activation(dst[0][:, 2 * b + half, :], fm[:, n % 4, :], ACT.Copy,
                                         scale=scale).then_inc(fm_hi, 1)
                        else:
                            e.activation(dst[0][:, 2 * b + half, :], fm[:, n % 4, :], ACT.Identity,
                                         bias=qk_bias[:, m:m + 1]).then_inc(fm_hi, 1)
                        n += 1

            @block.vector
            def _(e):
                dve_split()
                n = nv = 0
                for b in range(B):
                    for dst, half, m in tiles:
                        e.wait_ge(fm_hi, n + 1)
                        e.scalar_tensor_tensor(
                            out=dst[1][:, 2 * b + half, :], in0=fm[:, n % 4, :],
                            scalar=(q_scale if dst is q else 1.0) if qk_bias is None else qk_bias[:, m:m + 1],
                            in1=dst[0][:, 2 * b + half, :].bitcast(F32),
                            op0=ALU.mult if qk_bias is None else ALU.add, op1=ALU.subtract).then_inc(fm_lo, 1)
                        n += 1
                    for kt in range(TPB):
                        e.wait_ge(tm_ready, nv + 1)
                        src = tm[:, nv % 2, 0:v_cols]
                        d0, d1 = v_out(0, b, kt), v_out(1, b, kt)
                        if len(d0.shape) == 3:
                            src = src.rearrange("p (a c) -> p a c", a=d0.shape[1])
                        if v_bias is not None:
                            vb = v_bias[:] if len(d0.shape) == 2 else v_bias[:].rearrange("p (a c) -> p a c", a=d0.shape[1])
                        if not two:
                            e.tensor_copy(d0, src).then_inc(tm_hi, 1)
                        else:
                            vf = vtmp[:, nv % 2]
                            need(e, tm_lo, nv - 1)
                            e.tensor_tensor(vf, src, vb, ALU.add).then_inc(v_sum, 1)
                            e.wait_ge(v_sum, nv + 1)
                            e.tensor_copy(d0, vf).then_inc(tm_hi, 1)
                            e.wait_ge(tm_hi, nv + 1)
                            e.tensor_tensor(d1, vf, d0.bitcast(F32), ALU.subtract).then_inc(tm_lo, 1)
                        nv += 1

            @block.tensor
            def _(e):
                e.wait_ge(w_ready, n_split)
                n = nv = 0
                for b in range(B):
                    for dst, half, m in tiles:
                        need(e, fm_lo, n - 3)
                        for kk in range(KD):
                            for j, (wi, xi) in enumerate(HI_LO):
                                mm = e.matmul(fm[:, n % 4, :], wv[wi][:, kk, m * P:(m + 1) * P],
                                              core.XT[xi][:, kk, b * S:(b + 1) * S],
                                              start=(kk == 0 and j == 0), stop=(kk == KD - 1 and j == 2))
                        mm.then_inc(fm_ready, 1)
                        n += 1
                    for kt in range(TPB):
                        need(e, v_sum if two else tm_hi, nv - 1)
                        t = b * TPB + kt
                        for kk in range(KD):
                            for j, (xi, wi) in enumerate(HI_LO):
                                mm = e.matmul(tm[:, nv % 2, 0:v_cols], core.XT[xi][:, kk, t * P:(t + 1) * P],
                                              wv[wi][:, kk, 2 * D:2 * D + v_cols],
                                              start=(kk == 0 and j == 0), stop=(kk == KD - 1 and j == 2))
                        mm.then_inc(tm_ready, 1)
                        nv += 1


QUADS = 4


def attention_phase(core, tag, q, k, V, O, heads, hd, o_at, residual_bias, next_raw):
    nc = core.nc
    G = heads
    NS = G
    REP = 4 // G
    NU = B * 2 * QUADS
    RING = 3
    UNROLL = 4 if G == 4 else 12
    ring_order = [("max", 1, i) for i in range(4, 4 * G)] + [
        ("mt", 1, 0) if x == "MT" else ("to", -1, 0) if x == "TO" else ("max", 2, int(x[1]))
        for x in (LAST if G == 4 else LAST2).split() if x[0] == "M" or x == "TO"]
    filled = [(kind, u + du, i) for u in range(-2, NU + 1) for kind, du, i in ring_order if 0 <= u + du < NU]
    number = {item: n for n, item in enumerate(filled)}
    assert UNROLL * len(ring_order) % RING == 0
    with Phase(core, tag) as ph:
        PT = core.lend(f"{tag}_PT", [P, 2, 4, S], F32, 0)
        QA = core.lend(f"{tag}_QA", [P, 4, S], F32R, 16384)
        KR = core.lend(f"{tag}_KR", [P, 2, S], F32, 24576)
        OT = core.lend(f"{tag}_OT", [P, 2, S], F32, 28672)
        KA = ph.sb("KA", [P, 4, G, S], F32R)
        VA = ph.sb("VA", [P, 4, TPB, 32 if G == 4 else 64])
        mask = ph.sb("mask", [P, G])
        MX = ph.sb("MX", [P, 2, 4, G])
        RI = ph.sb("RI", [P, 4, 4])
        SM = ph.ps("SM", [P, RING, S])
        ST = ph.ps("ST", [P, 4, S])
        PV = ph.ps("PV", [P, S])
        q_in = [ph.sem(f"q_in{i}") for i in range(4)]
        k_in = [ph.sem(f"k_in{i}") for i in range(2)]
        mask_in = ph.sem("mask_in")
        zeroed = ph.sem("zeroed")
        ka_ready = ph.sem("ka_ready")
        va_ready = ph.sem("va_ready")
        sm_ready = ph.sem("sm_ready")
        mx_done = ph.sem("mx_done")
        mt_ready = ph.sem("mt_ready")
        m_done = ph.sem("m_done")
        st_ready = ph.sem("st_ready")
        exp_done = ph.sem("exp_done")
        pv_step = ph.sem("pv_step")
        ot_done = ph.sem("ot_done")
        to_ready = ph.sem("to_ready")
        ri_done = ph.sem("ri_done")
        os_done = ph.sem("os_done")
        o_done = ph.sem("o_done")
        bias_done = ph.sem("bias_done")
        seen_free = ph.sem("seen_free")
        zero_v = ph.sem("zero_v")
        bias_n = core.n_bias
        ROWS_M = 96

        def slot(kind, cu, i=0):
            return number[kind, cu, i] % RING

        def claim(e, kind, u, cu, i=0):
            n = number[kind, cu, i]
            if n >= RING:
                was, unit, j = filled[n - RING]
                unit = unit - cu + u
                sem, count = {"max": (mx_done, unit * (4 * G) + (j + 1)), "mt": (m_done, unit + 1),
                              "to": (o_done, unit + 1)}[was]
                e.wait_ge(sem, count)
            return SM[:, n % RING, :]

        def chunk(u, c):
            return [divmod(4 * c + i, G) for i in range(4)]

        def live(u):
            return not isinstance(u, int) or 0 <= u < NU

        def pe_max(e, u, cu, c, items=range(4)):
            if not live(u):
                return
            r = cu % 4
            if c == 0 and items[0] == 0:
                e.wait_ge(q_in[r], 12 * (u - r) + 48)
                e.wait_ge(ka_ready, G * u + G)
            for i in items:
                qt, g = chunk(u, c)[i]
                e.matmul(claim(e, "max", u, cu, 4 * c + i), QA[0:ROWS_M, r, qt * P:(qt + 1) * P], KA[0:ROWS_M, r, g, :],
                         start=True, stop=True).then_inc(sm_ready, 1)

        def dve_max(e, u, cu, c, items=range(4)):
            if not live(u):
                return
            r = cu % 4
            if c == 0 and items[0] == 0:
                need(e, mt_ready, u - 1)
            for i in items:
                qt, g = chunk(u, c)[i]
                e.wait_ge(sm_ready, u * (4 * G) + (4 * c + i + 1))
                e.tensor_reduce(MX[:, r % 2, qt, g:g + 1], SM[:, slot("max", cu, 4 * c + i), :], AXX, ALU.max).then_inc(mx_done, 1)

        def pe_mt(e, u, cu):
            if not live(u):
                return
            r = cu % 4
            e.wait_ge(mx_done, u * (4 * G) + 4 * G)
            maxima = claim(e, "mt", u, cu)
            for qt in range(4):
                mm = e.transpose(maxima[0:G, qt * P:(qt + 1) * P], MX[:, r % 2, qt, :], core.ident[:])
            mm.then_inc(mt_ready, 1)

        def dve_mrow(e, u, cu):
            if not live(u):
                return
            r = cu % 4
            e.wait_ge(mt_ready, u + 1)
            e.tensor_scalar(QA[ROWS_M:ROWS_M + G, r, :], SM[0:G, slot("mt", cu), :], -1.0, None, ALU.mult).then_inc(m_done, 1)

        def pe_scores(e, u, r, s, half):
            if not live(u):
                return
            if s == 0 and half == 0:
                e.wait_ge(m_done, u + 1)
            h = u * (2 * NS) + (2 * s + half)
            need(e, exp_done, h - 1)
            for a in (2 * half, 2 * half + 1):
                g, kt = a // REP, s * REP + a % REP
                mm = e.matmul(ST[:, a, :], KA[:, r, g, kt * P:(kt + 1) * P], QA[:, r, :], start=True, stop=True)
            mm.then_inc(st_ready, 1)

        def act_exp(e, u, s):
            if not live(u):
                return
            step = u * NS + s
            for half in range(2):
                e.wait_ge(st_ready, u * (2 * NS) + (2 * s + half + 1))
                if half == 0:
                    need(e, pv_step, step - 1)
                e.activation(PT[:, s % 2, 2 * half:2 * half + 2, :], ST[:, 2 * half:2 * half + 2, :],
                             ACT.Exp).then_inc(exp_done, 1)

        def pe_pv(e, u, r, s):
            if not live(u):
                return
            step = u * NS + s
            e.wait_ge(exp_done, u * (2 * NS) + (2 * s + 2))
            if s == 0:
                e.wait_ge(va_ready, u + 1)
                need(e, ot_done, u)
            for a in range(4):
                g, kt = a // REP, s * REP + a % REP
                va = VA[:, r, kt, 0:32] if G == 4 else VA[:, r, kt, 32 * g:32 * g + 32]
                mm = e.matmul(PV[32 * a:32 * a + 32, :], va, PT[:, s % 2, a, :], start=(s == 0), stop=(s == NS - 1),
                              tile_position=(0, 32 * a))
            mm.then_inc(pv_step, 1)

        def act_ot(e, u, r):
            if not live(u):
                return
            e.wait_ge(pv_step, u * NS + NS)
            need(e, to_ready, u - 1)
            e.activation(OT[:, r % 2, :], PV[:], ACT.Copy).then_inc(ot_done, 1)

        def pe_to(e, u, cu):
            if not live(u):
                return
            r = cu % 4
            e.wait_ge(ot_done, u + 1)
            out = claim(e, "to", u, cu)
            for qt in range(4):
                mm = e.transpose(out[:, qt * P:(qt + 1) * P], OT[:, r % 2, qt * P:(qt + 1) * P], core.ident[:])
            mm.then_inc(to_ready, 1)

        def dve_out(e, u, cu):
            if not live(u):
                return
            r = cu % 4
            out = SM[:, slot("to", cu), :]
            e.wait_ge(to_ready, u + 1)
            T = out.rearrange("p (t a c) -> p t a c", t=4, a=4)
            if G == 4:
                need(e, o_done, u)
                e.reciprocal(RI[:], T[:, :, :, hd]).then_inc(ri_done, 1)
                e.wait_ge(ri_done, u + 1)
                e.tensor_tensor(o_at(u, r), T[:, :, :, 0:hd],
                                RI[:].unsqueeze(3).broadcast_to([P, 4, 4, hd]), ALU.mult).then_inc(o_done, 1)
            else:
                T2 = out.rearrange("p (t g h c) -> p t g h c", t=4, g=2, h=2)
                need(e, o_done, u)
                e.tensor_copy(OP[:], T2[:, :, :, 0, 0:hd + 1]).then_inc(op_done, 1)
                e.wait_ge(op_done, 2 * u + 1)
                e.tensor_tensor(OP[:], OP[:], T2[:, :, :, 1, 0:hd + 1], ALU.add).then_inc(op_done, 1)
                e.wait_ge(op_done, 2 * u + 2)
                e.reciprocal(RI[:, :, 0:G], OP[:, :, :, hd]).then_inc(ri_done, 1)
                e.wait_ge(ri_done, u + 1)
                for g in range(2):
                    mm = e.tensor_tensor(o_at(u, r, g), OP[:, :, g, 0:hd],
                                         RI[:, :, g:g + 1].broadcast_to([P, 4, hd]), ALU.mult)
                mm.then_inc(o_done, 1)
        if G == 2:
            OP = ph.sb("OP", [P, 4, 2, hd + 1])
            op_done = ph.sem("op_done")

        def run(e, emit):
            rounds = (NU - 8) // UNROLL
            for u in range(-2, 3):
                emit(u, u)
            with e.Fori(0, rounds) as i:
                for c in range(3, 3 + UNROLL):
                    emit(UNROLL * i + c, c)
            for u in range(3 + UNROLL * rounds, NU + 1):
                emit(u, u)

        with nc.Block() as block:
            @block.sync
            def _(e):
                e.dma_start(mask[:], core.arrays[f"mask{G}"]).then_inc(mask_in, 16)
                core.load_raw(e, next_raw)

                def emit(i, r):
                    u = 4 * i + r
                    need(e, st_ready, (u - 3) * (2 * NS))
                    e.sem_inc(seen_free, 1)
                    for n, part in enumerate((0, 0, 1)):
                        e.dma_start(QA[32 * n:32 * n + 32, r, :].bitcast(F32),
                                    q[part][32 * r:32 * r + 32, bass.ds(i, 1), :].bitcast(F32)
                                    ).then_inc(q_in[r], 16)
                    need(e, ka_ready, (u - 1) * G)
                    e.sem_inc(seen_free, 1)
                    for n, part in enumerate((0, 1, 0)):
                        e.dma_start(KR[32 * n:32 * n + 32, r % 2, :],
                                    k[part][32 * r:32 * r + 32, bass.ds(i, 1), :].bitcast(F32)).then_inc(k_in[r % 2], 16)
                for r in range(4):
                    emit(0, r)
                with e.Fori(1, 8) as i:
                    for r in range(4):
                        emit(i, r)

            @block.gpsimd
            def _(e):
                e.wait_ge(mask_in, 16)
                e.wait_ge(zeroed, 1)

                def emit(i, r):
                    u = 4 * i + r
                    e.wait_ge(k_in[r % 2], 96 * i + 48 * (r // 2 + 1))
                    need(e, st_ready, (u - 3) * (2 * NS))
                    for g in range(G):
                        e.tensor_tensor(KA[:, r, g, :], KR[:, r % 2, :], mask[:, g:g + 1].broadcast_to([P, S]),
                                        ALU.mult).then_inc(ka_ready, 1)
                    need(e, pv_step, (u - 3) * NS)
                    if G == 4:
                        e.tensor_copy(VA[:, r, :, 0:hd], V[:, bass.ds(i, 1), :, r * hd:(r + 1) * hd]
                                      ).then_inc(va_ready, 1)
                    else:
                        for g in range(G):
                            mm = e.tensor_copy(VA[:, r, :, 32 * g:32 * g + hd],
                                               V[:, bass.ds(i, 1), :, (2 * r + g) * hd:(2 * r + g + 1) * hd])
                        mm.then_inc(va_ready, 1)
                for r in range(4):
                    emit(0, r)
                if residual_bias:
                    e.wait_ge(core.bias_loaded, bias_n)
                    e.wait_ge(core.x_loaded, 16)
                    e.tensor_tensor(core.X[:], core.X[:], core.bias[:].unsqueeze(1).broadcast_to([P, NT, D]),
                                    ALU.add).then_inc(bias_done, 1)
                with e.Fori(1, 8) as i:
                    for r in range(4):
                        emit(i, r)
                if residual_bias:
                    e.wait_ge(bias_done, 1)

            @block.scalar
            def _(e):
                def emit(u, c):
                    for s in range(NS):
                        act_exp(e, u, s)
                        if s == 0:
                            act_ot(e, u - 1, (c - 1) % 4)
                run(e, emit)

            @block.vector
            def _(e):
                e.memset(QA[ROWS_M:P, :, :].bitcast(F32), 0.0).then_inc(zero_v, 1)
                e.memset(KR[ROWS_M:P, :, :], 1.0).then_inc(zero_v, 1)
                e.memset(VA[:], 0.0).then_inc(zero_v, 1)
                e.wait_ge(zero_v, 3)
                ones = VA[:, :, :, hd:hd + 1] if G == 4 else \
                    VA[:].rearrange("p r t (g c) -> p r t g c", g=2)[:, :, :, :, hd:hd + 1]
                e.memset(ones, 1.0).then_inc(zeroed, 1)

                def emit(u, c):
                    for kind, du, n in ring_order:
                        if kind == "max":
                            dve_max(e, u + du, c + du, n // 4, [n % 4])
                        elif kind == "mt":
                            dve_mrow(e, u + du, c + du)
                        else:
                            dve_out(e, u + du, c + du)
                run(e, emit)
                e.wait_ge(o_done, NU)

            @block.tensor
            def _(e):
                e.wait_ge(zeroed, 1)

                def emit(u, c):
                    r, rp = c % 4, (c - 1) % 4
                    for s in range(NS - 1):
                        for x in (STEP if G == 4 else STEP2).split():
                            if x[0] == "M":
                                pe_max(e, u + 1, c + 1, s + 1, [int(x[1])])
                            elif x[0] == "S":
                                pe_scores(e, u, r, s, int(x[1]))
                            elif s == 0:
                                pe_pv(e, u - 1, rp, NS - 1)
                            else:
                                pe_pv(e, u, r, s - 1)
                    for x in (LAST if G == 4 else LAST2).split():
                        if x == "MT":
                            pe_mt(e, u + 1, c + 1)
                        elif x == "TO":
                            pe_to(e, u - 1, c - 1)
                        elif x == "P":
                            pe_pv(e, u, r, NS - 2)
                        elif x[0] == "M":
                            pe_max(e, u + 2, c + 2, 0, [int(x[1])])
                        else:
                            pe_scores(e, u, r, NS - 1, int(x[1]))
                run(e, emit)


def output_phase(core, tag, o_tile, next_raw, next_bias=None, absum=None):
    nc = core.nc
    with Phase(core, tag) as ph:
        w = [ph.sb("w_hi", [P, KD * D], F32R), ph.sb("w_lo", [P, KD * D], F32R)]
        wv = [x[:].rearrange("p (k c) -> p k c", k=KD) for x in w]
        act_split, dve_split, w_ready, n_split = split_on(ph, w[0], w[1], KD * D)
        OT = [ph.sb("OT_hi", [P, 2, D], F32R), ph.sb("OT_lo", [P, 2, D], F32R)]
        TP = ph.ps("TP", [P, 2, 512])
        tail = Tail(ph)
        raw_before = core.n_raw
        junk = ph.sb("junk", [P, 2048]) if absum is not None else None
        abs_done = ph.sem("abs_done")
        tp_ready = ph.sem("tp_ready")
        ot_hi = ph.sem("ot_hi")
        ot_lo = ph.sem("ot_lo")
        with nc.Block() as block:
            @block.sync
            def _(e):
                e.wait_ge(w_ready, n_split)
                core.load_raw(e, next_raw)
                if next_bias:
                    core.load_bias(e, next_bias)

            @block.gpsimd
            def _(e):
                tail.pool_steps()

            @block.tensor
            def _(e):
                for i in range(NT + 3):
                    if i < NT:
                        need(e, ot_lo, i - 1)
                        for k in range(KD):
                            mm = e.transpose(TP[:, i % 2, k * P:(k + 1) * P], o_tile(i, k), core.ident[:])
                        mm.then_inc(tp_ready, 1)
                    t = i - 1
                    if 0 <= t < NT:
                        if t == 0:
                            e.wait_ge(w_ready, n_split)
                        e.wait_ge(ot_lo, t + 1)
                        need(e, tail.summed, t - 1)
                        for k in range(KD):
                            for j, (oi, wi) in enumerate(HI_LO):
                                mm = e.matmul(tail.y[:, t % 2, 0:D], OT[oi][:, t % 2, k * P:(k + 1) * P],
                                              wv[wi][:, k, :], start=(k == 0 and j == 0),
                                              stop=(k == KD - 1 and j == 2))
                        mm.then_inc(tail.y_ready, 1)
                    if 0 <= i - 3 < NT:
                        tail.pe_transpose(i - 3)

            @block.scalar
            def _(e):
                act_split()
                for i in range(NT + 3):
                    if i < NT:
                        e.wait_ge(tp_ready, i + 1)
                        need(e, tail.y_ready, i - 1)
                        e.activation(OT[0][:, i % 2], TP[:, i % 2, 0:D], ACT.Copy).then_inc(ot_hi, 1)
                    m = i - NT
                    if absum is not None and m >= 0:
                        e.wait_ge(core.raw_loaded, raw_before + 48)
                        need(e, abs_done, m)
                        e.activation(junk[:], core.raw[:, 2048 * m:2048 * (m + 1)], ACT.Abs,
                                     accum_out=absum[:, m:m + 1]).then_inc(abs_done, 1)
                    if 0 <= i - 3 < NT:
                        tail.act_xt(i - 3)

            @block.vector
            def _(e):
                dve_split()
                for i in range(NT + 3):
                    if i < NT:
                        e.wait_ge(ot_hi, i + 1)
                        e.tensor_tensor(OT[1][:, i % 2], TP[:, i % 2, 0:D], OT[0][:, i % 2].bitcast(F32),
                                        ALU.subtract).then_inc(ot_lo, 1)
                    if 0 <= i - 1 < NT:
                        tail.dve_stats(i - 1)
                    if 0 <= i - 2 < NT:
                        tail.dve_norm(i - 2)


def feed_forward_phase(core, tag, inter, next_raw, next_bias=None, absum=None):
    nc = core.nc
    ternary = absum is not None
    M = [min(P, inter - a) for a in range(0, inter, P)]
    NM = len(M)
    cols = 2 * KD * inter + NM * D
    with Phase(core, tag) as ph:
        w = [ph.sb("w_hi", [P, cols], F32R)] + ([] if ternary else [ph.sb("w_lo", [P, cols], F32R)])
        parts_wx = [(wi, xi) for wi, xi in HI_LO if wi < len(w)]
        parts_hw = [(hi, wi) for hi, wi in HI_LO if wi < len(w)]
        up = [x[:, 0:2 * KD * inter].rearrange("p (s k c) -> p s k c", s=2, k=KD) for x in w]
        down = [x[:, 2 * KD * inter:cols].rearrange("p (m c) -> p m c", m=NM) for x in w]
        if ternary:
            scale = ph.sb("scale", [P, 4])
            prepare_ternary(core, tag, w[0], scale, absum)
        else:
            act_split, dve_split, w_ready, n_split = split_on(ph, w[0], w[1], cols)
        H = [ph.sb("H_hi", [P, 2, NM, S], F32R), ph.sb("H_lo", [P, 2, NM, S], F32R)]
        SU = ph.sb("SU", [P, 2, S])
        HF = ph.sb("HF", [P, 2, S])
        UG = ph.ps("UG", [P, 2, 2, S])
        tail = Tail(ph, y_scale=scale[:, 3:4] if ternary else None)
        up_ready = ph.sem("up_ready")
        gate_ready = ph.sem("gate_ready")
        silu_done = ph.sem("silu_done")
        h_done = ph.sem("h_done")
        h_hi = ph.sem("h_hi")
        h_lo = ph.sem("h_lo")

        def tail_steps(c):
            return range(c * TPB, (c + 1) * TPB + (2 if c == B - 1 else 0))

        with nc.Block() as block:
            @block.sync
            def _(e):
                if not ternary:
                    e.wait_ge(w_ready, n_split)
                core.load_raw(e, next_raw)
                if next_bias:
                    core.load_bias(e, next_bias)

            @block.gpsimd
            def _(e):
                tail.pool_steps()

            @block.tensor
            def _(e):
                def ups(c):
                    for m, rows in enumerate(M):
                        n = c * NM + m
                        for side, (free, ready) in enumerate(((silu_done, up_ready), (h_done, gate_ready))):
                            need(e, free, n - 1)
                            if not ternary and n == 0:
                                e.wait_ge(w_ready, -(-(side + 1) * KD * inter // 1024))
                            for k in range(KD):
                                for j, (wi, xi) in enumerate(parts_wx):
                                    mm = e.matmul(UG[0:rows, n % 2, side, :], up[wi][:, side, k, m * P:m * P + rows],
                                                  core.XT[xi][:, k, c * S:(c + 1) * S],
                                                  start=(k == 0 and j == 0),
                                                  stop=(k == KD - 1 and j == len(parts_wx) - 1))
                            mm.then_inc(ready, 1)

                def downs(c):
                    e.wait_ge(h_lo, (c + 1) * NM)
                    if not ternary and c == 0:
                        e.wait_ge(w_ready, n_split)
                    for t in tail_steps(c):
                        if t < NT:
                            need(e, tail.summed, t - 1)
                            a = (t % TPB) * P
                            for m, rows in enumerate(M):
                                for j, (hi, wi) in enumerate(parts_hw):
                                    mm = e.matmul(tail.y[:, t % 2, 0:D], H[hi][0:rows, c % 2, m, a:a + P],
                                                  down[wi][0:rows, m, :],
                                                  start=(m == 0 and j == 0),
                                                  stop=(m == NM - 1 and j == len(parts_hw) - 1))
                            mm.then_inc(tail.y_ready, 1)
                        if t >= 2:
                            tail.pe_transpose(t - 2)
                ups(0)
                for c in range(B):
                    if c + 1 < B:
                        ups(c + 1)
                    downs(c)

            @block.scalar
            def _(e):
                def hidden(c):
                    for m in range(NM + 1):
                        n = c * NM + m
                        if m < NM:
                            rows = M[m]
                            e.wait_ge(up_ready, n + 1)
                            need(e, h_done, n - 1)
                            e.activation(SU[0:rows, n % 2], UG[0:rows, n % 2, 0, :], ACT.Silu,
                                         scale=scale[0:rows, 0:1] if ternary else 1.0).then_inc(silu_done, 1)
                        if m >= 1:
                            rows = M[m - 1]
                            e.wait_ge(h_done, n)
                            if m == 1 and c >= 2:
                                e.wait_ge(tail.y_ready, (c - 1) * TPB)
                            e.activation(H[0][0:rows, c % 2, m - 1], HF[0:rows, (n - 1) % 2], ACT.Copy).then_inc(h_hi, 1)
                if not ternary:
                    act_split()
                hidden(0)
                for c in range(B):
                    if c + 1 < B:
                        hidden(c + 1)
                    for t in tail_steps(c):
                        if t >= 2:
                            tail.act_xt(t - 2)

            @block.vector
            def _(e):
                def hidden(c):
                    for m in range(NM + 1):
                        n = c * NM + m
                        if m < NM:
                            rows = M[m]
                            e.wait_ge(gate_ready, n + 1)
                            e.wait_ge(silu_done, n + 1)
                            need(e, h_lo, n - 1)
                            need(e, h_hi, n - 1)
                            e.tensor_tensor(HF[0:rows, n % 2], UG[0:rows, n % 2, 1, :], SU[0:rows, n % 2],
                                            ALU.mult).then_inc(h_done, 1)
                        if m >= 1:
                            rows = M[m - 1]
                            e.wait_ge(h_hi, n)
                            e.wait_ge(h_done, n)
                            e.tensor_tensor(H[1][0:rows, c % 2, m - 1], HF[0:rows, (n - 1) % 2],
                                            H[0][0:rows, c % 2, m - 1].bitcast(F32), ALU.subtract).then_inc(h_lo, 1)
                if not ternary:
                    dve_split()
                hidden(0)
                for c in range(B):
                    if c + 1 < B:
                        hidden(c + 1)
                    for t in tail_steps(c):
                        if t < NT:
                            tail.dve_stats(t)
                        if 1 <= t and t - 1 < NT:
                            tail.dve_norm(t - 1)


def prepare_ternary(core, tag, signs, scale, absum):
    nc = core.nc
    parts = [(0, 2048), (2048, 4096), (4096, 6144)]
    CH = 1024
    with Phase(core, tag + "t") as ph:
        ones = ph.sb("ones", [P, P])
        half = ph.sb("half", [P, 2, 3])
        below = ph.sb("below", [P, 2, CH])
        total = ph.ps("total", [P, 3])
        sem = {x: ph.sem(x) for x in ("ones_set", "total_ready", "scaled", "below_done", "signs_done")}
        pieces = [(m, a) for m, (lo, hi) in enumerate(parts) for a in range(lo, hi, CH)]
        with nc.Block() as block:
            @block.tensor
            def _(e):
                e.wait_ge(sem["ones_set"], 1)
                e.matmul(total[:], ones[:], absum[:], start=True, stop=True).then_inc(sem["total_ready"], 1)

            @block.vector
            def _(e):
                e.memset(ones[:], 1.0).then_inc(sem["ones_set"], 1)
                e.wait_ge(sem["total_ready"], 1)
                e.tensor_scalar(scale[:, 0:3], total[:], 1.0 / (D * 1024), 1e-8, ALU.mult, ALU.add
                                ).then_inc(sem["scaled"], 1)
                e.wait_ge(sem["scaled"], 1)
                e.tensor_scalar(half[:, 0, :], scale[:, 0:3], 0.5, None, ALU.mult).then_inc(sem["scaled"], 1)
                e.tensor_scalar(half[:, 1, :], scale[:, 0:3], -0.5, None, ALU.mult).then_inc(sem["scaled"], 1)
                e.tensor_tensor(scale[:, 3:4], scale[:, 1:2], scale[:, 2:3], ALU.mult).then_inc(sem["scaled"], 1)
                e.wait_ge(sem["scaled"], 4)
                for n in range(len(pieces) + 1):
                    if n < len(pieces):
                        m, a = pieces[n]
                        need(e, sem["signs_done"], n - 1)
                        e.tensor_scalar(below[:, n % 2], core.raw[:, a:a + CH], half[:, 1, m:m + 1], None,
                                        ALU.is_lt).then_inc(sem["below_done"], 1)
                    if n >= 1:
                        m, a = pieces[n - 1]
                        e.wait_ge(sem["below_done"], n)
                        e.scalar_tensor_tensor(out=signs[:, a:a + CH], in0=core.raw[:, a:a + CH],
                                               scalar=half[:, 0, m:m + 1], in1=below[:, (n - 1) % 2],
                                               op0=ALU.is_gt, op1=ALU.subtract).then_inc(sem["signs_done"], 1)
                e.wait_ge(sem["signs_done"], len(pieces))


def wide_attention_phase(core, tag, q, k, v, O, scale, next_raw):
    nc = core.nc
    with Phase(core, tag) as ph:
        SP = ph.ps("scores", [P, 3, S])
        TP = ph.ps("TP", [P, 2, S])
        CP = ph.ps("context", [P, 2, S])
        PR = core.lend(f"{tag}_probs", [P, 3, S], F32, 0)
        PT = [core.lend(f"{tag}_PT_{n}", [P, 2, TPB, P], F32R, 6144 + 4096 * i) for i, n in enumerate(("hi", "lo"))]
        mx = ph.sb("mx", [P, 3, 1])
        nm = ph.sb("nm", [P, 3, 1])
        rs = ph.sb("rs", [P, 3, 1])
        ri = ph.sb("ri", [P, 3, 1])
        s_ready = ph.sem("s_ready")
        mx_done = ph.sem("mx_done")
        nm_done = ph.sem("nm_done")
        exp_done = ph.sem("exp_done")
        ri_done = ph.sem("ri_done")
        p_done = ph.sem("p_done")
        tp_ready = ph.sem("tp_ready")
        pt_hi = ph.sem("pt_hi")
        pt_lo = ph.sem("pt_lo")
        c_ready = ph.sem("c_ready")
        c_done = ph.sem("c_done")
        bias_done = ph.sem("bias_done")
        bias_n = core.n_bias
        with nc.Block() as block:
            @block.sync
            def _(e):
                core.load_raw(e, next_raw)

            @block.gpsimd
            def _(e):
                e.wait_ge(core.bias_loaded, bias_n)
                e.tensor_tensor(core.X[:], core.X[:], core.bias[:].unsqueeze(1).broadcast_to([P, NT, D]),
                                ALU.add).then_inc(bias_done, 1)
                e.wait_ge(bias_done, 1)

            @block.tensor
            def _(e):
                for i in range(NT + 3):
                    if i < NT:
                        b, qt = divmod(i, TPB)
                        need(e, exp_done, i - 2)
                        for h in range(KD):
                            for j, (qi, ki) in enumerate(HI_LO):
                                mm = e.matmul(SP[:, i % 3, :], q[qi][:, 2 * b + h, qt * P:(qt + 1) * P],
                                              k[ki][:, 2 * b + h, :], start=(h == 0 and j == 0),
                                              stop=(h == KD - 1 and j == 2))
                        mm.then_inc(s_ready, 1)
                    t = i - 2
                    if 0 <= t < NT:
                        e.wait_ge(p_done, t + 1)
                        need(e, pt_lo, t - 1)
                        for kt in range(TPB):
                            mm = e.transpose(TP[:, t % 2, kt * P:(kt + 1) * P], PR[:, t % 3, kt * P:(kt + 1) * P],
                                             core.ident[:])
                        mm.then_inc(tp_ready, 1)
                    t = i - 3
                    if 0 <= t < NT:
                        b = t // TPB
                        e.wait_ge(pt_lo, t + 1)
                        need(e, c_done, t - 1)
                        for kt in range(TPB):
                            for j, (pi, vi) in enumerate(HI_LO):
                                mm = e.matmul(CP[:, t % 2, 0:D], PT[pi][:, t % 2, kt, :], v[vi][:, b * TPB + kt, :],
                                              start=(kt == 0 and j == 0), stop=(kt == TPB - 1 and j == 2))
                        mm.then_inc(c_ready, 1)

            @block.scalar
            def _(e):
                for i in range(NT + 3):
                    if i < NT:
                        e.wait_ge(nm_done, i + 1)
                        need(e, tp_ready, i - 2)
                        e.activation(PR[:, i % 3, :], SP[:, i % 3, :], ACT.Exp, bias=nm[:, i % 3], scale=scale,
                                     accum_out=rs[:, i % 3]).then_inc(exp_done, 1)
                    t = i - 2
                    if 0 <= t < NT:
                        e.wait_ge(tp_ready, t + 1)
                        need(e, c_ready, t - 1)
                        e.activation(PT[0][:, t % 2], TP[:, t % 2, :].rearrange("p (t n) -> p t n", t=TPB),
                                     ACT.Copy).then_inc(pt_hi, 1)
                    t = i - 3
                    if 0 <= t < NT:
                        e.wait_ge(c_ready, t + 1)
                        e.activation(O[:, t, :], CP[:, t % 2, 0:D], ACT.Copy).then_inc(c_done, 1)

            @block.vector
            def _(e):
                for i in range(NT + 3):
                    if i < NT:
                        e.wait_ge(s_ready, i + 1)
                        need(e, nm_done, i - 2)
                        e.tensor_reduce(mx[:, i % 3], SP[:, i % 3, :], AXX, ALU.max).then_inc(mx_done, 1)
                        e.wait_ge(mx_done, i + 1)
                        need(e, exp_done, i - 2)
                        e.tensor_scalar(nm[:, i % 3], mx[:, i % 3], -scale, None, ALU.mult).then_inc(nm_done, 1)
                    t = i - 1
                    if 0 <= t < NT:
                        e.wait_ge(exp_done, t + 1)
                        need(e, p_done, t - 2)
                        e.reciprocal(ri[:, t % 3], rs[:, t % 3]).then_inc(ri_done, 1)
                        e.wait_ge(ri_done, t + 1)
                        e.tensor_scalar(PR[:, t % 3, :], PR[:, t % 3, :], ri[:, t % 3], None,
                                        ALU.mult).then_inc(p_done, 1)
                    t = i - 2
                    if 0 <= t < NT:
                        e.wait_ge(pt_hi, t + 1)
                        e.tensor_tensor(PT[1][:, t % 2], TP[:, t % 2, :].rearrange("p (t n) -> p t n", t=TPB),
                                        PT[0][:, t % 2].bitcast(F32), ALU.subtract).then_inc(pt_lo, 1)
                e.wait_ge(pt_lo, NT)


def routing(ph, LGT, LG, comb, n_exp, n_top):
    core = ph.core
    n_s = 8 - n_top
    W = n_exp + n_s
    n_w = KD * n_exp
    w = [ph.sb("rw_hi", [P, n_w], F32R), ph.sb("rw_lo", [P, n_w], F32R)]
    wv = [x[:].rearrange("p (k c) -> p k c", k=KD) for x in w]
    act_split, dve_split, w_ready, n_split = split_on(ph, w[0], w[1], n_w, name="r")
    lgt = ph.sb("lgt", [n_exp, B * S])
    lgt_ready = ph.sem("lgt_ready")
    lgt_done = ph.sem("lgt_done")
    mx = ph.sb("mx", [P, NT])
    ex = ph.sb("ex", [P, NT, n_exp])
    sm = ph.sb("sm", [P, NT])
    probs = ph.sb("probs", [P, NT, W])
    top8 = ph.sb("top8", [P, NT, 8])
    vals = ph.sb("vals", [P, NT, 8])
    rest = ph.sb("rest", [P, NT, W])
    ws = ph.sb("ws", [P, NT])
    lg_ready = ph.sem("lg_ready")
    ex_in = ph.sem("ex_in")
    ex_done = ph.sem("ex_done")
    dv = ph.sem("dv")

    def pe():
        e = core.nc.tensor
        e.wait_ge(w_ready, n_split)
        for ch in range(B):
            need(e, lgt_done, ch - 1)
            for k in range(KD):
                for j, (wi, xi) in enumerate(HI_LO):
                    mm = e.matmul(LGT[0:n_exp, ch % 2, :], wv[wi][:, k, :], core.XT[xi][:, k, ch * S:(ch + 1) * S],
                                  start=(k == 0 and j == 0), stop=(k == KD - 1 and j == 2))
            mm.then_inc(lgt_ready, 1)
        e.wait_ge(lgt_done, B)
        for t in range(NT):
            mm = e.transpose(LG[:, t, :], lgt[:, t * P:(t + 1) * P], core.ident[0:n_exp, 0:n_exp])
        mm.then_inc(lg_ready, 1)

    def act_copies():
        e = core.nc.scalar
        for ch in range(B):
            e.wait_ge(lgt_ready, ch + 1)
            e.activation(lgt[:, ch * S:(ch + 1) * S], LGT[0:n_exp, ch % 2, :], ACT.Copy).then_inc(lgt_done, 1)

    def act_exp():
        e = core.nc.scalar
        e.wait_ge(ex_in, 1)
        e.activation(ex[:], ex[:], ACT.Exp).then_inc(ex_done, 1)

    def dve_first():
        e = core.nc.vector
        dve_split()
        for j in range(n_s):
            e.memset(probs[:, :, n_exp + j:n_exp + j + 1], -1.0 - j).then_inc(dv, 1)
            e.memset(vals[:, :, n_top + j:n_top + j + 1], -1.0 - j).then_inc(dv, 1)

    def dve_rest():
        e = core.nc.vector
        c = 2 * n_s
        e.wait_ge(lg_ready, 1)
        e.tensor_reduce(mx[:], LG[:], AXX, ALU.max).then_inc(dv, 1)
        c += 1
        e.wait_ge(dv, c)
        e.tensor_tensor(ex[:], LG[:], mx[:].unsqueeze(2).broadcast_to([P, NT, n_exp]),
                        ALU.subtract).then_inc(ex_in, 1)
        e.wait_ge(ex_done, 1)
        e.tensor_reduce(sm[:], ex[:], AXX, ALU.add).then_inc(dv, 1)
        c += 1
        e.wait_ge(dv, c)
        e.reciprocal(ws[:], sm[:]).then_inc(dv, 1)
        c += 1
        e.wait_ge(dv, c)
        e.tensor_tensor(probs[:, :, 0:n_exp], ex[:], ws[:].unsqueeze(2).broadcast_to([P, NT, n_exp]),
                        ALU.mult).then_inc(dv, 1)
        c += 1
        e.wait_ge(dv, c)
        for t in range(NT):
            e.max(top8[:, t, :], probs[:, t, 0:n_exp]).then_inc(dv, 1)
        c += NT
        e.wait_ge(dv, c)
        e.tensor_copy(vals[:, :, 0:n_top], top8[:, :, 0:n_top]).then_inc(dv, 1)
        e.tensor_reduce(sm[:], top8[:, :, 0:n_top], AXX, ALU.add).then_inc(dv, 1)
        c += 2
        e.wait_ge(dv, c)
        for t in range(NT):
            e.match_replace(out=rest[:, t, :], in_to_replace=vals[:, t, :], in_values=probs[:, t, :],
                            imm_value=0.0).then_inc(dv, 1)
        e.reciprocal(ws[:], sm[:]).then_inc(dv, 1)
        c += NT + 1
        e.wait_ge(dv, c)
        e.tensor_tensor(ex[:], probs[:, :, 0:n_exp], rest[:, :, 0:n_exp], ALU.subtract).then_inc(dv, 1)
        c += 1
        e.wait_ge(dv, c)
        e.tensor_tensor(comb, ex[:], ws[:].unsqueeze(2).broadcast_to([P, NT, n_exp]),
                        ALU.mult).then_inc(dv, 1)
        c += 1
        e.wait_ge(dv, c)

    return pe, act_split, act_copies, act_exp, dve_first, dve_rest, ex_in


def experts_phase(core, tag, n_exp, n_top, inter, next_raw, table, indices, looked_up):
    nc = core.nc
    N_LUT = 16
    LK_COLS = sum(cols for _, cols in indices)
    LK_W = LK_COLS // (n_exp * B // 2)
    assert LK_W * n_exp * B // 2 == LK_COLS
    NM = inter // P
    GU, DN = KD * 2 * inter, NM * D
    NG = n_exp * B
    with Phase(core, tag) as ph:
        rawe = ph.sb("rawe", [P, GU + DN])
        w = [ph.sb("w_hi", [P, 2, GU + DN], F32R), ph.sb("w_lo", [P, 2, GU + DN], F32R)]
        up = [x[:, :, 0:GU].rearrange("p e (k c) -> p e k c", k=KD) for x in w]
        down = [x[:, :, GU:GU + DN].rearrange("p e (m c) -> p e m c", m=NM) for x in w]
        H = [ph.sb("H_hi", [P, 2, NM, S], F32R), ph.sb("H_lo", [P, 2, NM, S], F32R)]
        SU = ph.sb("SU", [P, 2, S])
        HF = ph.sb("HF", [P, 2, S])
        lut = ph.sb("lut", [P, N_LUT])
        LK = ph.sb("looked_up", [P, LK_COLS])
        idx = ph.sb("idx", [P, LK_W])
        term = ph.sb("term", [P, 2, LK_W])
        total = ph.sb("total", [P, LK_W])
        lk_in = ph.sem("lk_in")
        lk = ph.sem("lk")
        lk_out = ph.sem("lk_out")
        UG = ph.ps("UG", [P, 2, 2, S])
        Y = ph.ps("Y", [P, TPB, S])
        comb = ph.sb("comb", [P, n_exp, NT])
        LG = Y[:, TPB - 1, 0:NT * n_exp].rearrange("p (t e) -> p t e", t=NT)
        (route_pe, route_act_split, route_act_copies, route_act_exp, route_dve_first, route_dve_rest,
         logits_read) = routing(ph, Y[:, 0:2, :], LG, comb[:].rearrange("p e t -> p t e"), n_exp, n_top)
        act_split, dve_split, w_ready, n_split = split_on(ph, w[0][:, 0, :], w[1][:, 0, :], GU + DN, at=KD * n_exp)
        rawe_in = ph.sem("rawe_in")
        rawe_free = ph.sem("rawe_free")
        whole = ph.sem("whole")
        up_ready = ph.sem("up_ready")
        gate_ready = ph.sem("gate_ready")
        silu_done = ph.sem("silu_done")
        h_done = ph.sem("h_done")
        h_hi = ph.sem("h_hi")
        h_lo = ph.sem("h_lo")
        y_ready = ph.sem("y_ready")
        added = ph.sem("added")
        src_gu, src_dn = core.arrays[tag + "_gu"], core.arrays[tag + "_dn"]

        def run(e, emit, at_first=None):
            for g in range(3):
                emit(g, g % 8)
            loops = (NG - 1 - 3) // 8
            with e.Fori(0, loops) as i:
                for c in range(3, 11):
                    emit(8 * i + c, c % 8)
            for g in range(3 + 8 * loops, NG):
                emit(g, g % 8)

        with nc.Block() as block:
            @block.sync
            def _(e):
                def load(x):
                    e.dma_start(rawe[:, 0:GU], src_gu[bass.ds(x, 1), :, :].rearrange("e p c -> (e p) c")).then_inc(rawe_in, 16)
                    e.dma_start(rawe[:, GU:GU + DN], src_dn[bass.ds(x, 1), :, :].rearrange("e p c -> (e p) c")).then_inc(rawe_in, 16)
                load(1)
                e.dma_start(lut[:], core.arrays[table].partition_broadcast(P)).then_inc(lk_in, 16)
                at = 0
                for name, cols in indices:
                    e.dma_start(LK[:, at:at + cols].bitcast(I32), core.arrays[name]).then_inc(lk_in, 16)
                    at += cols
                e.wait_ge(w_ready, n_split)
                core.load_raw(e, next_raw)
                for x in range(2, n_exp):
                    e.wait_ge(rawe_free, x - 1)
                    load(x)
                first = NG - 4
                split = first // 2 * LK_W
                e.wait_ge(lk, N_LUT * first)
                e.dma_start(core.arrays[looked_up][:, 0:split], LK[:, 0:split]).then_inc(lk_out, 16)
                e.wait_ge(lk_out, 16)
                e.wait_ge(lk, N_LUT * NG)
                e.dma_start(core.arrays[looked_up][:, split:], LK[:, split:]).then_inc(lk_out, 16)
                e.wait_ge(lk_out, 32)

            @block.gpsimd
            def _(e):
                for x in range(1, n_exp):
                    e.wait_ge(rawe_in, 32 * x)
                    need(e, y_ready, NT * (x - 1))
                    e.tensor_copy(w[0][:, x % 2, :], rawe[:]).then_inc(whole, 1)
                    e.wait_ge(whole, x)
                    e.tensor_tensor(w[1][:, x % 2, :], rawe[:], w[0][:, x % 2, :].bitcast(F32),
                                    ALU.subtract).then_inc(rawe_free, 1)

            @block.tensor
            def _(e):
                def ups(g, c):
                    x, ch = (c // 4) % 2, c % 4
                    if ch == 0:
                        if isinstance(g, int) and g == 0:
                            e.wait_ge(w_ready, n_split)
                        else:
                            e.wait_ge(rawe_free, (g - c) // 4 + c // 4)
                    for m in range(NM):
                        n = NM * g + m
                        for side, (free, ready) in enumerate(((silu_done, up_ready), (h_done, gate_ready))):
                            need(e, free, n - 1)
                            for k in range(KD):
                                for j, (wi, xi) in enumerate(HI_LO):
                                    a = side * inter + m * P
                                    mm = e.matmul(UG[:, m % 2, side, :], up[wi][:, x, k, a:a + P],
                                                  core.XT[xi][:, k, ch * S:(ch + 1) * S],
                                                  start=(k == 0 and j == 0), stop=(k == KD - 1 and j == 2))
                            mm.then_inc(ready, 1)

                def downs(g, c):
                    x, ch = (c // 4) % 2, c % 4
                    e.wait_ge(h_lo, NM * g + NM)
                    if isinstance(g, int) and g == 0:
                        e.wait_ge(logits_read, 1)
                    for tt in range(TPB):
                        need(e, added, TPB * g + (tt - 3))
                        for m in range(NM):
                            for j, (hi, wi) in enumerate(HI_LO):
                                mm = e.matmul(Y[:, tt, 0:D], H[hi][:, c % 2, m, tt * P:(tt + 1) * P],
                                              down[wi][:, x, m, :], start=(m == 0 and j == 0),
                                              stop=(m == NM - 1 and j == 2))
                        mm.then_inc(y_ready, 1)

                def emit(g, c):
                    if not isinstance(g, int) or g + 1 < NG:
                        ups(g + 1, (c + 1) % 8)
                    downs(g, c)
                route_pe()
                ups(0, 0)
                run(e, emit)

            @block.scalar
            def _(e):
                def hidden(g, c):
                    for m in range(NM + 1):
                        n = NM * g + m
                        if m < NM:
                            e.wait_ge(up_ready, n + 1)
                            need(e, h_done, n - 1)
                            e.activation(SU[:, m % 2], UG[:, m % 2, 0, :], ACT.Silu).then_inc(silu_done, 1)
                        if m >= 1:
                            e.wait_ge(h_done, n)
                            if m == 1:
                                need(e, y_ready, TPB * (g - 1))
                            e.activation(H[0][:, c % 2, m - 1], HF[:, (m - 1) % 2], ACT.Copy).then_inc(h_hi, 1)

                def emit(g, c):
                    if not isinstance(g, int) or g + 1 < NG:
                        hidden(g + 1, (c + 1) % 8)
                route_act_split()
                act_split()
                route_act_copies()
                hidden(0, 0)
                route_act_exp()
                run(e, emit)

            @block.vector
            def _(e):
                def hidden(g, c):
                    for m in range(NM + 1):
                        n = NM * g + m
                        if m < NM:
                            e.wait_ge(gate_ready, n + 1)
                            e.wait_ge(silu_done, n + 1)
                            need(e, h_lo, n - 1)
                            need(e, h_hi, n - 1)
                            e.tensor_tensor(HF[:, m % 2], UG[:, m % 2, 1, :], SU[:, m % 2], ALU.mult).then_inc(h_done, 1)
                        if m >= 1:
                            e.wait_ge(h_hi, n)
                            e.tensor_tensor(H[1][:, c % 2, m - 1], HF[:, (m - 1) % 2],
                                            H[0][:, c % 2, m - 1].bitcast(F32), ALU.subtract).then_inc(h_lo, 1)
                        if m < NM and not (isinstance(g, int) and g == 0):
                            lookup(g - 1, (c - 1) % 8, m)

                def lookup(g, c, m):
                    j = 8 * (c % 2) + 2 * m
                    base = N_LUT * g + 4 * m
                    piece = LK[:, bass.ds(((g - c) // 2 + c // 2) * LK_W, LK_W)]
                    if j == 0:
                        need(e, lk, base)
                        e.tensor_copy(idx[:], piece.bitcast(I32)).then_inc(lk, 1)
                        e.wait_ge(lk, base + 1)
                        e.tensor_scalar(total[:], idx[:], 0.0, lut[:, 0:1], ALU.is_equal, ALU.mult).then_inc(lk, 1)
                        e.tensor_scalar(term[:, 1], idx[:], 1.0, lut[:, 1:2], ALU.is_equal, ALU.mult).then_inc(lk, 1)
                    else:
                        e.wait_ge(lk, base - 1)
                        e.tensor_scalar(term[:, 0], idx[:], float(j), lut[:, j:j + 1],
                                        ALU.is_equal, ALU.mult).then_inc(lk, 1)
                        e.wait_ge(lk, base)
                        e.tensor_scalar(term[:, 1], idx[:], float(j + 1), lut[:, j + 1:j + 2],
                                        ALU.is_equal, ALU.mult).then_inc(lk, 1)
                        e.wait_ge(lk, base + 1)
                        e.tensor_tensor(total[:], total[:], term[:, 0], ALU.add).then_inc(lk, 1)
                    e.wait_ge(lk, base + 3)
                    e.tensor_tensor(piece if j + 2 == N_LUT else total[:], total[:], term[:, 1],
                                    ALU.add).then_inc(lk, 1)

                def emit(g, c):
                    if not isinstance(g, int) or g + 1 < NG:
                        hidden(g + 1, (c + 1) % 8)
                    if isinstance(g, int) and g + 1 == NG:
                        for m in range(NM):
                            lookup(g, c, m)
                    ch = c % 4
                    x = (g - c) // 4 + c // 4
                    for tt in range(TPB):
                        t = ch * TPB + tt
                        e.wait_ge(y_ready, TPB * g + (tt + 1))
                        e.scalar_tensor_tensor(out=core.X[:, t], in0=Y[:, tt, 0:D],
                                               scalar=comb[:, bass.ds(x, 1), t:t + 1].rearrange("p a b -> p (a b)"),
                                               in1=core.X[:, t], op0=ALU.mult, op1=ALU.add).then_inc(added, 1)
                route_dve_first()
                dve_split()
                e.wait_ge(lk_in, 16 * (len(indices) + 1))
                hidden(0, 0)
                route_dve_rest()
                run(e, emit)
                e.wait_ge(added, NG * TPB)


def head_mixing_phase(core, tag, O, next_raw, next_bias):
    nc = core.nc
    H, HD = 16, 16
    scratch = nc.dram_tensor("l3_mixed", [B, H, S, HD], F32).ap()
    with Phase(core, tag) as ph:
        n_w = KD * 3 * D
        w = [ph.sb("w_hi", [P, n_w], F32R), ph.sb("w_lo", [P, n_w], F32R)]
        wv = [x[:].rearrange("p (k c) -> p k c", k=KD) for x in w]
        act_split, dve_split, w_ready, n_split = split_on(ph, w[0], w[1], n_w)
        bias = ph.sb("bias", [1, 3 * D])
        ones = ph.sb("ones", [1, P])
        trig = ph.sb("trig", [P, 2, TPB, 8])
        NB = 6
        RT = ph.sb("RT", [P, 2, 2, 2 * D])
        VV = ph.sb("VV", [P, NB, D])
        RO = ph.sb("RO", [P, 3, 2 * D])
        PRD = ph.sb("PRD", [P, 2, HD, H * H])
        AVP = ph.sb("AVP", [P, 2, H * HD * H])
        SC = ph.sb("SC", [P, NB, H, H])
        mx = ph.sb("mx", [P, 2, H])
        sm = ph.sb("sm", [P, 2, H])
        OO = ph.sb("OO", [P, 2, D])
        qk_ps = ph.ps("qk", [P, 2, 512])
        v_ps = ph.ps("v", [P, 2, 512])
        sc_ps = ph.ps("sc", [P, 2, 512])
        const_in = ph.sem("const_in")
        ones_set = ph.sem("ones_set")
        qk_ready = ph.sem("qk_ready")
        v_ready = ph.sem("v_ready")
        rt_done = ph.sem("rt_done")
        v_done = ph.sem("v_done")
        ro_done = ph.sem("ro_done")
        prd_done = ph.sem("prd_done")
        sc_ready = ph.sem("sc_ready")
        mx_done = ph.sem("mx_done")
        sub_done = ph.sem("sub_done")
        exp_done = ph.sem("exp_done")
        sm_done = ph.sem("sm_done")
        rc_done = ph.sem("rc_done")
        a_done = ph.sem("a_done")
        av_done = ph.sem("av_done")
        av_rest = ph.sem("av_rest")
        o_done = ph.sem("o_done")
        stored = [ph.sem(f"stored{i}") for i in range(2)]
        o_in = ph.sem("o_in")
        bias_done = ph.sem("bias_done")
        bias_n = core.n_bias

        def av_product(e, t, lo, hi):
            shape = [P, hi - lo, HD, H]
            a = SC[:, t % NB, lo:hi].unsqueeze(2).broadcast_to(shape)
            v = VV[:, t % NB].rearrange("p (t d) -> p d t", t=H).unsqueeze(1).broadcast_to(shape)
            out = AVP[:, t % 2].rearrange("p (h d t) -> p h d t", h=H, d=HD)[:, lo:hi]
            return e.tensor_tensor(out, a, v, ALU.mult)

        def pool_heads(t):
            return 15 if t < NT - 4 else 9
        with nc.Block() as block:
            @block.sync
            def _(e):
                e.dma_start(bias[:], core.arrays["l3_bqkv"]).then_inc(const_in, 16)
                e.dma_start(trig[:], core.arrays["trig"].rearrange("f (t p) c -> p f t c", p=P)).then_inc(const_in, 16)
                e.wait_ge(w_ready, n_split)
                core.load_raw(e, next_raw)
                for t in range(NT):
                    b, st = divmod(t, TPB)
                    e.wait_ge(o_done, t + 1)
                    e.dma_start(scratch[b, :, st * P:(st + 1) * P, :].rearrange("h s d -> s h d"),
                                OO[:, t % 2, :].rearrange("p (h d) -> p h d", h=H)).then_inc(stored[t % 2], 16)
                    if st == TPB - 1:
                        e.wait_ge(stored[0], 8 * (t + 1))
                        e.wait_ge(stored[1], 8 * (t + 1))
                        e.dma_start(O[:, b * TPB:(b + 1) * TPB, :],
                                    scratch[b].rearrange("h s d -> (h s d)").rearrange("(t p c) -> p t c", p=P, c=D)
                                    ).then_inc(o_in, 16)
                e.wait_ge(o_in, 16 * B)

            @block.tensor
            def _(e):
                e.wait_ge(w_ready, n_split)
                e.wait_ge(const_in, 32)
                e.wait_ge(ones_set, 1)
                for i in range(NT + 2):
                    t = i
                    for ps, lo, hi, free, ready in ((qk_ps, 0, 2 * D, rt_done, qk_ready),
                                                    (v_ps, 2 * D, 3 * D, v_done, v_ready)) if i < NT else ():
                        need(e, free, t - 1)
                        out = ps[:, t % 2, 0:hi - lo]
                        e.matmul(out, ones[:], bias[:, lo:hi], start=True, stop=False)
                        for k in range(KD):
                            for j, (xi, wi) in enumerate(HI_LO):
                                mm = e.matmul(out, core.XT[xi][:, k, t * P:(t + 1) * P], wv[wi][:, k, lo:hi],
                                              start=False, stop=(k == KD - 1 and j == 2))
                        mm.then_inc(ready, 1)

                    t = i - 2
                    if 0 <= t < NT:
                        e.wait_ge(prd_done, t + 1)
                        need(e, sub_done, t - 1)
                        for d in range(HD):
                            mm = e.matmul(sc_ps[:, t % 2, 0:H * H], core.ident[:], PRD[:, t % 2, d, :],
                                          start=(d == 0), stop=(d == HD - 1))
                        mm.then_inc(sc_ready, 1)

            @block.scalar
            def _(e):
                act_split()
                e.wait_ge(const_in, 32)
                for i in range(NT + 2):
                    if i < NT:
                        s, st = i % 2, i % TPB
                        e.wait_ge(qk_ready, i + 1)
                        need(e, ro_done, i - 1)
                        x = qk_ps[:, s, :].rearrange("p (g c r) -> p c g r", c=8, r=2)
                        for f in range(2):
                            r = RT[:, s, f, :].rearrange("p (g c r) -> p c g r", c=8, r=2)
                            for c in range(8):
                                mm = e.activation(r[:, c], x[:, c], ACT.Identity, scale=trig[:, f, st, c:c + 1])
                        mm.then_inc(rt_done, 1)
                        e.wait_ge(v_ready, i + 1)
                        need(e, av_done, i - (NB - 1))
                        need(e, av_rest, i - (NB - 1))
                        e.activation(VV[:, i % NB], v_ps[:, i % 2, 0:D], ACT.Copy).then_inc(v_done, 1)
                    t = i - 2
                    if 0 <= t < NT:
                        e.wait_ge(sub_done, t + 1)
                        e.activation(SC[:, t % NB], SC[:, t % NB], ACT.Exp, scale=HD ** -0.5).then_inc(exp_done, 1)

            @block.gpsimd
            def _(e):
                for i in range(NT + 4):
                    if i == 3:
                        e.wait_ge(core.bias_loaded, bias_n)
                        e.tensor_tensor(core.X[:], core.X[:], core.bias[:].unsqueeze(1).broadcast_to([P, NT, D]),
                                        ALU.add).then_inc(bias_done, 1)
                    if i < NT:
                        e.wait_ge(rt_done, i + 1)
                        need(e, prd_done, i - 2)
                        tc = RT[:, i % 2, 0, :].rearrange("p (g r) -> p r g", r=2)
                        ts = RT[:, i % 2, 1, :].rearrange("p (g r) -> p r g", r=2)
                        r = RO[:, i % 3].rearrange("p (g r) -> p r g", r=2)
                        e.tensor_tensor(r[:, 0], tc[:, 0], ts[:, 1], ALU.subtract)
                        e.tensor_tensor(r[:, 1], ts[:, 0], tc[:, 1], ALU.add).then_inc(ro_done, 1)
                    t = i - 4
                    if 0 <= t < NT:
                        e.wait_ge(a_done, t + 1)
                        need(e, o_done, t - 1)
                        av_product(e, t, 0, pool_heads(t)).then_inc(av_done, 1)
                e.wait_ge(bias_done, 1)

            @block.vector
            def _(e):
                e.memset(ones[:], 1.0).then_inc(ones_set, 1)
                dve_split()
                for i in range(NT + 5):
                    if i < NT:
                        e.wait_ge(ro_done, i + 1)
                        need(e, sc_ready, i - 1)
                        qv = RO[:, i % 3, 0:D].rearrange("p (h d) -> p d h", h=H).unsqueeze(3).broadcast_to([P, HD, H, H])
                        kv = RO[:, i % 3, D:2 * D].rearrange("p (t d) -> p d t", t=H).unsqueeze(2).broadcast_to([P, HD, H, H])
                        e.tensor_tensor(PRD[:, i % 2].rearrange("p d (h t) -> p d h t", h=H), qv, kv,
                                        ALU.mult).then_inc(prd_done, 1)
                    t = i - 2
                    if 0 <= t < NT:
                        s = t % 2
                        e.wait_ge(exp_done, t + 1)
                        need(e, rc_done, t - 1)
                        e.tensor_reduce(sm[:, s], SC[:, t % NB], AXX, ALU.add).then_inc(sm_done, 1)
                        e.wait_ge(sm_done, t + 1)
                        e.reciprocal(mx[:, s], sm[:, s]).then_inc(rc_done, 1)
                        e.wait_ge(rc_done, t + 1)
                        e.tensor_tensor(SC[:, t % NB], SC[:, t % NB], mx[:, s].unsqueeze(2).broadcast_to([P, H, H]),
                                        ALU.mult).then_inc(a_done, 1)
                    t = i - 1
                    if 0 <= t < NT:
                        s = t % 2
                        sc = sc_ps[:, s, 0:H * H].rearrange("p (h t) -> p h t", h=H)
                        e.wait_ge(sc_ready, t + 1)
                        need(e, a_done, t - 1)
                        e.tensor_reduce(mx[:, s], sc, AXX, ALU.max).then_inc(mx_done, 1)
                        e.wait_ge(mx_done, t + 1)
                        need(e, av_done, t - (NB - 1))
                        need(e, av_rest, t - (NB - 1))
                        e.tensor_tensor(SC[:, t % NB], sc, mx[:, s].unsqueeze(2).broadcast_to([P, H, H]),
                                        ALU.subtract).then_inc(sub_done, 1)
                    t = i - 4
                    if 0 <= t < NT:
                        e.wait_ge(a_done, t + 1)
                        need(e, o_done, t - 1)
                        av_product(e, t, pool_heads(t), H).then_inc(av_rest, 1)
                    t = i - 5
                    if 0 <= t < NT:
                        e.wait_ge(av_done, t + 1)
                        e.wait_ge(av_rest, t + 1)
                        need(e, stored[t % 2], 16 * (t // 2))
                        e.tensor_reduce(OO[:, t % 2].rearrange("p (h d) -> p h d", h=H),
                                        AVP[:, t % 2].rearrange("p (h d t) -> p h d t", h=H, d=HD), AXX,
                                        ALU.add).then_inc(o_done, 1)


def mixture_weights_phase(core, tag, C, next_raw):
    nc = core.nc
    K, n_exp, n_top = 8, 128, 4
    n_s = 8 - n_top
    W = n_exp + n_s
    with Phase(core, tag) as ph:
        n_w = KD * n_exp
        w = [ph.sb("w_hi", [P, n_w], F32R), ph.sb("w_lo", [P, n_w], F32R)]
        wv = [x[:].rearrange("p (k c) -> p k c", k=KD) for x in w]
        act_split, dve_split, w_ready, n_split = split_on(ph, w[0], w[1], n_w)
        mx = ph.sb("mx", [P, NT])
        neg = ph.sb("neg", [P, NT])
        ex = ph.sb("ex", [P, NT, W])
        total = ph.sb("total", [P, NT])
        top8 = ph.sb("top8", [P, NT, 8])
        vals = ph.sb("vals", [P, NT, 8])
        rest = ph.sb("rest", [P, NT, W])
        comb = ph.sb("comb", [P, NT, n_exp])
        den = ph.sb("den", [P, 2, NT])
        amp = ph.sb("amp", [P, K, 2])
        es = ph.sb("es", [P, 1])
        sq = ph.sb("sq", [P, K, 2])
        p8 = ph.sb("p8", [P, K])
        s1 = ph.sb("s1", [P, 3])
        mix = ph.sb("mix", [P, K])
        CT = ph.sb("CT", [P, 2, P])
        LG = ph.ps("logits", [P, 4, 512])
        TP = ph.ps("TP", [P, 2, 512])
        CP = ph.ps("CP", [P, NT, K])
        consts_in = ph.sem("consts_in")
        fill = ph.sem("fill")
        dv = ph.sem("dv")
        lg_ready = ph.sem("lg_ready")
        mx_done = ph.sem("mx_done")
        neg_done = ph.sem("neg_done")
        ex_done = ph.sem("ex_done")
        top_done = ph.sem("top_done")
        vals_done = ph.sem("vals_done")
        rest_done = ph.sem("rest_done")
        comb_done = ph.sem("comb_done")
        tp_ready = ph.sem("tp_ready")
        ct_done = ph.sem("ct_done")
        c_ready = ph.sem("c_ready")
        den_done = ph.sem("den_done")
        with nc.Block() as block:
            @block.sync
            def _(e):
                e.dma_start(amp[:], core.arrays["l3_amp"]).then_inc(consts_in, 16)
                e.dma_start(es[:], core.arrays["l3_escale"].rearrange("(p o) -> p o", o=1)).then_inc(consts_in, 16)
                e.wait_ge(w_ready, n_split)
                core.load_raw(e, next_raw)

            @block.tensor
            def _(e):
                e.wait_ge(w_ready, n_split)
                for i in range(NT + 6):
                    if i < NT:
                        need(e, mx_done, i - 3)
                        need(e, ex_done, i - 3)
                        for k in range(KD):
                            for j, (xi, wi) in enumerate(HI_LO):
                                mm = e.matmul(LG[:, i % 4, 0:n_exp], core.XT[xi][:, k, i * P:(i + 1) * P],
                                              wv[wi][:, k, :], start=(k == 0 and j == 0),
                                              stop=(k == KD - 1 and j == 2))
                        mm.then_inc(lg_ready, 1)
                    t = i - 5
                    if 0 <= t < NT:
                        e.wait_ge(comb_done, t + 1)
                        need(e, ct_done, t - 1)
                        e.transpose(TP[:, t % 2, 0:P], comb[:, t, :], core.ident[:]).then_inc(tp_ready, 1)
                    t = i - 6
                    if 0 <= t < NT:
                        if t == 0:
                            e.wait_ge(dv, 6)
                        e.wait_ge(ct_done, t + 1)
                        e.matmul(CP[:, t, :], CT[:, t % 2, :], mix[:], start=True, stop=True).then_inc(c_ready, 1)

            @block.scalar
            def _(e):
                act_split()
                for i in range(NT + 5):
                    if i < NT:
                        e.wait_ge(neg_done, i + 1)
                        e.activation(ex[:, i, 0:n_exp], LG[:, i % 4, 0:n_exp], ACT.Exp, bias=neg[:, i:i + 1],
                                     accum_out=total[:, i:i + 1]).then_inc(ex_done, 1)
                    t = i - 5
                    if 0 <= t < NT:
                        e.wait_ge(tp_ready, t + 1)
                        need(e, c_ready, t - 1)
                        e.activation(CT[:, t % 2, :], TP[:, t % 2, 0:P], ACT.Copy).then_inc(ct_done, 1)

            @block.gpsimd
            def _(e):
                for t in range(NT):
                    e.wait_ge(rest_done, t + 1)
                    e.tensor_tensor(comb[:, t, :], ex[:, t, 0:n_exp], rest[:, t, 0:n_exp],
                                    ALU.subtract).then_inc(comb_done, 1)

            @block.vector
            def _(e):
                for j in range(n_s):
                    e.memset(ex[:, :, n_exp + j:n_exp + j + 1], -1.0 - j).then_inc(fill, 1)
                    e.memset(vals[:, :, n_top + j:n_top + j + 1], -1.0 - j).then_inc(fill, 1)
                dve_split()
                e.wait_ge(consts_in, 32)
                e.tensor_tensor(sq[:], amp[:], amp[:], ALU.mult).then_inc(dv, 1)
                e.wait_ge(dv, 1)
                e.tensor_reduce(p8[:], sq[:], AXX, ALU.add).then_inc(dv, 1)
                e.wait_ge(dv, 2)
                e.tensor_reduce(s1[:, 0:1], p8[:], AXX, ALU.add).then_inc(dv, 1)
                e.wait_ge(dv, 3)
                e.tensor_scalar(s1[:, 1:2], s1[:, 0:1], 1e-8, None, ALU.add).then_inc(dv, 1)
                e.wait_ge(dv, 4)
                e.reciprocal(s1[:, 2:3], s1[:, 1:2]).then_inc(dv, 1)
                e.wait_ge(dv, 5)
                e.tensor_scalar(mix[:], p8[:], s1[:, 2:3], es[:], ALU.mult, ALU.mult).then_inc(dv, 1)
                for i in range(NT + 3):
                    if i < NT:
                        e.wait_ge(lg_ready, i + 1)
                        e.tensor_reduce(mx[:, i:i + 1], LG[:, i % 4, 0:n_exp], AXX, ALU.max).then_inc(mx_done, 1)
                    t = i - 2
                    if 0 <= t < NT:
                        e.wait_ge(ex_done, t + 1)
                        e.max(top8[:, t, :], ex[:, t, 0:n_exp]).then_inc(top_done, 1)
                    if i < NT:
                        e.wait_ge(mx_done, i + 1)
                        e.tensor_scalar(neg[:, i:i + 1], mx[:, i:i + 1], -1.0, None, ALU.mult).then_inc(neg_done, 1)
                    if 0 <= t < NT:
                        e.wait_ge(top_done, t + 1)
                        if t == 0:
                            e.wait_ge(fill, 2 * n_s)
                        e.tensor_copy(vals[:, t, 0:n_top], top8[:, t, 0:n_top]).then_inc(vals_done, 1)
                    t = i - 3
                    if 0 <= t < NT:
                        e.wait_ge(vals_done, t + 1)
                        e.match_replace(out=rest[:, t, :], in_to_replace=vals[:, t, :], in_values=ex[:, t, :],
                                        imm_value=0.0).then_inc(rest_done, 1)
                e.tensor_reduce(den[:, 0, :], top8[:, :, 0:n_top], AXX, ALU.add).then_inc(den_done, 1)
                e.wait_ge(den_done, 1)
                e.scalar_tensor_tensor(out=den[:, 1, :], in0=total[:], scalar=1e-8, in1=den[:, 0, :],
                                       op0=ALU.mult, op1=ALU.add).then_inc(den_done, 1)
                e.wait_ge(den_done, 2)
                e.reciprocal(den[:, 0, :], den[:, 1, :]).then_inc(den_done, 1)
                e.wait_ge(den_done, 3)
                e.wait_ge(c_ready, NT)
                e.tensor_tensor(C[:], CP[:], den[:, 0, :].unsqueeze(2).broadcast_to([P, NT, K]),
                                ALU.mult).then_inc(den_done, 1)
                e.wait_ge(den_done, 4)


def mixture_phase(core, tag, C):
    nc = core.nc
    K, I = 8, 128
    NG, NSH = KD * K * I, KD * 2 * I
    cols = 2 * NG + 2 * NSH + 3 * D
    with Phase(core, tag) as ph:
        w = [ph.sb("w_hi", [P, cols], F32R), ph.sb("w_lo", [P, cols], F32R)]
        main = [x[:, 0:2 * NG].rearrange("p (s k c) -> p s k c", s=2, k=KD) for x in w]
        shared = [x[:, 2 * NG:2 * NG + 2 * NSH].rearrange("p (s k c) -> p s k c", s=2, k=KD) for x in w]
        down = [x[:, 2 * NG + 2 * NSH:cols].rearrange("p (m c) -> p m c", m=3) for x in w]
        act_split, dve_split, w_ready, n_split = split_on(ph, w[0], w[1], cols)
        SG = ph.sb("SG", [P, 2, 512])
        T = ph.sb("T", [P, 2, 512])
        MS = ph.sb("MS", [P, 2, 3, P])
        HT = [ph.sb("HT_hi", [P, 2, 3 * P], F32R), ph.sb("HT_lo", [P, 2, 3 * P], F32R)]
        UG = ph.ps("UG", [P, 2, 2, 512])
        TP = ph.ps("TP", [P, 2, 512])
        tail = Tail(ph, last=True)
        ug_ready = ph.sem("ug_ready")
        silu_done = ph.sem("silu_done")
        t_done = ph.sem("t_done")
        acc_done = ph.sem("acc_done")
        tp_ready = ph.sem("tp_ready")
        ht_hi = ph.sem("ht_hi")
        ht_lo = ph.sem("ht_lo")
        with nc.Block() as block:
            @block.sync
            def _(e):
                for t in range(NT):
                    tail.sync_store(t)
                e.wait_ge(tail.stored, 16 * NT)

            @block.gpsimd
            def _(e):
                tail.pool_steps()

            def pe_t(e, t):
                e.wait_ge(acc_done, K * (t + 1))
                e.wait_ge(t_done, 3 * (t + 1))
                need(e, ht_lo, t - 1)
                for m in range(3):
                    mm = e.transpose(TP[:, t % 2, m * P:(m + 1) * P], MS[:, t % 2, m, :], core.ident[:])
                mm.then_inc(tp_ready, 1)

            def pe_down(e, t):
                e.wait_ge(ht_lo, t + 1)
                need(e, tail.summed, t - 1)
                for m in range(3):
                    for j, (hi, wi) in enumerate(HI_LO):
                        mm = e.matmul(tail.y[:, t % 2, 0:D], HT[hi][:, t % 2, m * P:(m + 1) * P], down[wi][:, m, :],
                                      start=(m == 0 and j == 0), stop=(m == 2 and j == 2))
                mm.then_inc(tail.y_ready, 1)

            @block.tensor
            def _(e):
                for i in range(NT + 2):
                    if i < NT:
                        for it in range(3):
                            n = 3 * i + it
                            need(e, t_done, n - 1)
                            for side in range(2):
                                if i == 0:
                                    e.wait_ge(w_ready, 2 * side + 2 if it < 2 else n_split)
                                N = 512 if it < 2 else 256
                                for k in range(KD):
                                    for j, (xi, wi) in enumerate(HI_LO):
                                        rhs = main[wi][:, side, k, it * 512:(it + 1) * 512] if it < 2 else \
                                            shared[wi][:, side, k, :]
                                        mm = e.matmul(UG[:, n % 2, side, 0:N], core.XT[xi][:, k, i * P:(i + 1) * P], rhs,
                                                      start=(k == 0 and j == 0), stop=(k == KD - 1 and j == 2))
                            mm.then_inc(ug_ready, 1)
                            if it == 0 and 0 <= i - 1 < NT:
                                pe_t(e, i - 1)
                            if it == 1 and 0 <= i - 1 < NT:
                                pe_down(e, i - 1)
                    elif i - 1 < NT:
                        pe_t(e, i - 1)
                        pe_down(e, i - 1)

            @block.scalar
            def _(e):
                act_split()
                for i in range(NT + 1):
                    for it in range(3):
                        if i < NT:
                            n = 3 * i + it
                            N = 512 if it < 2 else 256
                            e.wait_ge(ug_ready, n + 1)
                            need(e, t_done, n - 1)
                            e.activation(SG[:, n % 2, 0:N], UG[:, n % 2, 0, 0:N], ACT.Silu).then_inc(silu_done, 1)
                        if it == 0 and i >= 1:
                            t = i - 1
                            e.wait_ge(tp_ready, t + 1)
                            need(e, tail.y_ready, t - 1)
                            e.activation(HT[0][:, t % 2], TP[:, t % 2, 0:3 * P], ACT.Copy).then_inc(ht_hi, 1)

            @block.vector
            def _(e):
                dve_split()

                def item(i, it):
                    n = 3 * i + it
                    e.wait_ge(silu_done, n + 1)
                    if it == 2:
                        need(e, tp_ready, i - 1)
                        e.tensor_tensor(MS[:, i % 2, 1:3, :].rearrange("p a b -> p (a b)"), SG[:, n % 2, 0:256],
                                        UG[:, n % 2, 1, 0:256], ALU.mult).then_inc(t_done, 1)
                        return
                    need(e, acc_done, K * i + 4 * it - 4)
                    e.tensor_tensor(T[:, it, :], SG[:, n % 2, :], UG[:, n % 2, 1, :], ALU.mult).then_inc(t_done, 1)
                    e.wait_ge(t_done, n + 1)
                    for kk in range(4):
                        k = 4 * it + kk
                        src, c = T[:, it, kk * I:(kk + 1) * I], C[:, i, k:k + 1]
                        if k == 0:
                            need(e, tp_ready, i - 1)
                            e.tensor_scalar(MS[:, i % 2, 0, :], src, c, None, ALU.mult).then_inc(acc_done, 1)
                        else:
                            e.wait_ge(acc_done, K * i + k)
                            e.scalar_tensor_tensor(out=MS[:, i % 2, 0, :], in0=src, scalar=c, in1=MS[:, i % 2, 0, :],
                                                   op0=ALU.mult, op1=ALU.add).then_inc(acc_done, 1)

                for i in range(NT + 2):
                    if i < NT:
                        item(i, 0)
                    if 0 <= i - 1 < NT:
                        t = i - 1
                        e.wait_ge(ht_hi, t + 1)
                        e.tensor_tensor(HT[1][:, t % 2], TP[:, t % 2, 0:3 * P], HT[0][:, t % 2].bitcast(F32),
                                        ALU.subtract).then_inc(ht_lo, 1)
                    if i < NT:
                        item(i, 1)
                        item(i, 2)
                    if 0 <= i - 1 < NT:
                        tail.dve_stats(i - 1)
                    if 0 <= i - 2 < NT:
                        tail.dve_norm(i - 2)
                e.wait_ge(tail.normed, NT)


def program(nc, arrays, out):
    with ExitStack() as ctx:
        core = Core(nc, ctx, arrays, out)
        arrays["l1e_gu0"], arrays["l1e_dn0"] = arrays["l1e_gu"][0], arrays["l1e_dn"][0]
        arrays["l2_weights"] = nc.dram_tensor("l2_weights", [P, 4288], F32).ap()
        start_phase(core, [("l0_qkv", 1152)], "l0_bp")
        with Phase(core, "l0") as big:
            q = [big.sb("q_hi", [P, 8, S], F32R), big.sb("q_lo", [P, 8, S], F32R)]
            k = [big.sb("k_hi", [P, 8, S], F32R), big.sb("k_lo", [P, 8, S], F32R)]
            V = big.sb("V", [P, 8, TPB, 32])
            projection_phase(core, "l0p", q, k, V, 64, 576, 32 ** -0.5, [("l0_wp", 512)],
                             v_out=lambda part, b, kt: None if part else V[:, 2 * b:2 * b + 2, kt, :])
            O = big.sb("O", [P, 8, TPB, P])
            attention_phase(core, "l0a", q, k, V, O, 4, 8,
                            lambda u, r: O[:, bass.ds((u - r) // 4, 1), :, 32 * r:32 * r + 32].rearrange(
                                "p i t (a c) -> p (i t) a c", a=4), True, [])
            output_phase(core, "l0o", lambda t, kk: O[:, 2 * (t // TPB) + kk, t % TPB, :],
                         [("l0_up", 2048), ("l0_gate", 2048), ("l0_down", 2048)], absum=core.absum)
        feed_forward_phase(core, "l0f", 1024, [("l1_qkv", 1536)], "l1_bo", absum=core.absum)
        with Phase(core, "l1") as big:
            q = [big.sb("q_hi", [P, 8, S], F32R), big.sb("q_lo", [P, 8, S], F32R)]
            k = [big.sb("k_hi", [P, 8, S], F32R), big.sb("k_lo", [P, 8, S], F32R)]
            v = [big.sb("v_hi", [P, NT, D], F32R), big.sb("v_lo", [P, NT, D], F32R)]
            O = big.sb("O", [P, NT, D])
            bqk, bv = load_biases(core, big, "l1_bqk", "l1_bv")
            projection_phase(core, "l1p", q, k, v, D, 768, 1.0, [("l1_wo", 512)], qk_bias=bqk, v_bias=bv,
                             v_out=lambda part, b, kt: v[part][:, b * TPB + kt, :])
            wide_attention_phase(core, "l1a", q, k, v, O, 1.0 / 16, [])
            output_phase(core, "l1o", lambda t, kk: O[:, t, kk * P:(kk + 1) * P],
                         [("l1_router", 16), ("l1e_gu0", 2048), ("l1e_dn0", 1024)])
        experts_phase(core, "l1e", 8, 2, 512, [("l1_base_gu", 2048), ("l1_base_dn", 1024)],
                      "l2_lut", [("l2_gate", 1376), ("l2_up", 1376), ("l2_down", 1536)], "l2_weights")
        feed_forward_phase(core, "l1f", 512, [("l2_qkv", 1536)], "l2_bo")
        with Phase(core, "l2") as big:
            O = big.sb("O", [P, B, TPB, D])
            with Phase(core, "l2x") as inner:
                q = [inner.sb("q_hi", [P, 8, S], F32R), inner.sb("q_lo", [P, 8, S], F32R)]
                k = [inner.sb("k_hi", [P, 8, S], F32R), inner.sb("k_lo", [P, 8, S], F32R)]
                V = inner.sb("V", [P, 8, TPB, P])
                projection_phase(core, "l2p", q, k, V, D, 768, 16 ** -0.5, [("l2_wo", 512)],
                                 v_out=lambda part, b, kt: None if part else V[:, 2 * b:2 * b + 2, kt, :])

                def o_at(u, r, g):
                    nh = 2 * ((u - r) // 4) + r // 2
                    return O[:, (2 * r + g) % 4, :, bass.ds(nh * 16, 16)]
                attention_phase(core, "l2a", q, k, V, O, 2, 16, o_at, True, [])
            output_phase(core, "l2o", lambda t, kk: O[:, t // TPB, t % TPB, kk * P:(kk + 1) * P],
                         [("l2_weights", 4288)])
        feed_forward_phase(core, "l2f", 688, [("l3_qkv", 1536)], "l3_bo")
        with Phase(core, "l3") as big:
            O = big.sb("O", [P, NT, D])
            head_mixing_phase(core, "l3a", O, [("l3_wo", 512)], None)
            output_phase(core, "l3o", lambda t, kk: O[:, t, kk * P:(kk + 1) * P], [("l3_router", 256)])
        with Phase(core, "l3m") as big:
            C = big.sb("C", [P, NT, 8])
            mixture_weights_phase(core, "l3w", C, [("l3_gate", 2048), ("l3_up", 2048), ("l3_sgate", 512),
                                                   ("l3_sup", 512), ("l3_down", 256), ("l3_sdown", 512)])
            mixture_phase(core, "l3f", C)


def load_biases(core, big, qk_name, v_name):
    bqk = big.sb("bqk", [P, 4])
    bv = big.sb("bv", [P, D])
    done = big.sem("bias_in")
    with core.nc.Block() as block:
        @block.sync
        def _(e):
            e.dma_start(bqk[:], core.arrays[qk_name]).then_inc(done, 16)
            e.dma_start(bv[:], core.arrays[v_name].partition_broadcast(P)).then_inc(done, 16)
            e.wait_ge(done, 32)
    return bqk, bv


def by_partition(w):
    return np.ascontiguousarray(np.moveaxis(w.reshape((w.shape[0] // P, P) + w.shape[1:]), 0, 1)).reshape(P, -1)


def head_mask(G):
    m = np.zeros((P, G), np.float32)
    for row in range(96):
        m[row, (row % 32) // (32 // G)] = 1
    for g in range(G):
        m[96 + g, g] = 1
    return m


def layout(inp):
    a = {}
    x = np.asarray(inp["L0_attn_x"]).reshape(NT * P, D)
    a["x"], a["xT"] = x, np.ascontiguousarray(x.T)
    wkv = np.asarray(inp["L0_attn_Wkv"])
    wk = np.repeat(wkv[:, :64].reshape(D, 8, 1, 8), 4, axis=2).reshape(D, D)
    a["l0_qkv"] = by_partition(np.concatenate([np.asarray(inp["L0_attn_Wq"]), wk, wkv[:, 64:]], axis=1))
    a["l0_wp"] = by_partition(np.asarray(inp["L0_attn_Wp"]))
    a["l0_up"] = by_partition(np.ascontiguousarray(np.asarray(inp["L0_ffn_W_up"]).T))
    a["l0_gate"] = by_partition(np.ascontiguousarray(np.asarray(inp["L0_ffn_W_gate"]).T))
    a["l0_down"] = by_partition(np.ascontiguousarray(np.asarray(inp["L0_ffn_W_down"]).T))
    a["l1_qkv"] = by_partition(np.ascontiguousarray(np.asarray(inp["L1_attn_w_qkv"]).T))
    b = np.asarray(inp["L1_attn_b_qkv"])
    a["l1_bqk"], a["l1_bv"] = by_partition(b[:512]), b[512:]
    a["l1_wo"] = by_partition(np.ascontiguousarray(np.asarray(inp["L1_attn_w_out"]).T))
    a["l1_bo"] = np.asarray(inp["L1_attn_b_out"])
    a["l1_router"] = by_partition(np.asarray(inp["L1_ffn_gate_w"]))
    gu = np.asarray(inp["L1_ffn_expert_gate_up"])
    a["l1e_gu"] = np.stack([by_partition(g) for g in gu])
    a["l1e_dn"] = np.stack([by_partition(g) for g in np.asarray(inp["L1_ffn_expert_down"])])
    g = np.asarray(inp["L1_ffn_base_gate_up"])
    a["l1_base_gu"] = np.concatenate([by_partition(g[:, :512]), by_partition(g[:, 512:])], axis=1)
    a["l1_base_dn"] = by_partition(np.asarray(inp["L1_ffn_base_down"]))
    w = np.asarray(inp["L2_attn_Wqkv"]).T.reshape(D, 16, 3, 16)
    a["l2_qkv"] = by_partition(np.concatenate([w[:, :, i].reshape(D, D) for i in range(3)], axis=1))
    a["l2_wo"] = by_partition(np.ascontiguousarray(np.asarray(inp["L2_attn_Wproj"]).T))
    a["l2_bo"] = np.asarray(inp["L2_attn_bproj"])
    a["l2_gate"] = by_partition(np.ascontiguousarray(np.asarray(inp["L2_ffn_gate_idx"]).T))
    a["l2_up"] = by_partition(np.ascontiguousarray(np.asarray(inp["L2_ffn_up_idx"]).T))
    dn = np.zeros((768, D), np.asarray(inp["L2_ffn_down_idx"]).dtype)
    dn[:688] = np.asarray(inp["L2_ffn_down_idx"]).T
    a["l2_down"] = by_partition(dn)
    a["l2_lut"] = np.asarray(inp["L2_ffn_lut"])
    f = {k: np.asarray(v) for k, v in inp.items() if k.startswith("L3")}
    a["l3_qkv"] = by_partition(np.concatenate([f[f"L3_attn_W{c}"].T for c in "qkv"], axis=1))
    a["l3_bqkv"] = np.concatenate([f[f"L3_attn_b{c}"] for c in "qkv"]).reshape(1, -1)
    a["l3_wo"] = by_partition(np.ascontiguousarray(f["L3_attn_Wo"].T))
    a["l3_bo"] = f["L3_attn_bo"]
    a["l3_router"] = by_partition(f["L3_ffn_w_router"])
    a["l3_escale"] = f["L3_ffn_expert_scale"]
    a["l3_amp"] = f["L3_ffn_amplitudes"]
    for name, key in (("gate", "w_gate"), ("up", "w_up"), ("sgate", "shared_w_gate"), ("sup", "shared_w_up"),
                      ("down", "w_down"), ("sdown", "shared_w_down")):
        a[f"l3_{name}"] = by_partition(f[f"L3_ffn_{key}"])
    freqs = np.outer(np.arange(S, dtype=np.float32),
                     (1.0 / 10000.0 ** (np.arange(0, 16, 2, dtype=np.float32) / 16)).astype(np.float32))
    a["trig"] = np.stack([np.cos(freqs), np.sin(freqs)]).astype(np.float32)
    a["l0_bp"] = np.asarray(inp["L0_attn_bp"])
    a["mask4"], a["mask2"] = head_mask(4), head_mask(2)
    return a


def kernel(**inputs):
    import concourse.bacc as _bacc
    from concourse.bass_utils import run_bass_kernel_spmd as _run

    nc = _bacc.Bacc("TRN2", target_bir_lowering=False, num_devices=1)
    arrays = {name: np.ascontiguousarray(a) for name, a in layout(inputs).items()}
    handles = {name: nc.dram_tensor(name, a.shape, mybir.dt.from_np(a.dtype), kind="ExternalInput").ap()
               for name, a in arrays.items()}
    out = nc.dram_tensor("out", (NT * P, D), F32, kind="ExternalOutput").ap()
    program(nc, handles, out)
    r = _run(nc, [arrays], core_ids=[0])
    return r.results[0]["out"].reshape(B, S, D)
```
